# Optimizing a Trainium2 kernel written in Bass

```python
import numpy as np
import jax
import jax.numpy as jnp

def _softmax(x, axis=-1):
    return jax.nn.softmax(x, axis=axis)

def _gelu(x):
    return jax.nn.gelu(x, approximate=True)

def _silu(x):
    return jax.nn.silu(x)

def _sigmoid(x):
    return jax.nn.sigmoid(x)

def _layernorm(x, axis=-1, eps=1e-05):
    m = jnp.mean(x, axis=axis, keepdims=True)
    v = jnp.var(x, axis=axis, keepdims=True)
    return (x - m) / jnp.sqrt(v + eps)

def _scatter_add(tgt, idx, src, axis=0):
    return tgt.at[idx].add(src)

def _segment_sum(src, seg, n):
    return jax.ops.segment_sum(src, seg, n)
kernel_name = 'mk_conv_seq_d1_conv_nchw16_r2_d6abf6'

def setup_inputs(seed: int=0):
    np.random.seed(seed)
    _w = jnp.asarray

    def _rec_inputs():
        import jax
        import jax.numpy as jnp
        _gk = jax.random.key(seed)
        x = -0.0009896 + 1 * jax.random.normal(jax.random.fold_in(_gk, 1), (8, 16, 56, 56), jnp.float32)
        return x
    x = _rec_inputs()

    def _L0_conv_setup():
        import jax, jax.numpy as jnp
        import numpy as np
        B, C, H, W = (8, 16, 56, 56)
        K = 9
        FS = 9
        WIN = 7
        DIM = K * C + C
        HEADS = 5
        HEAD_DIM = DIM // HEADS
        MLP_DIM = 4 * DIM
        SHIFTS = (0, WIN // 2)
        NW = H // WIN * (W // WIN)
        CONV_DN = ('NCHW', 'OIHW', 'NCHW')

        def _rel_idx():
            co = np.stack(np.meshgrid(np.arange(WIN), np.arange(WIN), indexing='ij')).reshape(2, -1)
            rel = (co[:, :, None] - co[:, None, :]).transpose(1, 2, 0) + WIN - 1
            return rel[..., 0] * (2 * WIN - 1) + rel[..., 1]
        REL_IDX = jnp.asarray(_rel_idx())

        def _attn_mask(shift):
            img = np.zeros((H, W))
            sl = (slice(0, -WIN), slice(-WIN, -shift), slice(-shift, None))
            c = 0
            for hs in sl:
                for ws in sl:
                    img[hs, ws] = c
                    c += 1
            m = img.reshape(H // WIN, WIN, W // WIN, WIN).transpose(0, 2, 1, 3).reshape(NW, WIN * WIN)
            am = m[:, None, :] - m[:, :, None]
            return jnp.asarray(np.where(am != 0, -100.0, 0.0).astype(np.float32))
        MASK1 = _attn_mask(SHIFTS[1])

        def _ln(x, g, b, eps=1e-05):
            mu = x.mean(-1, keepdims=True)
            var = ((x - mu) ** 2).mean(-1, keepdims=True)
            return (x - mu) * jax.lax.rsqrt(var + eps) * g + b

        def _win_part(x):
            Bb = x.shape[0]
            x = x.reshape(Bb, H // WIN, WIN, W // WIN, WIN, DIM).transpose(0, 1, 3, 2, 4, 5)
            return x.reshape(Bb * NW, WIN * WIN, DIM)

        def _win_rev(xw, Bb):
            x = xw.reshape(Bb, H // WIN, W // WIN, WIN, WIN, DIM).transpose(0, 1, 3, 2, 4, 5)
            return x.reshape(Bb, H, W, DIM)

        def _swin_block(x, shift, mask, ln1g, ln1b, qkvw, qkvb, projw, projb, rpb, ln2g, ln2b, w1, b1, w2, b2):
            Bb = x.shape[0]
            sc = x
            x = _ln(x, ln1g, ln1b)
            if shift:
                x = jnp.roll(x, (-shift, -shift), axis=(1, 2))
            xw = _win_part(x)
            qkv = xw @ qkvw + qkvb
            q, k, v = jnp.split(qkv, 3, axis=-1)
            heads = lambda t: t.reshape(-1, WIN * WIN, HEADS, HEAD_DIM).transpose(0, 2, 1, 3)
            q, k, v = (heads(q), heads(k), heads(v))
            attn = jnp.einsum('whid,whjd->whij', q, k) * HEAD_DIM ** (-0.5)
            bias = rpb[REL_IDX].transpose(2, 0, 1)
            attn = attn + bias[None]
            if mask is not None:
                attn = attn.reshape(Bb, NW, HEADS, WIN * WIN, WIN * WIN) + mask[None, :, None]
                attn = attn.reshape(Bb * NW, HEADS, WIN * WIN, WIN * WIN)
            attn = jax.nn.softmax(attn, axis=-1)
            out = jnp.einsum('whij,whjd->whid', attn, v).transpose(0, 2, 1, 3).reshape(-1, WIN * WIN, DIM)
            out = out @ projw + projb
            x = _win_rev(out, Bb)
            if shift:
                x = jnp.roll(x, (shift, shift), axis=(1, 2))
            x = sc + x
            h = _ln(x, ln2g, ln2b)
            h = jax.nn.gelu(h @ w1 + b1) @ w2 + b2
            return x + h

        def _forward(x, f_ana, f_syn, ln1g, ln1b, qkvw, qkvb, projw, projb, rpb, ln2g, ln2b, w1, b1, w2, b2, linw, linb, convw, convb):
            x2 = jax.nn.relu(x)
            sub = jax.lax.conv_general_dilated(x2.reshape(B * C, 1, H, W), f_ana, (1, 1), 'SAME', dimension_numbers=CONV_DN)
            x_trans = sub.reshape(B, C, K, H, W).transpose(0, 2, 1, 3, 4).reshape(B, K * C, H, W)
            x3 = jnp.concatenate([x_trans, x2], axis=1).transpose(0, 2, 3, 1)
            for i, (shift, mask) in enumerate(zip(SHIFTS, (None, MASK1))):
                x3 = _swin_block(x3, shift, mask, ln1g[i], ln1b[i], qkvw[i], qkvb[i], projw[i], projb[i], rpb[i], ln2g[i], ln2b[i], w1[i], b1[i], w2[i], b2[i])
            x3 = x3 @ linw + linb
            y = x3.transpose(0, 3, 1, 2)
            ti = y.reshape(B, K, C, H, W).transpose(0, 2, 1, 3, 4).reshape(B * C, K, H, W)
            y_trans = jax.lax.conv_general_dilated(ti, f_syn, (1, 1), 'SAME', dimension_numbers=CONV_DN).reshape(B, C, H, W)
            yc = jnp.concatenate([y_trans, y], axis=1)
            return jax.lax.conv_general_dilated(yc, convw, (1, 1), 'SAME', dimension_numbers=CONV_DN) + convb[None, :, None, None]
        key = jax.random.key(seed)
        ks = jax.random.split(key, 12)
        s = 0.02
        return {'x': jax.random.normal(ks[0], (B, C, H, W), jnp.float32), 'f_ana': jax.random.normal(ks[1], (K, 1, FS, FS), jnp.float32) * s, 'f_syn': jax.random.normal(ks[2], (1, K, FS, FS), jnp.float32) * s, 'ln1g': jnp.ones((2, DIM), jnp.float32), 'ln1b': jnp.zeros((2, DIM), jnp.float32), 'qkvw': jax.random.normal(ks[3], (2, DIM, 3 * DIM), jnp.float32) * s, 'qkvb': jnp.zeros((2, 3 * DIM), jnp.float32), 'projw': jax.random.normal(ks[4], (2, DIM, DIM), jnp.float32) * s, 'projb': jnp.zeros((2, DIM), jnp.float32), 'rpb': jax.random.normal(ks[5], (2, (2 * WIN - 1) ** 2, HEADS), jnp.float32) * s, 'ln2g': jnp.ones((2, DIM), jnp.float32), 'ln2b': jnp.zeros((2, DIM), jnp.float32), 'w1': jax.random.normal(ks[6], (2, DIM, MLP_DIM), jnp.float32) * s, 'b1': jnp.zeros((2, MLP_DIM), jnp.float32), 'w2': jax.random.normal(ks[7], (2, MLP_DIM, DIM), jnp.float32) * s, 'b2': jnp.zeros((2, DIM), jnp.float32), 'linw': jax.random.normal(ks[8], (DIM, K * C), jnp.float32) * s, 'linb': jnp.zeros((K * C,), jnp.float32), 'convw': jax.random.normal(ks[9], (C, DIM, 1, 1), jnp.float32) * s, 'convb': jnp.zeros((C,), jnp.float32)}
    _L0_conv_all = _L0_conv_setup()
    _L0_conv_in = {k: v for k, v in _L0_conv_all.items() if k in ('f_ana', 'f_syn', 'ln1g', 'ln1b', 'qkvw', 'qkvb', 'projw', 'projb', 'rpb', 'ln2g', 'ln2b', 'w1', 'b1', 'w2', 'b2', 'linw', 'linb', 'convw', 'convb')}
    del _L0_conv_all
    return {'x': x, 'L0_conv_f_ana': _L0_conv_in['f_ana'], 'L0_conv_f_syn': _L0_conv_in['f_syn'], 'L0_conv_ln1g': _L0_conv_in['ln1g'], 'L0_conv_ln1b': _L0_conv_in['ln1b'], 'L0_conv_qkvw': _L0_conv_in['qkvw'], 'L0_conv_qkvb': _L0_conv_in['qkvb'], 'L0_conv_projw': _L0_conv_in['projw'], 'L0_conv_projb': _L0_conv_in['projb'], 'L0_conv_rpb': _L0_conv_in['rpb'], 'L0_conv_ln2g': _L0_conv_in['ln2g'], 'L0_conv_ln2b': _L0_conv_in['ln2b'], 'L0_conv_w1': _L0_conv_in['w1'], 'L0_conv_b1': _L0_conv_in['b1'], 'L0_conv_w2': _L0_conv_in['w2'], 'L0_conv_b2': _L0_conv_in['b2'], 'L0_conv_linw': _L0_conv_in['linw'], 'L0_conv_linb': _L0_conv_in['linb'], 'L0_conv_convw': _L0_conv_in['convw'], 'L0_conv_convb': _L0_conv_in['convb']}

def reference(x, L0_conv_f_ana, L0_conv_f_syn, L0_conv_ln1g, L0_conv_ln1b, L0_conv_qkvw, L0_conv_qkvb, L0_conv_projw, L0_conv_projb, L0_conv_rpb, L0_conv_ln2g, L0_conv_ln2b, L0_conv_w1, L0_conv_b1, L0_conv_w2, L0_conv_b2, L0_conv_linw, L0_conv_linb, L0_conv_convw, L0_conv_convb):
    import jax
    import jax.numpy as jnp

    def _L0_conv_ref(x, f_ana, f_syn, ln1g, ln1b, qkvw, qkvb, projw, projb, rpb, ln2g, ln2b, w1, b1, w2, b2, linw, linb, convw, convb):
        import jax, jax.numpy as jnp
        import numpy as np
        B, C, H, W = (8, 16, 56, 56)
        K = 9
        FS = 9
        WIN = 7
        DIM = K * C + C
        HEADS = 5
        HEAD_DIM = DIM // HEADS
        MLP_DIM = 4 * DIM
        SHIFTS = (0, WIN // 2)
        NW = H // WIN * (W // WIN)
        CONV_DN = ('NCHW', 'OIHW', 'NCHW')

        def _rel_idx():
            co = np.stack(np.meshgrid(np.arange(WIN), np.arange(WIN), indexing='ij')).reshape(2, -1)
            rel = (co[:, :, None] - co[:, None, :]).transpose(1, 2, 0) + WIN - 1
            return rel[..., 0] * (2 * WIN - 1) + rel[..., 1]
        REL_IDX = jnp.asarray(_rel_idx())

        def _attn_mask(shift):
            img = np.zeros((H, W))
            sl = (slice(0, -WIN), slice(-WIN, -shift), slice(-shift, None))
            c = 0
            for hs in sl:
                for ws in sl:
                    img[hs, ws] = c
                    c += 1
            m = img.reshape(H // WIN, WIN, W // WIN, WIN).transpose(0, 2, 1, 3).reshape(NW, WIN * WIN)
            am = m[:, None, :] - m[:, :, None]
            return jnp.asarray(np.where(am != 0, -100.0, 0.0).astype(np.float32))
        MASK1 = _attn_mask(SHIFTS[1])

        def _ln(x, g, b, eps=1e-05):
            mu = x.mean(-1, keepdims=True)
            var = ((x - mu) ** 2).mean(-1, keepdims=True)
            return (x - mu) * jax.lax.rsqrt(var + eps) * g + b

        def _win_part(x):
            Bb = x.shape[0]
            x = x.reshape(Bb, H // WIN, WIN, W // WIN, WIN, DIM).transpose(0, 1, 3, 2, 4, 5)
            return x.reshape(Bb * NW, WIN * WIN, DIM)

        def _win_rev(xw, Bb):
            x = xw.reshape(Bb, H // WIN, W // WIN, WIN, WIN, DIM).transpose(0, 1, 3, 2, 4, 5)
            return x.reshape(Bb, H, W, DIM)

        def _swin_block(x, shift, mask, ln1g, ln1b, qkvw, qkvb, projw, projb, rpb, ln2g, ln2b, w1, b1, w2, b2):
            Bb = x.shape[0]
            sc = x
            x = _ln(x, ln1g, ln1b)
            if shift:
                x = jnp.roll(x, (-shift, -shift), axis=(1, 2))
            xw = _win_part(x)
            qkv = xw @ qkvw + qkvb
            q, k, v = jnp.split(qkv, 3, axis=-1)
            heads = lambda t: t.reshape(-1, WIN * WIN, HEADS, HEAD_DIM).transpose(0, 2, 1, 3)
            q, k, v = (heads(q), heads(k), heads(v))
            attn = jnp.einsum('whid,whjd->whij', q, k) * HEAD_DIM ** (-0.5)
            bias = rpb[REL_IDX].transpose(2, 0, 1)
            attn = attn + bias[None]
            if mask is not None:
                attn = attn.reshape(Bb, NW, HEADS, WIN * WIN, WIN * WIN) + mask[None, :, None]
                attn = attn.reshape(Bb * NW, HEADS, WIN * WIN, WIN * WIN)
            attn = jax.nn.softmax(attn, axis=-1)
            out = jnp.einsum('whij,whjd->whid', attn, v).transpose(0, 2, 1, 3).reshape(-1, WIN * WIN, DIM)
            out = out @ projw + projb
            x = _win_rev(out, Bb)
            if shift:
                x = jnp.roll(x, (shift, shift), axis=(1, 2))
            x = sc + x
            h = _ln(x, ln2g, ln2b)
            h = jax.nn.gelu(h @ w1 + b1) @ w2 + b2
            return x + h

        def _forward(x, f_ana, f_syn, ln1g, ln1b, qkvw, qkvb, projw, projb, rpb, ln2g, ln2b, w1, b1, w2, b2, linw, linb, convw, convb):
            x2 = jax.nn.relu(x)
            sub = jax.lax.conv_general_dilated(x2.reshape(B * C, 1, H, W), f_ana, (1, 1), 'SAME', dimension_numbers=CONV_DN)
            x_trans = sub.reshape(B, C, K, H, W).transpose(0, 2, 1, 3, 4).reshape(B, K * C, H, W)
            x3 = jnp.concatenate([x_trans, x2], axis=1).transpose(0, 2, 3, 1)
            for i, (shift, mask) in enumerate(zip(SHIFTS, (None, MASK1))):
                x3 = _swin_block(x3, shift, mask, ln1g[i], ln1b[i], qkvw[i], qkvb[i], projw[i], projb[i], rpb[i], ln2g[i], ln2b[i], w1[i], b1[i], w2[i], b2[i])
            x3 = x3 @ linw + linb
            y = x3.transpose(0, 3, 1, 2)
            ti = y.reshape(B, K, C, H, W).transpose(0, 2, 1, 3, 4).reshape(B * C, K, H, W)
            y_trans = jax.lax.conv_general_dilated(ti, f_syn, (1, 1), 'SAME', dimension_numbers=CONV_DN).reshape(B, C, H, W)
            yc = jnp.concatenate([y_trans, y], axis=1)
            return jax.lax.conv_general_dilated(yc, convw, (1, 1), 'SAME', dimension_numbers=CONV_DN) + convb[None, :, None, None]
        return _forward(x, f_ana, f_syn, ln1g, ln1b, qkvw, qkvb, projw, projb, rpb, ln2g, ln2b, w1, b1, w2, b2, linw, linb, convw, convb)

    def _gn(v, G=8, eps=1e-05):
        B_, C_, H_, W_ = v.shape
        g = v.reshape(B_, G, C_ // G, H_, W_)
        m = jnp.mean(g, axis=(2, 3, 4), keepdims=True)
        s = jnp.var(g, axis=(2, 3, 4), keepdims=True)
        return ((g - m) / jnp.sqrt(s + eps)).reshape(v.shape)

    def _ln_c(v, eps=1e-06):
        m = jnp.mean(v, axis=1, keepdims=True)
        s = jnp.var(v, axis=1, keepdims=True)
        return (v - m) / jnp.sqrt(s + eps)

    def _ln_t(v, eps=1e-05):
        m = jnp.mean(v, axis=-1, keepdims=True)
        s = jnp.var(v, axis=-1, keepdims=True)
        return (v - m) / jnp.sqrt(s + eps)

    def _to_tokens(v):
        B_, C_, H_, W_ = v.shape
        return v.reshape(B_, C_, H_ * W_).transpose(0, 2, 1)

    def _from_tokens(t, like):
        B_, C_, H_, W_ = like.shape
        return t.transpose(0, 2, 1).reshape(B_, C_, H_, W_)
    x = _L0_conv_ref(x, L0_conv_f_ana, L0_conv_f_syn, L0_conv_ln1g, L0_conv_ln1b, L0_conv_qkvw, L0_conv_qkvb, L0_conv_projw, L0_conv_projb, L0_conv_rpb, L0_conv_ln2g, L0_conv_ln2b, L0_conv_w1, L0_conv_b1, L0_conv_w2, L0_conv_b2, L0_conv_linw, L0_conv_linb, L0_conv_convw, L0_conv_convb)
    return x

_drawn_inputs = setup_inputs


def setup_inputs(seed=0):
    import zlib

    import numpy as np

    out = dict(_drawn_inputs(seed))
    spreads = {'L0_conv_ln1g': (1.0, 0.6),
     'L0_conv_ln1b': (0.0, 0.8),
     'L0_conv_qkvb': (0.0, 0.477),
     'L0_conv_projb': (0.0, 0.1),
     'L0_conv_ln2g': (1.0, 0.6),
     'L0_conv_ln2b': (0.0, 0.8),
     'L0_conv_b1': (0.0, 0.1),
     'L0_conv_b2': (0.0, 0.1),
     'L0_conv_linb': (0.0, 0.1),
     'L0_conv_convb': (0.0, 0.1)}
    factors = {'L0_conv_rpb': 189.01}
    for name, (base, spread) in spreads.items():
        noise = np.random.default_rng([zlib.crc32(name.encode()), seed]).standard_normal(out[name].shape)
        drawn = base * np.exp(spread * noise) if base else spread * noise
        out[name] = jnp.asarray(drawn.astype(out[name].dtype))
    for name, factor in factors.items():
        out[name] = (out[name] * factor).astype(out[name].dtype)
    return out
```

```python
from contextlib import ExitStack

import concourse.bass as bass
from concourse import mybir

F32 = mybir.dt.float32
F32R = mybir.dt.float32r
ALU = mybir.AluOpType
ACT = mybir.ActivationFunctionType
AX = mybir.AxisListType

B, C, H, W = 8, 16, 56, 56
K, FS, WIN = 9, 9, 7
DIM = K * C + C
HEADS, HD = 5, 32
MLP = 4 * DIM
SHIFT = WIN // 2
EPS = 1e-5
LO, REST = 128, DIM - 128
CR = 3 * REST
CK = CR + 2
TT = 2 * W
NT = H // 2
PADT = NT + 4
NJ = 5
SR = 2 * WIN
ST = SR // 2
SN = SR * W
SPI = H // SR
NS = B * SPI
HALF = [(0, 4), (4, 3)]
WT = WIN * WIN
WP = 64
QP = WP + WT
GK = 2 * WT
NG = W // (2 * WIN)
VW = HD + 1
FT = MLP // 128
PADF = W - FS // 2 - 1
FROW = 112
ZW = 128 + CR
HP = H + SHIFT


def view(t, p0, n, off, dims):
    row = t.shape[-1]
    return bass.AP(tensor=t, offset=p0 * row + off, ap=[[row, n]] + [list(d) for d in dims])


def dram(t, off, dims):
    return bass.AP(tensor=t, offset=off, ap=[list(d) for d in dims])


def reach(engine, sem, value):
    if isinstance(value, int) and value <= 0:
        return
    engine.wait_ge(sem, value)


class Ring:

    def __init__(self, uses, banks, readers):
        self.uses, self.banks = uses, banks
        self.at = {u: n for n, u in enumerate(uses)}
        self.weight = [readers.get(u, 1) for u in uses]

    def slot(self, use):
        return self.at[use] % self.banks

    def filled(self, use):
        return self.at[use] // self.banks + 1

    def freed_before(self, use):
        n = self.at[use]
        return sum(self.weight[m] for m in range(n % self.banks, n, self.banks))

    def fills(self, slot):
        return len(range(slot, len(self.uses), self.banks))

    def frees(self, slot):
        return sum(self.weight[slot::self.banks])


def split_passes(nc, out, hi, lo, rest, w_hi, w_lo, w_rest, act_moves):
    pairs = [(hi, w_hi), (lo, w_hi), (hi, w_lo), (rest, w_rest)]
    for n, (a, w) in enumerate(pairs):
        lhs, rhs = (w, a) if act_moves else (a, w)
        last = nc.tensor.matmul(out, lhs, rhs, start=(n == 0), stop=(n == len(pairs) - 1))
    return last


def build(nc, x, xf, f_ana, f_syn, ln1g, ln1b, qkvw, qkvb, projw, projb, rel, ln2g, ln2b, w1, b1, w2, b2,
          linwT, linb, convwT, convb, wmask, out):
    xs0 = nc.dram_tensor("xs0", [B, H, W, DIM], F32, kind="Internal")
    xs1 = nc.dram_tensor("xs1", [B, HP, HP, DIM], F32, kind="Internal")
    ys = nc.dram_tensor("ys", [B, H, W, DIM], F32, kind="Internal")
    relT = nc.dram_tensor("relT", [WT, 2 * HEADS * WT], F32, kind="Internal")
    with ExitStack() as ctx:
        keep = Persistent(nc, ctx)
        phase_a(nc, keep, x, xf, f_ana, ln1g, ln1b, qkvw, qkvb, projw, projb, rel, relT, ln2g, ln2b, w1, b1,
                w2, b2, linwT, linb, convwT, convb, wmask, xs0)
        phase_b(nc, keep, xs0, xs1, ys)
        phase_c(nc, keep, f_syn, ys, out)


class Persistent:

    def __init__(self, nc, ctx):
        def sb(name, shape, dt=F32):
            return ctx.enter_context(nc.sbuf_tensor(name, shape, dt))
        self.ident = sb("ident", [128, 128])
        self.flip = sb("flip", [128, TT])
        self.qmask = sb("qmask", [128, 4])
        self.kmask = sb("kmask", [GK, 2])
        self.tabs = sb("tabs", [QP, 5 * HEADS * GK])
        self.w = {}
        for l in range(2):
            for name, n in (("qkv", 3 * DIM), ("proj", DIM), ("w1", MLP)):
                self.w[name, l] = self.split(sb, f"{name}{l}", n)
            self.w["w2", l] = sb(f"w2_{l}", [128, FT * DIM])
            self.w["b2", l] = sb(f"b2_{l}", [TT, DIM])
        self.w["lin", 1] = self.split(sb, "lin", DIM)

    @staticmethod
    def split(sb, name, n):
        return (sb(name + "_hi", [128, n], F32R), sb(name + "_lo", [128, n], F32R), sb(name + "_rest", [CK, n], F32R))


def phase_a(nc, keep, x, xf, f_ana, ln1g, ln1b, qkvw, qkvb, projw, projb, rel, relT, ln2g, ln2b, w1, b1, w2, b2,
            linwT, linb, convwT, convb, wmask, xs0):
    with ExitStack() as ctx:
        def sb(name, shape, dt=F32):
            return ctx.enter_context(nc.sbuf_tensor(name, shape, dt))

        def sem(name):
            return ctx.enter_context(nc.semaphore(name))

        NB = 5
        psum = [ctx.enter_context(nc.psum_tensor(f"a_ps{n}", [128, 512], F32)) for n in range(8)]
        nat_ps, mir_ps, conv_ps = psum[0], psum[1], psum[3:]
        taps = [sb(f"a_taps{n}", [TT, NJ * TT]) for n in range(2)]
        band_hi = sb("a_band_hi", [TT, K * NJ * TT], F32R)
        band_lo = sb("a_band_lo", [TT, K * NJ * TT], F32R)
        xin = [sb(f"a_xin{u}", [TT, 4 * TT]) for u in range(2)]
        xfin = [sb(f"a_xfin{u}", [TT, 4 * TT]) for u in range(2)]
        img_hi = sb("a_img_hi", [TT, PADT * C], F32R)
        img_lo = sb("a_img_lo", [TT, PADT * C], F32R)
        tok = [sb(f"a_tok{u}", [TT, NT * DIM]) for u in range(2)]
        mats = []
        for l in range(2):
            mats += [("qkv", l, 3 * DIM, qkvw, qkvb, 0), ("proj", l, DIM, projw, projb, None),
                     ("w1", l, MLP, w1, b1, 1)]
        raw_a = {m[:2]: sb(f"raw_a_{m[0]}{m[1]}", [128, m[2]]) for m in mats}
        raw_c = {m[:2]: sb(f"raw_c_{m[0]}{m[1]}", [CR, m[2]]) for m in mats}
        gain_a, gain_c = sb("gain_a", [128, 4]), sb("gain_c", [CR, 4])
        lnb_a, lnb_c = sb("lnb_a", [128, 4]), sb("lnb_c", [CR, 4])
        scaled, scaled_c = sb("scaled", [128, MLP]), sb("scaled_c", [CR, MLP])
        starts, width = {}, 0
        for m in mats:
            starts[m[:2]], width = width, width + m[2]
        starts["lin", 1], width = width, width + DIM
        brow = sb("brow", [CK, width])
        bhi, blo = sb("bhi", [CK, MLP], F32R), sb("blo", [CK, MLP])
        lwt_a, lwt_b = sb("lwt_a", [128, ZW]), sb("lwt_b", [C, ZW])
        mix_a, mix_b = sb("mix_a", [128, DIM]), sb("mix_b", [C, DIM])
        linb_a, linb_b = sb("linb_a", [128, 1]), sb("linb_b", [C, 1])
        relb, msk = sb("relb", [QP, 2 * HEADS * WT]), sb("msk", [QP, 4 * GK])

        s_taps = [sem(f"a_taps_in{n}") for n in range(2)]
        s_bhi, s_blo = sem("a_band_hi_done"), sem("a_band_lo_done")
        s_xin = [sem(f"a_x_in{u}") for u in range(2)]
        s_nat_T, s_mir_T, s_nat, s_ihi, s_ilo = sem("a_nat_T"), sem("a_mir_T"), sem("a_nat"), sem("a_img_hi"), sem("a_img_lo")
        s_conv = [sem(f"a_conv{n}") for n in range(NB)]
        s_free = [sem(f"a_conv_free{n}") for n in range(NB)]
        s_store = [sem(f"a_store{u}") for u in range(2)]
        s_pool, s_zero, s_ident, s_mixz = sem("a_pool"), sem("a_zero"), sem("a_ident"), sem("a_mixz")
        s_raw, s_small, s_mix = sem("a_raw"), sem("a_small"), sem("a_mix")
        s_relT, s_relb = sem("a_relT"), sem("a_relb")
        s_bps, s_prep = sem("a_bias_ps"), sem("a_prep")

        def bank_of(u, k):
            return (u * K + k) % NB

        def nth(u, k):
            return (u * K + k) // NB

        per = [len(range(b, 2 * K, NB)) for b in range(NB)]
        def pieces(m, cols):
            if m != "qkv":
                return [(0, 0, cols)]
            return [(0, 0, 128), (128, DIM, 128), (2 * 128, 128, HD), (2 * 128 + HD, DIM + 128, HD), (2 * DIM, 2 * DIM, DIM)]

        n_pieces = sum(len(pieces(m[0], m[2])) for m in mats)
        RAWS = 16 * (4 * n_pieces)
        SMALL = 16 * (4 * 4 * 2 + 2 * 2 + 2 + 8 + n_pieces + 1)
        MIX = 16 * (K + 2)
        block = ctx.enter_context(nc.Block())

        @block.sync
        def _(sp):
            def load_taps(k):
                for r in range(2):
                    for yy in range(2):
                        if k >= 2 and (r, yy) == (0, 0):
                            sp.wait_ge(s_blo, k - 1)
                        sp.dma_start(view(taps[k % 2], r * W, W, yy * W, [[TT, NJ], [1, W]]),
                                     dram(f_ana.tensor, (k * 11 + r - yy + 1) * FROW, [[1, W], [2 * FROW, NJ], [1, W]])
                                     ).then_inc(s_taps[k % 2], 16)

            def load_image(img, u):
                for t, src in ((xin[u], x), (xfin[u], xf)):
                    sp.dma_start(view(t, 0, TT, 0, [[TT, 4], [1, TT]]),
                                 dram(src.tensor, img * (C * H * W), [[TT, TT], [TT * TT, 4], [1, TT]])
                                 ).then_inc(s_xin[u], 16)

            def store_image(pair, u):
                for k in (K - 2, K - 1):
                    sp.wait_ge(s_free[bank_of(u, k)], pair * per[bank_of(u, k)] + nth(u, k) + 1)
                sp.wait_ge(s_nat, pair * 2 + u + 1)
                sp.dma_start(dram(xs0, (pair * 2 + u) * (H * W * DIM), [[DIM, TT], [TT * DIM, NT], [1, DIM]]),
                             view(tok[u], 0, TT, 0, [[DIM, NT], [1, DIM]])).then_inc(s_store[u], 16)

            load_image(0, 0)
            load_taps(0)
            load_taps(1)
            load_image(1, 1)
            for k in range(2, K):
                load_taps(k)
            with sp.Fori(0, B // 2 - 1) as pair:
                for u in range(2):
                    sp.wait_ge(s_nat_T, pair * 2 + u + 1)
                    sp.wait_ge(s_mir_T, pair * 2 + u + 1)
                    load_image(pair * 2 + u + 2, u)
                    store_image(pair, u)
            for u in range(2):
                store_image(B // 2 - 1, u)
            for u in range(2):
                sp.wait_ge(s_store[u], 16 * (B // 2))

        @block.gpsimd
        def _(pool):
            gp = nc.gpsimd
            n = [0]

            def step(ins):
                n[0] += 1
                ins.then_inc(s_pool, 1)
                pool.wait_ge(s_pool, n[0])

            for t in (mix_a, mix_b, keep.flip):
                gp.memset(t[:], 0.0)
            gp.memset(relb[:], 0.0)
            gp.memset(keep.qmask[:], float(HD) ** -0.5)
            gp.memset(keep.kmask[:], 1.0)
            gp.memset(keep.ident[:], 0.0).then_inc(s_mixz, 1)
            pool.wait_ge(s_mixz, 1)
            step(gp.affine_select(out=keep.ident[:], in_=keep.ident[:], compare_op=ALU.not_equal, fill=1.0, base=0,
                                  pattern=[[-1, 128]], channel_multiplier=1))
            for r in range(2):
                cols = keep.flip[:, r * W:(r + 1) * W]
                gp.affine_select(out=cols, in_=cols, compare_op=ALU.not_equal, fill=1.0,
                                 base=-(r * W + W - 1), pattern=[[1, W]], channel_multiplier=1)
            step(gp.affine_select(out=keep.qmask[:], in_=keep.qmask[:], compare_op=ALU.is_ge, fill=0.0, base=0,
                                  pattern=[[-HD, 4]], channel_multiplier=1))
            gp.affine_select(out=keep.qmask[:], in_=keep.qmask[:], compare_op=ALU.is_ge, fill=0.0, base=HD - 1,
                             pattern=[[HD, 4]], channel_multiplier=-1)
            gp.affine_select(out=keep.kmask[:, 0:1], in_=keep.kmask[:, 0:1], compare_op=ALU.is_ge, fill=0.0,
                             base=WT - 1, pattern=[[0, 1]], channel_multiplier=-1)
            gp.affine_select(out=keep.kmask[:, 1:2], in_=keep.kmask[:, 1:2], compare_op=ALU.is_ge, fill=0.0,
                             base=-WT, pattern=[[0, 1]], channel_multiplier=1)
            with pool.Fori(0, WIN) as yi:
                for xi in range(WIN):
                    pool.dma_start(dram(relT, yi * (WIN * 2 * HEADS * WT) + xi * (2 * HEADS * WT),
                                        [[WT, 2 * HEADS], [WIN, WIN], [1, WIN]]),
                                   dram(rel.tensor, yi * (-(2 * WIN - 1)) + ((WIN - 1) * (2 * WIN - 1) + WIN - 1 - xi),
                                        [[(2 * WIN - 1) ** 2, 2 * HEADS], [2 * WIN - 1, WIN], [1, WIN]])
                                   ).then_inc(s_relT, 16)
            pool.wait_ge(s_relT, 16 * WT)
            for p0 in (0, WP):
                pool.dma_start(relb[p0:p0 + WT, :],
                               dram(relT, 0, [[2 * HEADS * WT, WT], [1, 2 * HEADS * WT]])).then_inc(s_relb, 16)
            pool.dma_start(msk[:], wmask).then_inc(s_relb, 16)
            pool.wait_ge(s_raw, RAWS)
            pool.wait_ge(s_small, SMALL)
            for m, l, cols, _, _, ln in mats:
                hi, lo, rest = keep.w[m, l]
                ra, rc = raw_a[m, l], raw_c[m, l]
                if ln is not None:
                    g = 2 * l + ln
                    gp.tensor_scalar(scaled[:, 0:cols], ra[:], gain_a[:, g:g + 1], None, ALU.mult)
                    step(gp.tensor_scalar(scaled_c[:, 0:cols], rc[:], gain_c[:, g:g + 1], None, ALU.mult))
                    ra, rc = scaled, scaled_c
                gp.tensor_copy(hi[:], ra[:, 0:cols])
                step(gp.tensor_copy(rest[0:CR, :], rc[:, 0:cols]))
                step(gp.tensor_tensor(lo[:], ra[:, 0:cols], hi[:].bitcast(F32), ALU.subtract))
                step(gp.tensor_tensor(rest[2 * REST:CR, :], rc[2 * REST:CR, 0:cols],
                                      rest[2 * REST:CR, :].bitcast(F32), ALU.subtract))
            pool.wait_ge(s_relb, 48)
            for edge in range(5):
                for h in range(HEADS):
                    o = view(keep.tabs, 0, QP, edge * HEADS * GK + h * GK, [[WT, 2], [1, WT]])
                    r = view(relb, 0, QP, (min(edge, 1) * HEADS + h) * WT, [[0, 2], [1, WT]])
                    if edge == 0:
                        last = gp.tensor_copy(o, r)
                    else:
                        last = gp.tensor_tensor(o, r, view(msk, 0, QP, (edge - 1) * GK, [[WT, 2], [1, WT]]), ALU.add)
            step(last)

        @block.scalar
        def _(act):
            for m, l, cols, wt, _, _ in mats:
                for d0, s0, nn in pieces(m, cols):
                    act.dma_start(raw_a[m, l][:, d0:d0 + nn],
                                  dram(wt.tensor, l * DIM * cols + s0, [[cols, 128], [1, nn]])).then_inc(s_raw, 16)
                    for rep in range(3):
                        act.dma_start(raw_c[m, l][rep * REST:(rep + 1) * REST, d0:d0 + nn],
                                      dram(wt.tensor, (l * DIM + 128) * cols + s0, [[cols, REST], [1, nn]])).then_inc(s_raw, 16)
            for l in range(2):
                for ln, (g, b) in enumerate(((ln1g, ln1b), (ln2g, ln2b))):
                    col = 2 * l + ln
                    for ta, tc, src in ((gain_a, gain_c, g), (lnb_a, lnb_c, b)):
                        act.dma_start(ta[:, col:col + 1], dram(src.tensor, l * DIM, [[1, 128], [1, 1]])).then_inc(s_small, 16)
                        for rep in range(3):
                            act.dma_start(tc[rep * REST:(rep + 1) * REST, col:col + 1],
                                          dram(src.tensor, l * DIM + 128, [[1, REST], [1, 1]])).then_inc(s_small, 16)
                act.dma_start(view(keep.w["w2", l], 0, 128, 0, [[DIM, FT], [1, DIM]]),
                              dram(w2.tensor, l * MLP * DIM, [[DIM, 128], [128 * DIM, FT], [1, DIM]])).then_inc(s_small, 16)
                act.dma_start(keep.w["b2", l][:], dram(b2.tensor, l * DIM, [[0, TT], [1, DIM]])).then_inc(s_small, 16)
            act.wait_ge(s_zero, 1)
            for m, l, cols, _, b, _ in mats:
                c0 = starts[m, l]
                for d0, s0, nn in pieces(m, cols):
                    act.dma_start(brow[CR:CK, c0 + d0:c0 + d0 + nn],
                                  dram(b.tensor, l * cols + s0, [[0, 2], [1, nn]])).then_inc(s_small, 16)
            for t, r0, r1 in ((lwt_a, 0, 128), (lwt_b, 128, K * C)):
                act.dma_start(t[:, 0:128], linwT[r0:r1, 0:128]).then_inc(s_small, 16)
                for rep in range(3):
                    act.dma_start(t[:, 128 + rep * REST:128 + (rep + 1) * REST], linwT[r0:r1, 128:DIM]).then_inc(s_small, 16)
            act.dma_start(linb_a[:], dram(linb.tensor, 0, [[1, 128], [1, 1]])).then_inc(s_small, 16)
            act.dma_start(linb_b[:], dram(linb.tensor, 128, [[1, C], [1, 1]])).then_inc(s_small, 16)
            c0 = starts["lin", 1]
            act.dma_start(brow[CR:CK, c0 + K * C:c0 + DIM], dram(convb.tensor, 0, [[0, 2], [1, C]])).then_inc(s_small, 16)
            act.wait_ge(s_mixz, 1)
            for k in range(K):
                t, p0 = (mix_a, k * C) if k < 8 else (mix_b, 0)
                act.dma_start(t[p0:p0 + C, k * C:(k + 1) * C], convwT[0:C, :]).then_inc(s_mix, 16)
            act.dma_start(mix_a[:, K * C:DIM], convwT[C:C + 128, :]).then_inc(s_mix, 16)
            act.dma_start(mix_b[:, K * C:DIM], convwT[C + 128:DIM, :]).then_inc(s_mix, 16)
            for k in range(K):
                act.wait_ge(s_taps[k % 2], 64 * (k // 2 + 1))
                nc.scalar.activation(band_hi[:, k * NJ * TT:(k + 1) * NJ * TT], taps[k % 2][:], ACT.Copy).then_inc(s_bhi, 1)

            with act.Fori(0, B // 2) as pair:
                for u in range(2):
                    img = pair * 2 + u
                    act.wait_ge(s_mir_T, img + 1)
                    b = bank_of(1 - u, K - 1)
                    act.wait_ge(s_conv[b], pair * per[b] + u * (nth(0, K - 1) + 1))
                    act.wait_ge(s_zero, 1)
                    nc.scalar.activation(view(img_hi, 0, TT, 2 * C, [[1, C], [C, NT]]),
                                         view(mir_ps, 0, TT, 0, [[NT, C], [1, NT]]), ACT.Relu).then_inc(s_ihi, 1)
                    act.wait_ge(s_nat_T, img + 1)
                    act.wait_ge(s_store[u], pair * 16)
                    nc.scalar.activation(view(tok[u], 0, TT, K * C, [[1, C], [DIM, NT]]),
                                         view(nat_ps, 0, TT, 0, [[NT, C], [1, NT]]), ACT.Relu).then_inc(s_nat, 1)
                    for k in range(0, K, 2):
                        b = bank_of(u, k)
                        act.wait_ge(s_conv[b], pair * per[b] + nth(u, k) + 1)
                        nc.scalar.activation(view(tok[u], 0, TT, k * C, [[DIM, NT], [1, C]]),
                                             view(conv_ps[b], 0, TT, 0, [[C, NT], [1, C]]), ACT.Copy).then_inc(s_free[b], 1)

        @block.vector
        def _(dve):
            nc.vector.memset(brow[:], 0.0)
            nc.vector.memset(img_hi[:].bitcast(F32), 0.0)
            nc.vector.memset(img_lo[:].bitcast(F32), 0.0).then_inc(s_zero, 1)
            for k in range(K):
                dve.wait_ge(s_bhi, k + 1)
                cols = slice(k * NJ * TT, (k + 1) * NJ * TT)
                nc.vector.tensor_tensor(band_lo[:, cols], taps[k % 2][:], band_hi[:, cols].bitcast(F32),
                                        ALU.subtract).then_inc(s_blo, 1)
            with dve.Fori(0, B // 2) as pair:
                for u in range(2):
                    img = pair * 2 + u
                    dve.wait_ge(s_ihi, img + 1)
                    nc.vector.scalar_tensor_tensor(view(img_lo, 0, TT, 2 * C, [[1, C], [C, NT]]),
                                                   view(mir_ps, 0, TT, 0, [[NT, C], [1, NT]]), 0.0,
                                                   view(img_hi, 0, TT, 2 * C, [[1, C], [C, NT]]).bitcast(F32),
                                                   ALU.max, ALU.subtract).then_inc(s_ilo, 1)
                    for k in range(1, K, 2):
                        b = bank_of(u, k)
                        dve.wait_ge(s_conv[b], pair * per[b] + nth(u, k) + 1)
                        dve.wait_ge(s_store[u], pair * 16)
                        nc.vector.tensor_copy(view(tok[u], 0, TT, k * C, [[DIM, NT], [1, C]]),
                                              view(conv_ps[b], 0, TT, 0, [[C, NT], [1, C]])).then_inc(s_free[b], 1)
            n = 0

            def step(ins):
                nonlocal n
                n += 1
                ins.then_inc(s_prep, 1)
                dve.wait_ge(s_prep, n)

            dve.wait_ge(s_small, SMALL)
            dve.wait_ge(s_bps, 1)
            dve.wait_ge(s_pool, 1)
            hi, lo, rest = keep.w["lin", 1]
            nc.vector.tensor_copy(hi[:], psum[6][:, 0:DIM])
            step(nc.vector.tensor_copy(rest[0:CR, :], psum[6][0:CR, DIM:2 * DIM]))
            nc.vector.tensor_tensor(lo[:], psum[6][:, 0:DIM], hi[:].bitcast(F32), ALU.subtract)
            nc.vector.tensor_tensor(rest[2 * REST:CR, :], psum[6][2 * REST:CR, DIM:2 * DIM],
                                    rest[2 * REST:CR, :].bitcast(F32), ALU.subtract)
            for m, l, banks in (("qkv", 0, (0,)), ("w1", 0, (1, 2)), ("qkv", 1, (3,)), ("w1", 1, (4, 5)), ("lin", 1, (7,))):
                c0 = starts[m, l]
                left = {"qkv": 3 * DIM, "w1": MLP, "lin": DIM}[m]
                for b in banks:
                    nn = min(512, left)
                    last = nc.vector.tensor_tensor(brow[CR:CK, c0:c0 + nn], brow[CR:CK, c0:c0 + nn],
                                                   psum[b][CR:CK, 0:nn], ALU.add)
                    c0, left = c0 + nn, left - nn
            step(last)
            for m, l in starts:
                rest = keep.w[m, l][2]
                cols = rest.shape[1]
                src = brow[CR:CK, starts[m, l]:starts[m, l] + cols]
                step(nc.vector.tensor_copy(bhi[CR:CK, 0:cols], src))
                step(nc.vector.tensor_tensor(blo[CR:CK, 0:cols], src, bhi[CR:CK, 0:cols].bitcast(F32), ALU.subtract))
                step(nc.vector.tensor_scalar(blo[CR:CK, 0:cols], blo[CR:CK, 0:cols], keep.ident[CR:CK, CR + 1:CK], None, ALU.mult))
                step(nc.vector.scalar_tensor_tensor(rest[CR:CK, :], bhi[CR:CK, 0:cols].bitcast(F32), keep.ident[CR:CK, CR:CR + 1],
                                                    blo[CR:CK, 0:cols], ALU.mult, ALU.add))

        @block.tensor
        def _(pe):
            def turn(u, img):
                pe.wait_ge(s_xin[u], (img - u) * 16 + 32)
                pe.wait_ge(s_ilo, img)
                for q in range(4):
                    last = nc.tensor.transpose(mir_ps[0:TT, q * TT:(q + 1) * TT], xfin[u][:, q * TT:(q + 1) * TT],
                                               keep.ident[0:TT, 0:TT])
                last.then_inc(s_mir_T, 1)
                pe.wait_ge(s_nat, img)
                for q in range(4):
                    last = nc.tensor.transpose(nat_ps[0:TT, q * TT:(q + 1) * TT], xin[u][:, q * TT:(q + 1) * TT],
                                               keep.ident[0:TT, 0:TT])
                last.then_inc(s_nat_T, 1)

            pe.wait_ge(s_pool, 1)
            pe.wait_ge(s_blo, K)
            with pe.Fori(0, B // 2) as pair:
                for u in range(2):
                    img = pair * 2 + u
                    turn(u, img)
                    pe.wait_ge(s_ilo, img + 1)
                    for k in range(K):
                        b = bank_of(u, k)
                        pe.wait_ge(s_free[b], pair * per[b] + nth(u, k))
                        n = 0
                        for j in range(NJ):
                            cols = slice((k * NJ + j) * TT, (k * NJ + j + 1) * TT)
                            rows = slice(j * C, (j + NT) * C)
                            for a, m in ((band_hi, img_hi), (band_hi, img_lo), (band_lo, img_hi)):
                                last = nc.tensor.matmul(conv_ps[b][0:TT, 0:NT * C], a[:, cols], m[:, rows],
                                                        start=(n == 0), stop=(n == 3 * NJ - 1))
                                n += 1
                        last.then_inc(s_conv[b], 1)
            pe.wait_ge(s_raw, RAWS)
            pe.wait_ge(s_small, SMALL)
            pe.wait_ge(s_mix, MIX)
            for b in range(NB):
                pe.wait_ge(s_free[b], per[b] * (B // 2))
            pe.wait_ge(s_nat, B)
            pe.wait_ge(s_ilo, B)

            def bcast(t, p, col, n):
                return view(t, 0, p, col, [[0, n]])

            for (m, l, ln), banks in ((("qkv", 0, 0), (0,)), (("w1", 0, 1), (1, 2)), (("qkv", 1, 0), (3,)), (("w1", 1, 1), (4, 5))):
                c0, total = 0, raw_a[m, l].shape[1]
                for b in banks:
                    nn = min(512, total - c0)
                    nc.tensor.matmul(psum[b][0:CK, 0:nn], bcast(lnb_a, 128, 2 * l + ln, CK), raw_a[m, l][:, c0:c0 + nn],
                                     start=True, stop=False)
                    nc.tensor.matmul(psum[b][0:CK, 0:nn], bcast(lnb_c, REST, 2 * l + ln, CK), raw_c[m, l][0:REST, c0:c0 + nn],
                                     start=False, stop=True)
                    c0 += nn
            for o, wa, wb in ((psum[6][:, 0:DIM], lwt_a[:, 0:128], lwt_b[:, 0:128]),
                              (psum[6][0:CR, DIM:2 * DIM], lwt_a[:, 128:ZW], lwt_b[:, 128:ZW]),
                              (psum[7][0:CK, 0:DIM], bcast(linb_a, 128, 0, CK), bcast(linb_b, C, 0, CK))):
                nc.tensor.matmul(o, wa, mix_a[:], start=True, stop=False)
                last = nc.tensor.matmul(o, wb, mix_b[:], start=False, stop=True)
            last.then_inc(s_bps, 1)


def phase_b(nc, keep, xs0, xs1, ys):
    with ExitStack() as ctx:
        def sb(name, shape, dt=F32):
            return ctx.enter_context(nc.sbuf_tensor(name, shape, dt))

        def sem(name):
            return ctx.enter_context(nc.semaphore(name))

        def bank(name):
            return ctx.enter_context(nc.psum_tensor(name, [128, 512], F32))

        ra = [bank(f"ra{n}") for n in range(3)]
        rm = [bank(f"rm{n}") for n in range(2)]
        s_ps, pt_ps, o_ps = bank("s_ps"), bank("pt_ps"), bank("o_ps")
        PT4 = HEADS * 2 * VW

        xa, xr = sb("xa", [TT, ST * DIM]), sb("xr", [TT, ST * DIM])
        x1, x1b = sb("x1", [TT, ST * DIM]), sb("x1b", [TT, ST * DIM])
        xo, yz = sb("xo", [TT, ST * ZW]), sb("yz", [TT, ST * DIM])
        z1, z2 = sb("z1", [TT, ST * ZW]), sb("z2", [TT, ST * ZW])
        st = [sb(f"st{n}", [TT, ST * 6]) for n in range(2)]
        mean = [sb(f"mean{n}", [TT, ST]) for n in range(2)]
        rs = [sb(f"rs{n}", [TT, ST]) for n in range(2)]
        half, mhalf, by_dim, eps = sb("half", [TT, ST]), sb("mhalf", [TT, ST]), sb("by_dim", [TT, ST]), sb("eps", [TT, ST])
        one = sb("one", [TT, 1])
        ln_tmp = [[sb(f"ln_tmp{n}_{k}", [TT, ST]) for k in range(8)] for n in range(2)]
        z1t = [sb("z1t_hi", [128, SN], F32R), sb("z1t_lo", [128, SN], F32R), sb("z1t_rest", [CK, SN], F32R)]
        z2t = [sb("z2t_hi", [128, SN], F32R), sb("z2t_lo", [128, SN], F32R), sb("z2t_rest", [CK, SN], F32R)]
        ot = [sb("ot_hi", [128, SN], F32R), sb("ot_lo", [128, SN], F32R), sb("ot_rest", [CK, SN], F32R)]
        qm = sb("qm", [128, 4 * SN])
        kt = sb("kt", [128, SN])
        q4, k4 = sb("q4", [128, SN]), sb("k4", [128, SN])
        vb = sb("vb", [GK, 2 * 2 * HEADS * VW])
        sc = sb("sc", [QP, HEADS * GK])
        mx = sb("mx", [QP, 2 * HEADS])
        sm = sb("sm", [QP, HEADS * GK])
        pr = sb("pr", [QP, HEADS * GK])
        pt = sb("pt", [GK, HEADS * QP])
        rd = sb("rd", [QP, 2 * HEADS])
        os_ = sb("os", [QP, 2 * ZW])
        ht = sb("ht", [128, FT * SN])

        s_xa, s_xr, s_xo, s_yz, s_dup = sem("xa_in"), sem("xr_in"), sem("xo_out"), sem("yz_out"), sem("dup")
        s_init = sem("b_init")
        ra_full = [sem(f"ra_full{n}") for n in range(3)]
        ra_free = [sem(f"ra_free{n}") for n in range(3)]
        rm_full = [sem(f"rm_full{n}") for n in range(2)]
        rm_free = [sem(f"rm_free{n}") for n in range(2)]
        s_st = [sem("stats1"), sem("stats2")]
        s_rs = [sem("rs1"), sem("rs2")]
        s_norm = [sem("norm1"), sem("norm2")]
        s_z = [sem("z1_full"), sem("z2_full")]
        s_hi1, s_hi2, s_oth = sem("z1t_hi_done"), sem("z2t_hi_done"), sem("ot_hi_done")
        s_sfull, s_sadd, s_smax, s_ssub = sem("s_full"), sem("s_add"), sem("s_max"), sem("s_sub")
        s_exp, s_ptf, s_pte, s_of, s_rec, s_od = (sem("exp_done"), sem("pt_full"), sem("pt_out"), sem("o_full"),
                                                  sem("o_rec"), sem("o_done"))
        s_x1b, s_xod = sem("x1b_done"), sem("xo_dup")

        RA = Ring(["T1A0", "T1C0", "T1A1", "T1C1", "Q0", "K0", "B0", "Q1", "K1", "B1", "V0", "V1", "OT0", "V2", "OT1",
                   "V3", "OT2", "OT3", "P0", "P1", "P2"], 3, {f"V{j}": 2 for j in range(NG)})
        MLP_USES = ["T2A0", "T2C0", "T2A1", "T2C1"] + [f"G{g}" for g in range(2 * FT)] + ["W0", "W1", "W2", "W3"]
        LIN_USES = ["T3A0", "T3C0", "T3A1", "T3C1", "L0", "L1", "L2", "L3"]
        RM = [Ring(MLP_USES, 2, {}), Ring(MLP_USES + LIN_USES, 2, {})]
        NM = [len(r.uses) // 2 for r in RM]
        PAIRS = [(0, 2), (2, 2), (4, 2), (6, 1)]
        RS_STEPS = 5
        PROJ = [(0, 3), (3, 3), (6, 1)]
        QH = SN // 2

        def a_full(i, use):
            s = RA.slot(use)
            return ra_full[s], i * RA.fills(s) + RA.filled(use)

        def a_freed(i, use):
            s = RA.slot(use)
            return ra_free[s], i * RA.frees(s) + RA.freed_before(use) + RA.weight[RA.at[use]]

        def a_room(i, use):
            s = RA.slot(use)
            return ra_free[s], i * RA.frees(s) + RA.freed_before(use)

        def m_base(m, l):
            return m * NM[0] if l == 0 else m * NM[1] + NS * (NM[0] - NM[1])

        def m_full(m, l, use):
            return rm_full[RM[l].slot(use)], m_base(m, l) + RM[l].filled(use)

        def m_freed(m, l, use):
            return rm_free[RM[l].slot(use)], m_base(m, l) + RM[l].filled(use)

        def m_room(m, l, use):
            return rm_free[RM[l].slot(use)], m_base(m, l) + RM[l].filled(use) - 1

        def hi2(m, l, n):
            return (m * 4 if l == 0 else m * 8 - NS * 4) + n

        block = ctx.enter_context(nc.Block())

        def bodies(engine, body):
            body(0, 0, None)
            with engine.Fori(1, NS) as i:
                body(i, 0, 0)
            body(NS, 1, 0)
            with engine.Fori(NS + 1, 2 * NS - 1) as i:
                body(i, 1, 1)
            body(2 * NS - 1, 1, 1)
            body(2 * NS, None, 1)

        @block.sync
        def _(sp):
            def strip(n, l, yy):
                if l == 0:
                    return dram(xs0, n * (SR * W * DIM) + yy * W * DIM, [[DIM, W], [TT * DIM, ST], [1, DIM]])
                k = n - NS
                off = k * (SR * HP * DIM) + (k // SPI) * (SHIFT * HP * DIM) + (SHIFT + yy) * HP * DIM + SHIFT * DIM
                return dram(xs1, off, [[DIM, W], [2 * HP * DIM, ST], [1, DIM]])

            def load(t, s, n, l):
                for yy in range(2):
                    sp.dma_start(view(t, yy * W, W, 0, [[DIM, ST], [1, DIM]]), strip(n, l, yy)).then_inc(s, 16)

            def store(m, l):
                for yy in range(2):
                    if l == 0:
                        off = m * (SR * HP * DIM) + (m // SPI) * (SHIFT * HP * DIM) + yy * HP * DIM
                        sp.dma_start(dram(xs1, off, [[DIM, W], [2 * HP * DIM, ST], [1, DIM]]),
                                     view(xo, yy * W, W, 0, [[ZW, ST], [1, DIM]])).then_inc(s_xo, 16)
                    else:
                        sp.dma_start(dram(ys, (m - NS) * (SR * W * DIM) + yy * W * DIM, [[DIM, W], [TT * DIM, ST], [1, DIM]]),
                                     view(yz, yy * W, W, 0, [[DIM, ST], [1, DIM]])).then_inc(s_yz, 16)

            def repeat_margins(b0, nb):
                img, row = HP * HP * DIM, HP * DIM
                for b in range(b0, b0 + nb):
                    sp.dma_start(dram(xs1, b * img + W * DIM, [[row, H], [1, SHIFT * DIM]]),
                                 dram(xs1, b * img, [[row, H], [1, SHIFT * DIM]])).then_inc(s_dup, 16)
                    sp.dma_start(dram(xs1, b * img + H * row, [[row, SHIFT], [1, W * DIM]]),
                                 dram(xs1, b * img, [[row, SHIFT], [1, W * DIM]])).then_inc(s_dup, 16)
                    sp.dma_start(dram(xs1, b * img + H * row + W * DIM, [[row, SHIFT], [1, SHIFT * DIM]]),
                                 dram(xs1, b * img, [[row, SHIFT], [1, SHIFT * DIM]])).then_inc(s_dup, 16)

            def body(i, la, lm, ahead=None):
                if ahead is not None:
                    sp.wait_ge(s_norm[0], i + 2)
                    load(xa, s_xa, i + 2, ahead)
                if lm is not None:
                    use = "W3" if lm == 0 else "L3"
                    sp.wait_ge(*m_freed(i - 1, lm, use))
                    store(i - 1, lm)
                if la is not None and not (isinstance(i, int) and i == 2 * NS - 1):
                    sp.wait_ge(*a_freed(i, "P2"))
                    nxt = 1 if (isinstance(i, int) and i == NS - 1) or la == 1 else 0
                    load(xr, s_xr, i + 1, nxt)

            load(xa, s_xa, 0, 0)
            load(xr, s_xr, 0, 0)
            sp.wait_ge(s_norm[0], 1)
            load(xa, s_xa, 1, 0)
            body(0, 0, None, 0)
            with sp.Fori(1, NS - 2) as i:
                body(i, 0, 0, 0)
            sp.wait_ge(s_xo, 32 * (NS - 3))
            repeat_margins(0, B - 1)
            sp.wait_ge(s_dup, 48 * (B - 1))
            body(NS - 2, 0, 0, 1)
            body(NS - 1, 0, 0, 1)
            body(NS, 1, 0, 1)
            sp.wait_ge(s_xo, 32 * NS)
            repeat_margins(B - 1, 1)
            sp.wait_ge(s_dup, 48 * B)
            with sp.Fori(NS + 1, 2 * NS - 2) as i:
                body(i, 1, 1, 1)
            body(2 * NS - 2, 1, 1)
            body(2 * NS - 1, 1, 1)
            body(2 * NS, None, 1)
            sp.wait_ge(s_yz, 32 * NS)

        @block.gpsimd
        def _(pool):
            gp = nc.gpsimd

            def inv_std(n, i):
                me, se, mo, so = (view(st[n], 0, TT, c, [[6, ST]]) for c in (1, 2, 4, 5))
                total, diff, sq, hdiff, sq1, hsq, sq2, var = ln_tmp[n]
                steps = [[(total[:], me, mo, ALU.add), (diff[:], me, mo, ALU.subtract), (sq[:], se, so, ALU.add)],
                         [(mean[n][:], total[:], half[:], ALU.mult), (hdiff[:], diff[:], half[:], ALU.mult),
                          (sq1[:], sq[:], by_dim[:], ALU.mult)],
                         [(hsq[:], hdiff[:], hdiff[:], ALU.mult), (sq2[:], sq1[:], eps[:], ALU.add)],
                         [(var[:], hsq[:], sq2[:], ALU.add)],
                         [(rs[n][:], var[:], mhalf[:], ALU.pow)]]
                pool.wait_ge(s_st[n], i + 1)
                for k, ops in enumerate(steps):
                    if k:
                        pool.wait_ge(s_rs[n], len(steps) * i + k)
                    for o, x_, y_, op in ops:
                        ins = gp.tensor_tensor(o, x_, y_, op)
                    ins.then_inc(s_rs[n], 1)
                assert len(steps) == RS_STEPS

            def repeat_rest(t, s):
                once = view(t, 0, TT, 128, [[ZW, ST], [0, 2], [1, REST]])
                gp.tensor_tensor(view(t, 0, TT, DIM, [[ZW, ST], [REST, 2], [1, REST]]), once,
                                 view(one, 0, TT, 0, [[0, ST], [0, 2], [0, REST]]), ALU.mult).then_inc(s, 1)

            for t, c in ((half, 0.5), (by_dim, 1.0 / DIM), (eps, EPS), (one, 1.0)):
                gp.memset(t[:], c)
            gp.memset(mhalf[:], -0.5).then_inc(s_init, 1)
            pool.wait_ge(s_init, 1)
            inv_std(0, 0)
            pool.wait_ge(s_norm[0], 1)
            repeat_rest(z1, s_z[0])

            def body(i, la, lm):
                if lm is not None:
                    pool.wait_ge(s_norm[1], i)
                    repeat_rest(z2, s_z[1])
                if la is not None and not (isinstance(i, int) and i == 2 * NS - 1):
                    inv_std(0, i + 1)
                    pool.wait_ge(s_norm[0], i + 2)
                    repeat_rest(z1, s_z[0])
                if la is not None:
                    inv_std(1, i)
                    if lm is not None:
                        pool.wait_ge(*m_freed(i - 1, lm, "W3"))
                    for n, t in enumerate(range(ST)):
                        ins = gp.tensor_tensor(x1b[:, t * DIM:(t + 1) * DIM], x1[:, t * DIM:(t + 1) * DIM],
                                               keep.w["b2", la][:], ALU.add)
                    ins.then_inc(s_x1b, 1)
                if lm == 1:
                    pool.wait_ge(*m_freed(i - 1, 1, "W3"))
                    repeat_rest(xo, s_xod)

            bodies(pool, body)

        @block.scalar
        def _(act):
            act_ = nc.scalar.activation

            def body(i, la, lm):
                m = i - 1

                if la is not None:
                    for hf, (t0, nt) in enumerate(HALF):
                        for part, dst, rows in (("A", z1t[0], 128), ("C", z1t[2], CR)):
                            use = f"T1{part}{hf}"
                            act.wait_ge(*a_full(i, use))
                            act_(view(dst, 0, rows, t0 * 2 * WIN, [[WIN, 2 * nt], [GK, 8], [1, WIN]]),
                                 view(ra[RA.slot(use)], 0, rows, 0, [[W, 2 * nt], [WIN, 8], [1, WIN]]), ACT.Copy).then_inc(s_hi1, 1)
                    for hf in range(2):
                        use = f"Q{hf}"
                        act.wait_ge(*a_full(i, use))
                        for h in range(4):
                            last = act_(qm[:, h * SN + hf * QH:h * SN + (hf + 1) * QH], ra[RA.slot(use)][:, 0:QH], ACT.Copy,
                                        scale=keep.qmask[:, h:h + 1])
                        last.then_inc(ra_free[RA.slot(use)], 1)

                def values(j, p):
                    use = f"V{j}"
                    act.wait_ge(*a_full(i, use))
                    act_(view(vb, 0, GK, p * 2 * HEADS * VW, [[VW, 2 * HEADS], [1, HD]]),
                         view(ra[RA.slot(use)], 0, GK, 0, [[HD, 2 * HEADS], [1, HD]]), ACT.Copy,
                         scale=keep.kmask[:, p:p + 1]).then_inc(ra_free[RA.slot(use)], 1)

                def exps(j):
                    act.wait_ge(s_ssub, i * NG + j + 1)
                    act_(pr[:], sm[:], ACT.Exp).then_inc(s_exp, 1)

                def weights_out(j):
                    act.wait_ge(s_ptf, i * NG + j + 1)
                    act_(pt[:, 0:4 * QP], pt_ps[0:GK, 0:4 * QP], ACT.Copy)
                    act_(pt[:, 4 * QP:5 * QP], o_ps[0:GK, PT4:PT4 + QP], ACT.Copy).then_inc(s_pte, 1)

                def outputs_hi(j):
                    use = f"OT{j}"
                    act.wait_ge(*a_full(i, use))
                    for dst, rows, c0 in ((ot[0], 128, 0), (ot[2], CR, 2 * QP)):
                        for p in range(2):
                            last = act_(view(dst, 0, rows, p * WIN * W + j * 2 * WIN, [[WIN, 2], [W, WIN], [1, WIN]]),
                                        view(ra[RA.slot(use)], 0, rows, c0 + p * QP, [[WP, 2], [WIN, WIN], [1, WIN]]), ACT.Copy)
                    last.then_inc(s_oth, 1)

                def t_hi(name, l):
                    for hf, (t0, nt) in enumerate(HALF):
                        for part, dst, rows in (("A", z2t[0], 128), ("C", z2t[2], CR)):
                            use = f"{name}{part}{hf}"
                            act.wait_ge(*m_full(m, l, use))
                            act_(dst[0:rows, t0 * TT:(t0 + nt) * TT], rm[RM[l].slot(use)][0:rows, 0:nt * TT],
                                 ACT.Copy).then_inc(s_hi2, 1)

                if la is not None:
                    values(0, 0)
                if lm is not None:
                    t_hi("T2", lm)
                    for g in range(2 * FT):
                        hf, f = divmod(g, FT)
                        t0, nt = HALF[hf]
                        use = f"G{g}"
                        act.wait_ge(*m_full(m, lm, use))
                        act_(ht[:, f * SN + t0 * TT:f * SN + (t0 + nt) * TT], rm[RM[lm].slot(use)][:, 0:nt * TT],
                             ACT.Gelu_apprx_tanh).then_inc(rm_free[RM[lm].slot(use)], 1)
                if la is not None:
                    exps(0)
                    weights_out(0)
                    for j in range(1, NG):
                        values(j, 0)
                        exps(j)
                        outputs_hi(j - 1)
                        weights_out(j)
                    outputs_hi(NG - 1)
                if lm == 1:
                    t_hi("T3", 1)

            bodies(act, body)

        @block.vector
        def _(dve):
            v = nc.vector

            def stats(n, x_, i, tiles=range(ST), last=True):
                for t in tiles:
                    ins = v.bn_stats(st[n][:, t * 6:(t + 1) * 6], x_[:, t * DIM:(t + 1) * DIM])
                if last:
                    ins.then_inc(s_st[n], 1)

            def normalise(n, z, x_, i):
                dve.wait_ge(s_rs[n], RS_STEPS * (i + 1))
                for t in range(ST):
                    ins = v.tensor_scalar(z[:, t * ZW:t * ZW + DIM], x_[:, t * DIM:(t + 1) * DIM],
                                          mean[n][:, t:t + 1], rs[n][:, t:t + 1], ALU.subtract, ALU.mult)
                ins.then_inc(s_norm[n], 1)

            v.memset(q4[:], 0.0)
            v.memset(k4[:], 0.0)
            for t in (z1t[2], z2t[2], ot[2]):
                v.memset(t[CR:CK, :].bitcast(F32), 1.0)
            for p in range(2):
                v.tensor_copy(view(vb, 0, GK, p * 2 * HEADS * VW + HD, [[VW, 2 * HEADS]]),
                              view(keep.kmask, 0, GK, p, [[0, 2 * HEADS]]))
            v.memset(s_ps[:], 0.0)
            v.memset(o_ps[:], 1.0).then_inc(s_init, 1)
            dve.wait_ge(s_xa, 32)
            stats(0, xa, 0)
            normalise(0, z1, xa, 0)

            def body(i, la, lm):
                m = i - 1
                if la is not None:
                    for hf, (t0, nt) in enumerate(HALF):
                        for n, (part, dst, src, p0, rows) in enumerate((("A", z1t[1], z1t[0], 0, 128),
                                                                       ("C", z1t[2], z1t[2], REST, REST))):
                            use = f"T1{part}{hf}"
                            dve.wait_ge(s_hi1, i * 4 + 2 * hf + n + 1)
                            dims = [[WIN, 2 * nt], [GK, 8], [1, WIN]]
                            v.tensor_tensor(view(dst, p0, rows, t0 * 2 * WIN, dims),
                                            view(ra[RA.slot(use)], p0, rows, 0, [[W, 2 * nt], [WIN, 8], [1, WIN]]),
                                            view(src, p0, rows, t0 * 2 * WIN, dims).bitcast(F32),
                                            ALU.subtract).then_inc(ra_free[RA.slot(use)], 1)
                if lm is not None:
                    normalise(1, z2, x1, m)
                if la is not None:
                    for hf in range(2):
                        use = f"K{hf}"
                        dve.wait_ge(*a_full(i, use))
                        cols = slice(hf * QH, (hf + 1) * QH)
                        v.tensor_copy(kt[:, cols], ra[RA.slot(use)][:, 0:QH]).then_inc(ra_free[RA.slot(use)], 1)
                        use = f"B{hf}"
                        dve.wait_ge(*a_full(i, use))
                        v.tensor_scalar(q4[0:HD, cols], ra[RA.slot(use)][0:HD, 0:QH], float(HD) ** -0.5, None, ALU.mult)
                        v.tensor_copy(k4[0:HD, cols], ra[RA.slot(use)][HD:2 * HD, 0:QH]).then_inc(ra_free[RA.slot(use)], 1)

                def values(j, p):
                    use = f"V{j}"
                    dve.wait_ge(*a_full(i, use))
                    first = RA.freed_before(use) + 1
                    dve.wait_ge(ra_free[RA.slot(use)], i * RA.frees(RA.slot(use)) + first)
                    v.tensor_scalar(view(vb, 0, GK, p * 2 * HEADS * VW, [[VW, 2 * HEADS], [1, HD]]),
                                    view(ra[RA.slot(use)], 0, GK, 0, [[HD, 2 * HEADS], [1, HD]]),
                                    keep.kmask[:, p:p + 1], None, ALU.mult).then_inc(ra_free[RA.slot(use)], 1)

                def scores(j):
                    n = i * NG + j + 1
                    dve.wait_ge(s_sfull, n)
                    if la == 0:
                        tab = keep.tabs[:, 0:HEADS * GK]
                    else:
                        bottom = (i % SPI) // (SPI - 1)
                        off = bottom * (2 * HEADS * GK) + (1 + (j == NG - 1)) * HEADS * GK
                        tab = view(keep.tabs, 0, QP, off, [[1, HEADS * GK]])
                    v.tensor_tensor(sc[:], s_ps[0:QP, 0:HEADS * GK], tab, ALU.add).then_inc(s_sadd, 1)
                    dve.wait_ge(s_sadd, n)
                    s3 = sc[:].rearrange("q (g k) -> q g k", k=WT)
                    v.tensor_reduce(mx[:], s3, AX.X, ALU.max).then_inc(s_smax, 1)
                    dve.wait_ge(s_smax, n)
                    reach(dve, s_exp, i * NG + j)
                    v.tensor_tensor(sm[:].rearrange("q (g k) -> q g k", k=WT), s3,
                                    view(mx, 0, QP, 0, [[1, 2 * HEADS], [0, WT]]), ALU.subtract).then_inc(s_ssub, 1)

                def outputs(j):
                    n = i * NG + j + 1
                    dve.wait_ge(s_of, n)
                    v.reciprocal(rd[:], view(o_ps, 0, QP, HD, [[VW, 2 * HEADS]])).then_inc(s_rec, 1)
                    dve.wait_ge(s_rec, n)
                    for p in range(2):
                        v.tensor_tensor(view(os_, 0, QP, p * ZW, [[HD, 4], [1, HD]]),
                                        view(o_ps, 0, QP, p * VW, [[2 * VW, 4], [1, HD]]),
                                        view(rd, 0, QP, p, [[2, 4], [0, HD]]), ALU.mult)
                    v.tensor_tensor(view(os_, 0, QP, 128, [[ZW, 2], [HD, 3], [1, HD]]),
                                    view(o_ps, 0, QP, 4 * 2 * VW, [[VW, 2], [0, 3], [1, HD]]),
                                    view(rd, 0, QP, 8, [[1, 2], [0, 3], [0, HD]]), ALU.mult).then_inc(s_od, 1)

                def outputs_lo(j):
                    use = f"OT{j}"
                    dve.wait_ge(s_oth, i * NG + j + 1)
                    for dst, src, p0, rows, c0 in ((ot[1], ot[0], 0, 128, 0), (ot[2], ot[2], REST, REST, 2 * QP)):
                        for p in range(2):
                            o = p * WIN * W + j * 2 * WIN
                            dims = [[WIN, 2], [W, WIN], [1, WIN]]
                            ins = v.tensor_tensor(view(dst, p0, rows, o, dims),
                                                  view(ra[RA.slot(use)], p0, rows, c0 + p * QP, [[WP, 2], [WIN, WIN], [1, WIN]]),
                                                  view(src, p0, rows, o, dims).bitcast(F32), ALU.subtract)
                    ins.then_inc(ra_free[RA.slot(use)], 1)

                def t_lo(name, l, first):
                    for hf, (t0, nt) in enumerate(HALF):
                        cols = slice(t0 * TT, (t0 + nt) * TT)
                        for n, (part, dst, src, rows) in enumerate((("A", z2t[1], z2t[0], slice(0, 128)),
                                                                   ("C", z2t[2], z2t[2], slice(REST, 2 * REST)))):
                            use = f"{name}{part}{hf}"
                            dve.wait_ge(s_hi2, hi2(m, l, first + 2 * hf + n + 1))
                            v.tensor_tensor(dst[rows, cols], rm[RM[l].slot(use)][rows, 0:nt * TT], src[rows, cols].bitcast(F32),
                                            ALU.subtract).then_inc(rm_free[RM[l].slot(use)], 1)

                def mlp_out(n):
                    use = f"W{n}"
                    t0, nt = PAIRS[n]
                    dve.wait_ge(*m_full(m, lm, use))
                    if n == 0:
                        dve.wait_ge(s_x1b, m + 1)
                        reach(dve, s_xo, 32 * m if lm == 0 else 32 * NS)
                    v.tensor_tensor(view(xo, 0, TT, t0 * ZW, [[ZW, nt], [1, DIM]]),
                                    view(rm[RM[lm].slot(use)], 0, TT, 0, [[DIM, nt], [1, DIM]]),
                                    view(x1b, 0, TT, t0 * DIM, [[DIM, nt], [1, DIM]]),
                                    ALU.add).then_inc(rm_free[RM[lm].slot(use)], 1)

                if la is not None:
                    values(0, 1)
                    scores(0)
                if lm is not None:
                    t_lo("T2", lm, 0)
                if la is not None and not (isinstance(i, int) and i == 2 * NS - 1):
                    dve.wait_ge(s_xa, 32 * (i + 2))
                    stats(0, xa, i + 1)
                    normalise(0, z1, xa, i + 1)
                if lm is not None:
                    mlp_out(0)
                if la is not None:
                    scores(1)
                    outputs(0)
                    values(1, 1)
                if lm is not None:
                    mlp_out(1)
                if la is not None:
                    outputs_lo(0)
                    scores(2)
                    outputs(1)
                    values(2, 1)
                if lm is not None:
                    mlp_out(2)
                if la is not None:
                    outputs_lo(1)
                    scores(3)
                    outputs(2)
                    values(3, 1)
                if lm is not None:
                    mlp_out(3)
                if la is not None:
                    outputs_lo(2)
                    outputs(3)
                    outputs_lo(3)
                    dve.wait_ge(s_xr, 32 * (i + 1))
                    reach(dve, s_x1b, i)
                    for n, (t0, nt) in enumerate(PROJ):
                        use = f"P{n}"
                        dve.wait_ge(*a_full(i, use))
                        cols = slice(t0 * DIM, (t0 + nt) * DIM)
                        v.tensor_tensor(x1[:, cols], ra[RA.slot(use)][0:TT, 0:nt * DIM], xr[:, cols],
                                        ALU.add).then_inc(ra_free[RA.slot(use)], 1)
                    for n, (t0, nt) in enumerate(PROJ):
                        dve.wait_ge(*a_freed(i, f"P{n}"))
                        stats(1, x1, i, range(t0, t0 + nt), last=(n == 2))
                if lm == 1:
                    t_lo("T3", 1, 4)
                    for n in range(4):
                        use = f"L{n}"
                        t0, nt = PAIRS[n]
                        dve.wait_ge(*m_full(m, 1, use))
                        if n == 0:
                            reach(dve, s_yz, 32 * (m - NS))
                        v.tensor_copy(yz[:, t0 * DIM:(t0 + nt) * DIM],
                                      rm[RM[1].slot(use)][0:TT, 0:nt * DIM]).then_inc(rm_free[RM[1].slot(use)], 1)

            bodies(dve, body)

        @block.tensor
        def _(pe):
            mm, tr = nc.tensor.matmul, nc.tensor.transpose
            pe.wait_ge(s_init, 2)

            def turn(z, banks, room, full, name):
                for hf, (t0, nt) in enumerate(HALF):
                    for part, f0, rows in (("A", 0, 128), ("C", 128, CR)):
                        use = f"{name}{part}{hf}"
                        b, s_full = full(use)
                        reach(pe, *room(use))
                        for t in range(nt):
                            c = (t0 + t) * ZW + f0
                            last = tr(banks[b][0:rows, t * TT:(t + 1) * TT], z[:, c:c + rows], keep.ident[0:TT, 0:TT])
                        last.then_inc(s_full, 1)

            def body(i, la, lm):
                m = i - 1

                def bank_a(use):
                    return ra[RA.slot(use)]

                def room_a(use):
                    reach(pe, *a_room(i, use))

                def bank_m(use):
                    return rm[RM[lm].slot(use)]

                def room_m(use):
                    reach(pe, *m_room(m, lm, use))

                def values(j):
                    use = f"V{j}"
                    room_a(use)
                    wv = [w[:, 2 * DIM:3 * DIM] for w in keep.w["qkv", la]]
                    for w in range(2):
                        c = slice((2 * j + w) * GK, (2 * j + w + 1) * GK)
                        last = split_passes(nc, bank_a(use)[0:GK, w * DIM:(w + 1) * DIM], *[t[:, c] for t in z1t], *wv, False)
                    last.then_inc(ra_full[RA.slot(use)], 1)

                def scores(j):
                    reach(pe, s_sadd, i * NG + j)
                    for h in range(HEADS):
                        for p in range(2):
                            for w in range(2):
                                c = (2 * j + w) * GK + p * WT
                                q = qm[:, h * SN + c:h * SN + c + WT] if h < 4 else q4[:, c:c + WT]
                                k = (kt if h < 4 else k4)[:, c:c + WT]
                                last = mm(s_ps[w * WP:w * WP + WT, (2 * h + p) * WT:(2 * h + p + 1) * WT], q, k,
                                          start=True, stop=True)
                    last.then_inc(s_sfull, 1)

                def weights_turned(j):
                    n = i * NG + j
                    pe.wait_ge(s_exp, n + 1)
                    reach(pe, s_pte, n)
                    reach(pe, s_od, n)
                    for h in range(HEADS):
                        o = pt_ps[0:GK, h * QP:(h + 1) * QP] if h < 4 else o_ps[0:GK, PT4:PT4 + QP]
                        last = tr(o, pr[:, h * GK:(h + 1) * GK], keep.ident[0:QP, 0:QP])
                    last.then_inc(s_ptf, 1)

                def outputs(j):
                    pe.wait_ge(s_pte, i * NG + j + 1)
                    pe.wait_ge(*a_freed(i, f"V{j}"))
                    for h in range(HEADS):
                        for w in range(2):
                            last = mm(o_ps[w * WP:w * WP + WT, h * 2 * VW:(h + 1) * 2 * VW],
                                      pt[:, h * QP + w * WP:h * QP + w * WP + WT],
                                      view(vb, 0, GK, (w * HEADS + h) * VW, [[2 * HEADS * VW, 2], [1, VW]]),
                                      start=True, stop=True)
                    last.then_inc(s_of, 1)

                def outputs_turned(j):
                    use = f"OT{j}"
                    pe.wait_ge(s_od, i * NG + j + 1)
                    room_a(use)
                    for f0, rows, c0 in ((0, 128, 0), (128, CR, 2 * QP)):
                        for p in range(2):
                            last = tr(bank_a(use)[0:rows, c0 + p * QP:c0 + (p + 1) * QP],
                                      os_[:, p * ZW + f0:p * ZW + f0 + rows], keep.ident[0:QP, 0:QP])
                    last.then_inc(ra_full[RA.slot(use)], 1)

                def mlp_in(gs):
                    for g in gs:
                        use = f"G{g}"
                        hf, f = divmod(g, FT)
                        t0, nt = HALF[hf]
                        room_m(use)
                        last = split_passes(nc, bank_m(use)[:, 0:nt * TT], *[t[:, t0 * TT:(t0 + nt) * TT] for t in z2t],
                                            *[w[:, f * 128:(f + 1) * 128] for w in keep.w["w1", lm]], True)
                        last.then_inc(rm_full[RM[lm].slot(use)], 1)

                def mlp_out(n):
                    use = f"W{n}"
                    t0, nt = PAIRS[n]
                    room_m(use)
                    for t in range(nt):
                        for f in range(FT):
                            c = f * SN + (t0 + t) * TT
                            last = mm(bank_m(use)[0:TT, t * DIM:(t + 1) * DIM], ht[:, c:c + TT],
                                      keep.w["w2", lm][:, f * DIM:(f + 1) * DIM], start=(f == 0), stop=(f == FT - 1))
                    last.then_inc(rm_full[RM[lm].slot(use)], 1)

                if la is not None:
                    pe.wait_ge(s_z[0], i + 1)
                    turn(z1, ra, lambda u: a_room(i, u), lambda u: (RA.slot(u), ra_full[RA.slot(u)]), "T1")
                    pe.wait_ge(*a_freed(i, "T1C1"))
                    for hf in range(2):
                        for name, c0, n in (("Q", 0, 128), ("K", 128, 128), ("B", 256, 2 * HD)):
                            use = f"{name}{hf}"
                            room_a(use)
                            last = split_passes(nc, bank_a(use)[0:n, 0:QH], *[t[:, hf * QH:(hf + 1) * QH] for t in z1t],
                                                *[w[:, c0:c0 + n] for w in keep.w["qkv", la]], True)
                            last.then_inc(ra_full[RA.slot(use)], 1)
                    values(0)
                    for name in "QB":
                        pe.wait_ge(*a_freed(i, f"{name}1"))
                    scores(0)
                if lm is not None:
                    pe.wait_ge(s_z[1], m + 1)
                    turn(z2, rm, lambda u: m_room(m, lm, u), lambda u: (RM[lm].slot(u), rm_full[RM[lm].slot(u)]), "T2")
                    pe.wait_ge(*m_freed(m, lm, "T2C1"))
                    mlp_in(range(2 * FT))
                    mlp_out(0)
                if la is not None:
                    weights_turned(0)
                    scores(1)
                    outputs(0)
                    values(1)
                if lm is not None:
                    mlp_out(1)
                if la is not None:
                    outputs_turned(0)
                    weights_turned(1)
                    scores(2)
                    outputs(1)
                    values(2)
                if lm is not None:
                    mlp_out(2)
                if la is not None:
                    outputs_turned(1)
                    weights_turned(2)
                    scores(3)
                    outputs(2)
                    values(3)
                if lm is not None:
                    mlp_out(3)
                if la is not None:
                    outputs_turned(2)
                    weights_turned(3)
                    outputs(3)
                    outputs_turned(3)
                    pe.wait_ge(*a_freed(i, "OT3"))
                    for n, (t0, nt) in enumerate(PROJ):
                        use = f"P{n}"
                        room_a(use)
                        for t in range(nt):
                            c = slice((t0 + t) * TT, (t0 + t + 1) * TT)
                            last = split_passes(nc, bank_a(use)[0:TT, t * DIM:(t + 1) * DIM], *[o[:, c] for o in ot],
                                                *[w[:] for w in keep.w["proj", la]], False)
                        last.then_inc(ra_full[RA.slot(use)], 1)
                if lm == 1:
                    pe.wait_ge(s_xod, m - NS + 1)
                    turn(xo, rm, lambda u: m_room(m, 1, u), lambda u: (RM[1].slot(u), rm_full[RM[1].slot(u)]), "T3")
                    pe.wait_ge(*m_freed(m, 1, "T3C1"))
                    for n, (t0, nt) in enumerate(PAIRS):
                        use = f"L{n}"
                        room_m(use)
                        for t in range(nt):
                            c = slice((t0 + t) * TT, (t0 + t + 1) * TT)
                            last = split_passes(nc, bank_m(use)[0:TT, t * DIM:(t + 1) * DIM], *[z[:, c] for z in z2t],
                                                *[w[:] for w in keep.w["lin", 1]], False)
                        last.then_inc(rm_full[RM[1].slot(use)], 1)

            bodies(pe, body)


def phase_c(nc, keep, f_syn, ys, out):
    with ExitStack() as ctx:
        def sb(name, shape, dt=F32):
            return ctx.enter_context(nc.sbuf_tensor(name, shape, dt))

        def sem(name):
            return ctx.enter_context(nc.semaphore(name))

        KG = 3
        G = K // KG
        acc = [ctx.enter_context(nc.psum_tensor(f"c_acc{n}", [128, 512], F32)) for n in range(2)]
        fin = [ctx.enter_context(nc.psum_tensor(f"c_fin{n}", [128, 512], F32)) for n in range(2)]
        taps = [sb(f"c_taps{n}", [TT, NJ * TT]) for n in range(2)]
        band_hi = sb("c_band_hi", [TT, K * NJ * TT], F32R)
        band_lo = sb("c_band_lo", [TT, K * NJ * TT], F32R)
        y = [sb(f"c_y{u}", [TT, NT * DIM]) for u in range(2)]
        y_hi = sb("c_y_hi", [TT, PADT * K * C], F32R)
        y_lo = sb("c_y_lo", [TT, PADT * K * C], F32R)
        conv = [sb(f"c_conv{u}", [TT, C * NT]) for u in range(2)]
        direct = [sb(f"c_direct{u}", [TT, C * NT]) for u in range(2)]
        one = sb("c_one", [TT, 1])
        res = [sb(f"c_res{u}", [TT, 4 * TT]) for u in range(2)]

        s_taps = [sem(f"c_taps_in{n}") for n in range(2)]
        s_bhi, s_blo, s_zero, s_one = sem("c_band_hi_done"), sem("c_band_lo_done"), sem("c_zero"), sem("c_one_set")
        s_y = [sem(f"c_y_in{u}") for u in range(2)]
        s_hi, s_lo = sem("c_y_hi_done"), sem("c_y_lo_done")
        s_g = sem("c_filters")
        s_conv, s_dir, s_fin, s_res = sem("c_conv_out"), sem("c_direct_out"), sem("c_final"), sem("c_res_done")
        s_store = [sem(f"c_store{u}") for u in range(2)]
        KC = K * C
        block = ctx.enter_context(nc.Block())

        @block.sync
        def _(sp):
            def load_image(img, u):
                for yy in range(2):
                    first = 2 - yy
                    for t0, nt in ((0, first), (first, NT - first)):
                        y0 = (2 * t0 + yy - SHIFT) % H
                        for x0, nx in ((0, SHIFT), (SHIFT, W - SHIFT)):
                            off = y0 * W * DIM + ((x0 - SHIFT) % W) * DIM
                            sp.dma_start(view(y[u], yy * W + x0, nx, t0 * DIM, [[DIM, nt], [1, DIM]]),
                                         dram(ys, img * (H * W * DIM) + off, [[DIM, nx], [TT * DIM, nt], [1, DIM]])
                                         ).then_inc(s_y[u], 16)

            def load_taps(k):
                for r in range(2):
                    for yy in range(2):
                        if k >= 2 and (r, yy) == (0, 0):
                            sp.wait_ge(s_blo, k - 1)
                        sp.dma_start(view(taps[k % 2], r * W, W, yy * W, [[TT, NJ], [1, W]]),
                                     dram(f_syn.tensor, (k * 11 + r - yy + 1) * FROW, [[1, W], [2 * FROW, NJ], [1, W]])
                                     ).then_inc(s_taps[k % 2], 16)

            load_image(0, 0)
            load_taps(0)
            load_taps(1)
            load_image(1, 1)
            for k in range(2, K):
                load_taps(k)

            def store_image(img, u):
                sp.wait_ge(s_res, img + 1)
                sp.dma_start(dram(out.tensor, img * (C * H * W), [[TT, TT], [TT * TT, 4], [1, TT]]),
                             view(res[u], 0, TT, 0, [[TT, 4], [1, TT]])).then_inc(s_store[u], 16)

            with sp.Fori(0, B // 2 - 1) as pair:
                for u in range(2):
                    img = pair * 2 + u
                    sp.wait_ge(s_lo, (img + 1) * G)
                    sp.wait_ge(s_dir, img + 1)
                    load_image(img + 2, u)
                    store_image(img, u)
            for u in range(2):
                store_image(B - 2 + u, u)
            for u in range(2):
                sp.wait_ge(s_store[u], 16 * (B // 2))

        @block.gpsimd
        def _(pool):
            nc.gpsimd.memset(one[:], 1.0).then_inc(s_one, 1)
            pool.wait_ge(s_one, 1)
            with pool.Fori(0, B // 2) as pair:
                for u in range(2):
                    img = pair * 2 + u
                    pool.wait_ge(s_y[u], (pair + 1) * 128)
                    pool.wait_ge(s_fin, img - u)
                    src = view(y[u], 0, TT, KC, [[1, C], [DIM, NT]])
                    nc.gpsimd.tensor_tensor(direct[u][:].rearrange("p (c t) -> p c t", t=NT), src,
                                            view(one, 0, TT, 0, [[0, C], [0, NT]]), ALU.mult).then_inc(s_dir, 1)

        @block.scalar
        def _(act):
            for k in range(K):
                act.wait_ge(s_taps[k % 2], 64 * (k // 2 + 1))
                nc.scalar.activation(band_hi[:, k * NJ * TT:(k + 1) * NJ * TT], taps[k % 2][:], ACT.Copy).then_inc(s_bhi, 1)
            act.wait_ge(s_zero, 1)
            with act.Fori(0, B // 2) as pair:
                for u in range(2):
                    img = pair * 2 + u
                    act.wait_ge(s_y[u], (pair + 1) * 128)
                    for g in range(G):
                        if u == 0:
                            act.wait_ge(s_g, pair * (2 * G))
                        else:
                            act.wait_ge(s_g, pair * (2 * G) + g + 1)
                        nc.scalar.activation(view(y_hi, 0, TT, 2 * KC + g * KG * C, [[KC, NT], [1, KG * C]]),
                                             view(y[u], 0, TT, g * KG * C, [[DIM, NT], [1, KG * C]]), ACT.Copy).then_inc(s_hi, 1)
                    act.wait_ge(s_g, (img + 1) * G)
                    nc.scalar.activation(conv[u][:].rearrange("p (c t) -> p c t", t=NT),
                                         view(acc[u], 0, TT, 0, [[1, C], [C, NT]]), ACT.Copy).then_inc(s_conv, 1)

        @block.vector
        def _(dve):
            nc.vector.memset(y_hi[:].bitcast(F32), 0.0)
            nc.vector.memset(y_lo[:].bitcast(F32), 0.0).then_inc(s_zero, 1)
            for k in range(K):
                dve.wait_ge(s_bhi, k + 1)
                cols = slice(k * NJ * TT, (k + 1) * NJ * TT)
                nc.vector.tensor_tensor(band_lo[:, cols], taps[k % 2][:], band_hi[:, cols].bitcast(F32),
                                        ALU.subtract).then_inc(s_blo, 1)
            with dve.Fori(0, B // 2) as pair:
                for u in range(2):
                    img = pair * 2 + u
                    for g in range(G):
                        dve.wait_ge(s_hi, img * G + g + 1)
                        o = 2 * KC + g * KG * C
                        dims = [[KC, NT], [1, KG * C]]
                        nc.vector.tensor_tensor(view(y_lo, 0, TT, o, dims),
                                                view(y[u], 0, TT, g * KG * C, [[DIM, NT], [1, KG * C]]),
                                                view(y_hi, 0, TT, o, dims).bitcast(F32), ALU.subtract).then_inc(s_lo, 1)
                    dve.wait_ge(s_fin, img + 1)
                    dve.wait_ge(s_store[u], pair * 16)
                    nc.vector.tensor_copy(res[u][:], fin[u][0:TT, 0:4 * TT]).then_inc(s_res, 1)

        @block.tensor
        def _(pe):
            mm = nc.tensor.matmul
            pe.wait_ge(s_blo, K)
            with pe.Fori(0, B // 2) as pair:
                for u in range(2):
                    img = pair * 2 + u
                    pe.wait_ge(s_conv, img - u)
                    n = 0
                    for g in range(G):
                        pe.wait_ge(s_lo, img * G + g + 1)
                        for k in range(g * KG, (g + 1) * KG):
                            for j in range(NJ):
                                cols = slice((k * NJ + j) * TT, (k * NJ + j + 1) * TT)
                                o, dims = j * KC + k * C, [[KC, NT], [1, C]]
                                for a, b in ((band_hi, y_hi), (band_hi, y_lo), (band_lo, y_hi)):
                                    last = mm(acc[u][0:TT, 0:NT * C], a[:, cols], view(b, 0, TT, o, dims),
                                              start=(n == 0), stop=(n == K * NJ * 3 - 1))
                                    n += 1
                        last.then_inc(s_g, 1)
                    pe.wait_ge(s_conv, img + 1)
                    pe.wait_ge(s_dir, img + 1)
                    pe.wait_ge(s_res, img - u)
                    for q in range(4):
                        cols = slice(q * TT, (q + 1) * TT)
                        mm(fin[u][0:TT, cols], conv[u][:, cols], keep.flip[0:TT, :], start=True, stop=False)
                        last = mm(fin[u][0:TT, cols], direct[u][:, cols], keep.ident[0:TT, 0:TT], start=False, stop=True)
                    last.then_inc(s_fin, 1)


_ORDER = ["x", "xf", "f_ana", "f_syn", "ln1g", "ln1b", "qkvw", "qkvb", "projw", "projb", "rel", "ln2g", "ln2b",
          "w1", "b1", "w2", "b2", "linwT", "linb", "convwT", "convb", "wmask"]


def kernel(**inputs):
    import numpy as np
    import concourse.bacc as bacc
    from concourse.bass_utils import run_bass_kernel_spmd

    src = {k.replace("L0_conv_", ""): np.asarray(v) for k, v in inputs.items()}

    def padded_rows(f):
        rows = np.zeros((K, FS + 2, FROW), f.dtype)
        rows[:, 1:FS + 1, PADF:PADF + FS] = f
        return rows

    arrays = dict(src)
    arrays["xf"] = src["x"][..., ::-1]
    arrays["f_ana"] = padded_rows(src["f_ana"].reshape(K, FS, FS)[..., ::-1])
    arrays["f_syn"] = padded_rows(src["f_syn"].reshape(K, FS, FS))
    side = 2 * WIN - 1
    arrays["rel"] = src["rpb"].transpose(0, 2, 1).reshape(2 * HEADS, side, side)[:, ::-1, ::-1]
    arrays["linwT"] = src["linw"].T
    arrays["convwT"] = src["convw"].reshape(C, DIM).T
    late = np.arange(WIN) >= WIN - SHIFT
    apart_y = np.repeat(late, WIN)[:, None] != np.repeat(late, WIN)[None, :]
    apart_x = np.tile(late, WIN)[:, None] != np.tile(late, WIN)[None, :]
    wmask = np.zeros((QP, 4, 2, WT), np.float32)
    for bottom in range(2):
        for right in range(2):
            for w in range(2):
                for p in range(2):
                    apart = (apart_y & (bottom and p == 1)) | (apart_x & (right and w == 1))
                    wmask[w * WP:w * WP + WT, bottom * 2 + right, p] = np.where(apart, np.float32(-100), np.float32(0))
    arrays["wmask"] = wmask.reshape(QP, 4 * GK)

    nc = bacc.Bacc("TRN2", target_bir_lowering=False, num_devices=1)
    given, args = {}, []
    for name in _ORDER:
        a = np.ascontiguousarray(arrays[name])
        given[f"in_{name}"] = a
        args.append(nc.dram_tensor(f"in_{name}", a.shape, mybir.dt.from_np(a.dtype), kind="ExternalInput").ap())
    res = nc.dram_tensor("out_0", (B, C, H, W), F32, kind="ExternalOutput").ap()
    build(nc, *args, res)
    r = run_bass_kernel_spmd(nc, [given], core_ids=[0])
    return r.results[0]["out_0"]
```

```python
from contextlib import ExitStack

import concourse.bass as bass
from concourse import mybir

F32 = mybir.dt.float32
F32R = mybir.dt.float32r
ALU = mybir.AluOpType
ACT = mybir.ActivationFunctionType
AX = mybir.AxisListType

B, C, H, W = 8, 16, 56, 56
K, FS, WIN = 9, 9, 7
DIM = K * C + C
HEADS, HD = 5, 32
MLP = 4 * DIM
SHIFT = WIN // 2
EPS = 1e-5
LO, REST = 128, DIM - 128
CR = 3 * REST
CK = CR + 2
TT = 2 * W
NT = H // 2
PADT = NT + 4
NJ = 5
SR = 2 * WIN
ST = SR // 2
SN = SR * W
SPI = H // SR
NS = B * SPI
HALF = [(0, 4), (4, 3)]
WT = WIN * WIN
WP = 64
QP = WP + WT
GK = 2 * WT
NG = W // (2 * WIN)
VW = HD + 1
FT = MLP // 128
PADF = W - FS // 2 - 1
FROW = 112
ZW = 128 + CR
HP = H + SHIFT


def view(t, p0, n, off, dims):
    row = t.shape[-1]
    return bass.AP(tensor=t, offset=p0 * row + off, ap=[[row, n]] + [list(d) for d in dims])


def dram(t, off, dims):
    return bass.AP(tensor=t, offset=off, ap=[list(d) for d in dims])


def reach(engine, sem, value):
    if isinstance(value, int) and value <= 0:
        return
    engine.wait_ge(sem, value)


class Ring:

    def __init__(self, uses, banks, readers):
        self.uses, self.banks = uses, banks
        self.at = {u: n for n, u in enumerate(uses)}
        self.weight = [readers.get(u, 1) for u in uses]

    def slot(self, use):
        return self.at[use] % self.banks

    def filled(self, use):
        return self.at[use] // self.banks + 1

    def freed_before(self, use):
        n = self.at[use]
        return sum(self.weight[m] for m in range(n % self.banks, n, self.banks))

    def fills(self, slot):
        return len(range(slot, len(self.uses), self.banks))

    def frees(self, slot):
        return sum(self.weight[slot::self.banks])


def split_passes(nc, out, hi, lo, rest, w_hi, w_lo, w_rest, act_moves):
    pairs = [(hi, w_hi), (lo, w_hi), (hi, w_lo), (rest, w_rest)]
    for n, (a, w) in enumerate(pairs):
        lhs, rhs = (w, a) if act_moves else (a, w)
        last = nc.tensor.matmul(out, lhs, rhs, start=(n == 0), stop=(n == len(pairs) - 1))
    return last


def build(nc, x, xf, f_ana, f_syn, ln1g, ln1b, qkvw, qkvb, projw, projb, rel, ln2g, ln2b, w1, b1, w2, b2,
          linwT, linb, convwT, convb, wmask, out):
    xs0 = nc.dram_tensor("xs0", [B, H, W, DIM], F32, kind="Internal")
    xs1 = nc.dram_tensor("xs1", [B, HP, HP, DIM], F32, kind="Internal")
    ys = nc.dram_tensor("ys", [B, H, W, DIM], F32, kind="Internal")
    relT = nc.dram_tensor("relT", [WT, 2 * HEADS * WT], F32, kind="Internal")
    with ExitStack() as ctx:
        keep = Persistent(nc, ctx)
        phase_a(nc, keep, x, xf, f_ana, ln1g, ln1b, qkvw, qkvb, projw, projb, rel, relT, ln2g, ln2b, w1, b1,
                w2, b2, linwT, linb, convwT, convb, wmask, xs0)
        phase_b(nc, keep, xs0, xs1, ys)
        phase_c(nc, keep, f_syn, ys, out)


class Persistent:

    def __init__(self, nc, ctx):
        def sb(name, shape, dt=F32):
            return ctx.enter_context(nc.sbuf_tensor(name, shape, dt))
        self.ident = sb("ident", [128, 128])
        self.flip = sb("flip", [128, TT])
        self.qmask = sb("qmask", [128, 4])
        self.kmask = sb("kmask", [GK, 2])
        self.tabs = sb("tabs", [QP, 5 * HEADS * GK])
        self.w = {}
        for l in range(2):
            for name, n in (("qkv", 3 * DIM), ("proj", DIM), ("w1", MLP)):
                self.w[name, l] = self.split(sb, f"{name}{l}", n)
            self.w["w2", l] = sb(f"w2_{l}", [128, FT * DIM])
            self.w["b2", l] = sb(f"b2_{l}", [TT, DIM])
        self.w["lin", 1] = self.split(sb, "lin", DIM)

    @staticmethod
    def split(sb, name, n):
        return (sb(name + "_hi", [128, n], F32R), sb(name + "_lo", [128, n], F32R), sb(name + "_rest", [CK, n], F32R))


def phase_a(nc, keep, x, xf, f_ana, ln1g, ln1b, qkvw, qkvb, projw, projb, rel, relT, ln2g, ln2b, w1, b1, w2, b2,
            linwT, linb, convwT, convb, wmask, xs0):
    with ExitStack() as ctx:
        def sb(name, shape, dt=F32):
            return ctx.enter_context(nc.sbuf_tensor(name, shape, dt))

        def sem(name):
            return ctx.enter_context(nc.semaphore(name))

        NB = 5
        psum = [ctx.enter_context(nc.psum_tensor(f"a_ps{n}", [128, 512], F32)) for n in range(8)]
        nat_ps, mir_ps, conv_ps = psum[0], psum[1], psum[3:]
        taps = [sb(f"a_taps{n}", [TT, NJ * TT]) for n in range(2)]
        band_hi = sb("a_band_hi", [TT, K * NJ * TT], F32R)
        band_lo = sb("a_band_lo", [TT, K * NJ * TT], F32R)
        xin = [sb(f"a_xin{u}", [TT, 4 * TT]) for u in range(2)]
        xfin = [sb(f"a_xfin{u}", [TT, 4 * TT]) for u in range(2)]
        img_hi = sb("a_img_hi", [TT, PADT * C], F32R)
        img_lo = sb("a_img_lo", [TT, PADT * C], F32R)
        tok = [sb(f"a_tok{u}", [TT, NT * DIM]) for u in range(2)]
        mats = []
        for l in range(2):
            mats += [("qkv", l, 3 * DIM, qkvw, qkvb, 0), ("proj", l, DIM, projw, projb, None),
                     ("w1", l, MLP, w1, b1, 1)]
        raw_a = {m[:2]: sb(f"raw_a_{m[0]}{m[1]}", [128, m[2]]) for m in mats}
        raw_c = {m[:2]: sb(f"raw_c_{m[0]}{m[1]}", [CR, m[2]]) for m in mats}
        gain_a, gain_c = sb("gain_a", [128, 4]), sb("gain_c", [CR, 4])
        lnb_a, lnb_c = sb("lnb_a", [128, 4]), sb("lnb_c", [CR, 4])
        scaled, scaled_c = sb("scaled", [128, MLP]), sb("scaled_c", [CR, MLP])
        starts, width = {}, 0
        for m in mats:
            starts[m[:2]], width = width, width + m[2]
        starts["lin", 1], width = width, width + DIM
        brow = sb("brow", [CK, width])
        bhi, blo = sb("bhi", [CK, MLP], F32R), sb("blo", [CK, MLP])
        lwt_a, lwt_b = sb("lwt_a", [128, ZW]), sb("lwt_b", [C, ZW])
        mix_a, mix_b = sb("mix_a", [128, DIM]), sb("mix_b", [C, DIM])
        linb_a, linb_b = sb("linb_a", [128, 1]), sb("linb_b", [C, 1])
        relb, msk = sb("relb", [QP, 2 * HEADS * WT]), sb("msk", [QP, 4 * GK])

        s_taps = [sem(f"a_taps_in{n}") for n in range(2)]
        s_bhi, s_blo = sem("a_band_hi_done"), sem("a_band_lo_done")
        s_xin = [sem(f"a_x_in{u}") for u in range(2)]
        s_nat_T, s_mir_T, s_nat, s_ihi, s_ilo = sem("a_nat_T"), sem("a_mir_T"), sem("a_nat"), sem("a_img_hi"), sem("a_img_lo")
        s_conv = [sem(f"a_conv{n}") for n in range(NB)]
        s_free = [sem(f"a_conv_free{n}") for n in range(NB)]
        s_store = [sem(f"a_store{u}") for u in range(2)]
        s_pool, s_zero, s_ident, s_mixz = sem("a_pool"), sem("a_zero"), sem("a_ident"), sem("a_mixz")
        s_raw, s_small, s_mix = sem("a_raw"), sem("a_small"), sem("a_mix")
        s_relT, s_relb = sem("a_relT"), sem("a_relb")
        s_bps, s_prep = sem("a_bias_ps"), sem("a_prep")

        def bank_of(u, k):
            return (u * K + k) % NB

        def nth(u, k):
            return (u * K + k) // NB

        per = [len(range(b, 2 * K, NB)) for b in range(NB)]
        def pieces(m, cols):
            if m != "qkv":
                return [(0, 0, cols)]
            return [(0, 0, 128), (128, DIM, 128), (2 * 128, 128, HD), (2 * 128 + HD, DIM + 128, HD), (2 * DIM, 2 * DIM, DIM)]

        n_pieces = sum(len(pieces(m[0], m[2])) for m in mats)
        RAWS = 16 * (4 * n_pieces)
        SMALL = 16 * (4 * 4 * 2 + 2 * 2 + 2 + 8 + n_pieces + 1)
        MIX = 16 * (K + 2)
        block = ctx.enter_context(nc.Block())

        @block.sync
        def _(sp):
            def load_taps(k):
                for r in range(2):
                    for yy in range(2):
                        if k >= 2 and (r, yy) == (0, 0):
                            sp.wait_ge(s_blo, k - 1)
                        sp.dma_start(view(taps[k % 2], r * W, W, yy * W, [[TT, NJ], [1, W]]),
                                     dram(f_ana.tensor, (k * 11 + r - yy + 1) * FROW, [[1, W], [2 * FROW, NJ], [1, W]])
                                     ).then_inc(s_taps[k % 2], 16)

            def load_image(img, u):
                for t, src in ((xin[u], x), (xfin[u], xf)):
                    sp.dma_start(view(t, 0, TT, 0, [[TT, 4], [1, TT]]),
                                 dram(src.tensor, img * (C * H * W), [[TT, TT], [TT * TT, 4], [1, TT]])
                                 ).then_inc(s_xin[u], 16)

            def store_image(pair, u):
                for k in (K - 2, K - 1):
                    sp.wait_ge(s_free[bank_of(u, k)], pair * per[bank_of(u, k)] + nth(u, k) + 1)
                sp.wait_ge(s_nat, pair * 2 + u + 1)
                sp.dma_start(dram(xs0, (pair * 2 + u) * (H * W * DIM), [[DIM, TT], [TT * DIM, NT], [1, DIM]]),
                             view(tok[u], 0, TT, 0, [[DIM, NT], [1, DIM]])).then_inc(s_store[u], 16)

            load_image(0, 0)
            load_taps(0)
            load_taps(1)
            load_image(1, 1)
            for k in range(2, K):
                load_taps(k)
            with sp.Fori(0, B // 2 - 1) as pair:
                for u in range(2):
                    sp.wait_ge(s_nat_T, pair * 2 + u + 1)
                    sp.wait_ge(s_mir_T, pair * 2 + u + 1)
                    load_image(pair * 2 + u + 2, u)
                    store_image(pair, u)
            for u in range(2):
                store_image(B // 2 - 1, u)
            for u in range(2):
                sp.wait_ge(s_store[u], 16 * (B // 2))

        @block.gpsimd
        def _(pool):
            gp = nc.gpsimd
            n = [0]

            def step(ins):
                n[0] += 1
                ins.then_inc(s_pool, 1)
                pool.wait_ge(s_pool, n[0])

            for t in (mix_a, mix_b, keep.flip):
                gp.memset(t[:], 0.0)
            gp.memset(relb[:], 0.0)
            gp.memset(keep.qmask[:], float(HD) ** -0.5)
            gp.memset(keep.kmask[:], 1.0)
            gp.memset(keep.ident[:], 0.0).then_inc(s_mixz, 1)
            pool.wait_ge(s_mixz, 1)
            step(gp.affine_select(out=keep.ident[:], in_=keep.ident[:], compare_op=ALU.not_equal, fill=1.0, base=0,
                                  pattern=[[-1, 128]], channel_multiplier=1))
            for r in range(2):
                cols = keep.flip[:, r * W:(r + 1) * W]
                gp.affine_select(out=cols, in_=cols, compare_op=ALU.not_equal, fill=1.0,
                                 base=-(r * W + W - 1), pattern=[[1, W]], channel_multiplier=1)
            step(gp.affine_select(out=keep.qmask[:], in_=keep.qmask[:], compare_op=ALU.is_ge, fill=0.0, base=0,
                                  pattern=[[-HD, 4]], channel_multiplier=1))
            gp.affine_select(out=keep.qmask[:], in_=keep.qmask[:], compare_op=ALU.is_ge, fill=0.0, base=HD - 1,
                             pattern=[[HD, 4]], channel_multiplier=-1)
            gp.affine_select(out=keep.kmask[:, 0:1], in_=keep.kmask[:, 0:1], compare_op=ALU.is_ge, fill=0.0,
                             base=WT - 1, pattern=[[0, 1]], channel_multiplier=-1)
            gp.affine_select(out=keep.kmask[:, 1:2], in_=keep.kmask[:, 1:2], compare_op=ALU.is_ge, fill=0.0,
                             base=-WT, pattern=[[0, 1]], channel_multiplier=1)
            with pool.Fori(0, WIN) as yi:
                for xi in range(WIN):
                    pool.dma_start(dram(relT, yi * (WIN * 2 * HEADS * WT) + xi * (2 * HEADS * WT),
                                        [[WT, 2 * HEADS], [WIN, WIN], [1, WIN]]),
                                   dram(rel.tensor, yi * (-(2 * WIN - 1)) + ((WIN - 1) * (2 * WIN - 1) + WIN - 1 - xi),
                                        [[(2 * WIN - 1) ** 2, 2 * HEADS], [2 * WIN - 1, WIN], [1, WIN]])
                                   ).then_inc(s_relT, 16)
            pool.wait_ge(s_relT, 16 * WT)
            for p0 in (0, WP):
                pool.dma_start(relb[p0:p0 + WT, :],
                               dram(relT, 0, [[2 * HEADS * WT, WT], [1, 2 * HEADS * WT]])).then_inc(s_relb, 16)
            pool.dma_start(msk[:], wmask).then_inc(s_relb, 16)
            pool.wait_ge(s_raw, RAWS)
            pool.wait_ge(s_small, SMALL)
            for m, l, cols, _, _, ln in mats:
                hi, lo, rest = keep.w[m, l]
                ra, rc = raw_a[m, l], raw_c[m, l]
                if ln is not None:
                    g = 2 * l + ln
                    gp.tensor_scalar(scaled[:, 0:cols], ra[:], gain_a[:, g:g + 1], None, ALU.mult)
                    step(gp.tensor_scalar(scaled_c[:, 0:cols], rc[:], gain_c[:, g:g + 1], None, ALU.mult))
                    ra, rc = scaled, scaled_c
                gp.tensor_copy(hi[:], ra[:, 0:cols])
                step(gp.tensor_copy(rest[0:CR, :], rc[:, 0:cols]))
                step(gp.tensor_tensor(lo[:], ra[:, 0:cols], hi[:].bitcast(F32), ALU.subtract))
                step(gp.tensor_tensor(rest[2 * REST:CR, :], rc[2 * REST:CR, 0:cols],
                                      rest[2 * REST:CR, :].bitcast(F32), ALU.subtract))
            pool.wait_ge(s_relb, 48)
            for edge in range(5):
                for h in range(HEADS):
                    o = view(keep.tabs, 0, QP, edge * HEADS * GK + h * GK, [[WT, 2], [1, WT]])
                    r = view(relb, 0, QP, (min(edge, 1) * HEADS + h) * WT, [[0, 2], [1, WT]])
                    if edge == 0:
                        last = gp.tensor_copy(o, r)
                    else:
                        last = gp.tensor_tensor(o, r, view(msk, 0, QP, (edge - 1) * GK, [[WT, 2], [1, WT]]), ALU.add)
            step(last)

        @block.scalar
        def _(act):
            for m, l, cols, wt, _, _ in mats:
                for d0, s0, nn in pieces(m, cols):
                    act.dma_start(raw_a[m, l][:, d0:d0 + nn],
                                  dram(wt.tensor, l * DIM * cols + s0, [[cols, 128], [1, nn]])).then_inc(s_raw, 16)
                    for rep in range(3):
                        act.dma_start(raw_c[m, l][rep * REST:(rep + 1) * REST, d0:d0 + nn],
                                      dram(wt.tensor, (l * DIM + 128) * cols + s0, [[cols, REST], [1, nn]])).then_inc(s_raw, 16)
            for l in range(2):
                for ln, (g, b) in enumerate(((ln1g, ln1b), (ln2g, ln2b))):
                    col = 2 * l + ln
                    for ta, tc, src in ((gain_a, gain_c, g), (lnb_a, lnb_c, b)):
                        act.dma_start(ta[:, col:col + 1], dram(src.tensor, l * DIM, [[1, 128], [1, 1]])).then_inc(s_small, 16)
                        for rep in range(3):
                            act.dma_start(tc[rep * REST:(rep + 1) * REST, col:col + 1],
                                          dram(src.tensor, l * DIM + 128, [[1, REST], [1, 1]])).then_inc(s_small, 16)
                act.dma_start(view(keep.w["w2", l], 0, 128, 0, [[DIM, FT], [1, DIM]]),
                              dram(w2.tensor, l * MLP * DIM, [[DIM, 128], [128 * DIM, FT], [1, DIM]])).then_inc(s_small, 16)
                act.dma_start(keep.w["b2", l][:], dram(b2.tensor, l * DIM, [[0, TT], [1, DIM]])).then_inc(s_small, 16)
            act.wait_ge(s_zero, 1)
            for m, l, cols, _, b, _ in mats:
                c0 = starts[m, l]
                for d0, s0, nn in pieces(m, cols):
                    act.dma_start(brow[CR:CK, c0 + d0:c0 + d0 + nn],
                                  dram(b.tensor, l * cols + s0, [[0, 2], [1, nn]])).then_inc(s_small, 16)
            for t, r0, r1 in ((lwt_a, 0, 128), (lwt_b, 128, K * C)):
                act.dma_start(t[:, 0:128], linwT[r0:r1, 0:128]).then_inc(s_small, 16)
                for rep in range(3):
                    act.dma_start(t[:, 128 + rep * REST:128 + (rep + 1) * REST], linwT[r0:r1, 128:DIM]).then_inc(s_small, 16)
            act.dma_start(linb_a[:], dram(linb.tensor, 0, [[1, 128], [1, 1]])).then_inc(s_small, 16)
            act.dma_start(linb_b[:], dram(linb.tensor, 128, [[1, C], [1, 1]])).then_inc(s_small, 16)
            c0 = starts["lin", 1]
            act.dma_start(brow[CR:CK, c0 + K * C:c0 + DIM], dram(convb.tensor, 0, [[0, 2], [1, C]])).then_inc(s_small, 16)
            act.wait_ge(s_mixz, 1)
            for k in range(K):
                t, p0 = (mix_a, k * C) if k < 8 else (mix_b, 0)
                act.dma_start(t[p0:p0 + C, k * C:(k + 1) * C], convwT[0:C, :]).then_inc(s_mix, 16)
            act.dma_start(mix_a[:, K * C:DIM], convwT[C:C + 128, :]).then_inc(s_mix, 16)
            act.dma_start(mix_b[:, K * C:DIM], convwT[C + 128:DIM, :]).then_inc(s_mix, 16)
            for k in range(K):
                act.wait_ge(s_taps[k % 2], 64 * (k // 2 + 1))
                nc.scalar.activation(band_hi[:, k * NJ * TT:(k + 1) * NJ * TT], taps[k % 2][:], ACT.Copy).then_inc(s_bhi, 1)

            with act.Fori(0, B // 2) as pair:
                for u in range(2):
                    img = pair * 2 + u
                    act.wait_ge(s_mir_T, img + 1)
                    b = bank_of(1 - u, K - 1)
                    act.wait_ge(s_conv[b], pair * per[b] + u * (nth(0, K - 1) + 1))
                    act.wait_ge(s_zero, 1)
                    nc.scalar.activation(view(img_hi, 0, TT, 2 * C, [[1, C], [C, NT]]),
                                         view(mir_ps, 0, TT, 0, [[NT, C], [1, NT]]), ACT.Relu).then_inc(s_ihi, 1)
                    act.wait_ge(s_nat_T, img + 1)
                    act.wait_ge(s_store[u], pair * 16)
                    nc.scalar.activation(view(tok[u], 0, TT, K * C, [[1, C], [DIM, NT]]),
                                         view(nat_ps, 0, TT, 0, [[NT, C], [1, NT]]), ACT.Relu).then_inc(s_nat, 1)
                    for k in range(0, K, 2):
                        b = bank_of(u, k)
                        act.wait_ge(s_conv[b], pair * per[b] + nth(u, k) + 1)
                        nc.scalar.activation(view(tok[u], 0, TT, k * C, [[DIM, NT], [1, C]]),
                                             view(conv_ps[b], 0, TT, 0, [[C, NT], [1, C]]), ACT.Copy).then_inc(s_free[b], 1)

        @block.vector
        def _(dve):
            nc.vector.memset(brow[:], 0.0)
            nc.vector.memset(img_hi[:].bitcast(F32), 0.0)
            nc.vector.memset(img_lo[:].bitcast(F32), 0.0).then_inc(s_zero, 1)
            for k in range(K):
                dve.wait_ge(s_bhi, k + 1)
                cols = slice(k * NJ * TT, (k + 1) * NJ * TT)
                nc.vector.tensor_tensor(band_lo[:, cols], taps[k % 2][:], band_hi[:, cols].bitcast(F32),
                                        ALU.subtract).then_inc(s_blo, 1)
            with dve.Fori(0, B // 2) as pair:
                for u in range(2):
                    img = pair * 2 + u
                    dve.wait_ge(s_ihi, img + 1)
                    nc.vector.scalar_tensor_tensor(view(img_lo, 0, TT, 2 * C, [[1, C], [C, NT]]),
                                                   view(mir_ps, 0, TT, 0, [[NT, C], [1, NT]]), 0.0,
                                                   view(img_hi, 0, TT, 2 * C, [[1, C], [C, NT]]).bitcast(F32),
                                                   ALU.max, ALU.subtract).then_inc(s_ilo, 1)
                    for k in range(1, K, 2):
                        b = bank_of(u, k)
                        dve.wait_ge(s_conv[b], pair * per[b] + nth(u, k) + 1)
                        dve.wait_ge(s_store[u], pair * 16)
                        nc.vector.tensor_copy(view(tok[u], 0, TT, k * C, [[DIM, NT], [1, C]]),
                                              view(conv_ps[b], 0, TT, 0, [[C, NT], [1, C]])).then_inc(s_free[b], 1)
            n = 0

            def step(ins):
                nonlocal n
                n += 1
                ins.then_inc(s_prep, 1)
                dve.wait_ge(s_prep, n)

            dve.wait_ge(s_small, SMALL)
            dve.wait_ge(s_bps, 1)
            dve.wait_ge(s_pool, 1)
            hi, lo, rest = keep.w["lin", 1]
            nc.vector.tensor_copy(hi[:], psum[6][:, 0:DIM])
            step(nc.vector.tensor_copy(rest[0:CR, :], psum[6][0:CR, DIM:2 * DIM]))
            nc.vector.tensor_tensor(lo[:], psum[6][:, 0:DIM], hi[:].bitcast(F32), ALU.subtract)
            nc.vector.tensor_tensor(rest[2 * REST:CR, :], psum[6][2 * REST:CR, DIM:2 * DIM],
                                    rest[2 * REST:CR, :].bitcast(F32), ALU.subtract)
            for m, l, banks in (("qkv", 0, (0,)), ("w1", 0, (1, 2)), ("qkv", 1, (3,)), ("w1", 1, (4, 5)), ("lin", 1, (7,))):
                c0 = starts[m, l]
                left = {"qkv": 3 * DIM, "w1": MLP, "lin": DIM}[m]
                for b in banks:
                    nn = min(512, left)
                    last = nc.vector.tensor_tensor(brow[CR:CK, c0:c0 + nn], brow[CR:CK, c0:c0 + nn],
                                                   psum[b][CR:CK, 0:nn], ALU.add)
                    c0, left = c0 + nn, left - nn
            step(last)
            for m, l in starts:
                rest = keep.w[m, l][2]
                cols = rest.shape[1]
                src = brow[CR:CK, starts[m, l]:starts[m, l] + cols]
                step(nc.vector.tensor_copy(bhi[CR:CK, 0:cols], src))
                step(nc.vector.tensor_tensor(blo[CR:CK, 0:cols], src, bhi[CR:CK, 0:cols].bitcast(F32), ALU.subtract))
                step(nc.vector.tensor_scalar(blo[CR:CK, 0:cols], blo[CR:CK, 0:cols], keep.ident[CR:CK, CR + 1:CK], None, ALU.mult))
                step(nc.vector.scalar_tensor_tensor(rest[CR:CK, :], bhi[CR:CK, 0:cols].bitcast(F32), keep.ident[CR:CK, CR:CR + 1],
                                                    blo[CR:CK, 0:cols], ALU.mult, ALU.add))

        @block.tensor
        def _(pe):
            def turn(u, img):
                pe.wait_ge(s_xin[u], (img - u) * 16 + 32)
                pe.wait_ge(s_ilo, img)
                for q in range(4):
                    last = nc.tensor.transpose(mir_ps[0:TT, q * TT:(q + 1) * TT], xfin[u][:, q * TT:(q + 1) * TT],
                                               keep.ident[0:TT, 0:TT])
                last.then_inc(s_mir_T, 1)
                pe.wait_ge(s_nat, img)
                for q in range(4):
                    last = nc.tensor.transpose(nat_ps[0:TT, q * TT:(q + 1) * TT], xin[u][:, q * TT:(q + 1) * TT],
                                               keep.ident[0:TT, 0:TT])
                last.then_inc(s_nat_T, 1)

            pe.wait_ge(s_pool, 1)
            pe.wait_ge(s_blo, K)
            with pe.Fori(0, B // 2) as pair:
                for u in range(2):
                    img = pair * 2 + u
                    turn(u, img)
                    pe.wait_ge(s_ilo, img + 1)
                    for k in range(K):
                        b = bank_of(u, k)
                        pe.wait_ge(s_free[b], pair * per[b] + nth(u, k))
                        n = 0
                        for j in range(NJ):
                            cols = slice((k * NJ + j) * TT, (k * NJ + j + 1) * TT)
                            rows = slice(j * C, (j + NT) * C)
                            for a, m in ((band_hi, img_hi), (band_hi, img_lo), (band_lo, img_hi)):
                                last = nc.tensor.matmul(conv_ps[b][0:TT, 0:NT * C], a[:, cols], m[:, rows],
                                                        start=(n == 0), stop=(n == 3 * NJ - 1))
                                n += 1
                        last.then_inc(s_conv[b], 1)
            pe.wait_ge(s_raw, RAWS)
            pe.wait_ge(s_small, SMALL)
            pe.wait_ge(s_mix, MIX)
            for b in range(NB):
                pe.wait_ge(s_free[b], per[b] * (B // 2))
            pe.wait_ge(s_nat, B)
            pe.wait_ge(s_ilo, B)

            def bcast(t, p, col, n):
                return view(t, 0, p, col, [[0, n]])

            for (m, l, ln), banks in ((("qkv", 0, 0), (0,)), (("w1", 0, 1), (1, 2)), (("qkv", 1, 0), (3,)), (("w1", 1, 1), (4, 5))):
                c0, total = 0, raw_a[m, l].shape[1]
                for b in banks:
                    nn = min(512, total - c0)
                    nc.tensor.matmul(psum[b][0:CK, 0:nn], bcast(lnb_a, 128, 2 * l + ln, CK), raw_a[m, l][:, c0:c0 + nn],
                                     start=True, stop=False)
                    nc.tensor.matmul(psum[b][0:CK, 0:nn], bcast(lnb_c, REST, 2 * l + ln, CK), raw_c[m, l][0:REST, c0:c0 + nn],
                                     start=False, stop=True)
                    c0 += nn
            for o, wa, wb in ((psum[6][:, 0:DIM], lwt_a[:, 0:128], lwt_b[:, 0:128]),
                              (psum[6][0:CR, DIM:2 * DIM], lwt_a[:, 128:ZW], lwt_b[:, 128:ZW]),
                              (psum[7][0:CK, 0:DIM], bcast(linb_a, 128, 0, CK), bcast(linb_b, C, 0, CK))):
                nc.tensor.matmul(o, wa, mix_a[:], start=True, stop=False)
                last = nc.tensor.matmul(o, wb, mix_b[:], start=False, stop=True)
            last.then_inc(s_bps, 1)


def phase_b(nc, keep, xs0, xs1, ys):
    with ExitStack() as ctx:
        def sb(name, shape, dt=F32):
            return ctx.enter_context(nc.sbuf_tensor(name, shape, dt))

        def sem(name):
            return ctx.enter_context(nc.semaphore(name))

        def bank(name):
            return ctx.enter_context(nc.psum_tensor(name, [128, 512], F32))

        ra = [bank(f"ra{n}") for n in range(3)]
        rm = [bank(f"rm{n}") for n in range(2)]
        s_ps, pt_ps, o_ps = bank("s_ps"), bank("pt_ps"), bank("o_ps")
        PT4 = HEADS * 2 * VW

        xa, xr = sb("xa", [TT, ST * DIM]), sb("xr", [TT, ST * DIM])
        x1, x1b = sb("x1", [TT, ST * DIM]), sb("x1b", [TT, ST * DIM])
        xo, yz = sb("xo", [TT, ST * ZW]), sb("yz", [TT, ST * DIM])
        z1, z2 = sb("z1", [TT, ST * ZW]), sb("z2", [TT, ST * ZW])
        st = [sb(f"st{n}", [TT, ST * 6]) for n in range(2)]
        mean = [sb(f"mean{n}", [TT, ST]) for n in range(2)]
        rs = [sb(f"rs{n}", [TT, ST]) for n in range(2)]
        half, mhalf, by_dim, eps = sb("half", [TT, ST]), sb("mhalf", [TT, ST]), sb("by_dim", [TT, ST]), sb("eps", [TT, ST])
        one = sb("one", [TT, 1])
        ln_tmp = [[sb(f"ln_tmp{n}_{k}", [TT, ST]) for k in range(8)] for n in range(2)]
        z1t = [sb("z1t_hi", [128, SN], F32R), sb("z1t_lo", [128, SN], F32R), sb("z1t_rest", [CK, SN], F32R)]
        z2t = [sb("z2t_hi", [128, SN], F32R), sb("z2t_lo", [128, SN], F32R), sb("z2t_rest", [CK, SN], F32R)]
        ot = [sb("ot_hi", [128, SN], F32R), sb("ot_lo", [128, SN], F32R), sb("ot_rest", [CK, SN], F32R)]
        qm = sb("qm", [128, 4 * SN])
        kt = sb("kt", [128, SN])
        q4, k4 = sb("q4", [128, SN]), sb("k4", [128, SN])
        VG = 2 * 2 * HEADS * VW
        vb = sb("vb", [GK, NG * VG])
        sc = sb("sc", [QP, HEADS * GK])
        mx = sb("mx", [QP, 2 * HEADS])
        sm = sb("sm", [QP, HEADS * GK])
        pr = sb("pr", [QP, HEADS * GK])
        pt = sb("pt", [GK, HEADS * QP])
        rd = sb("rd", [QP, 2 * HEADS])
        os_ = sb("os", [QP, 2 * ZW])
        ht = sb("ht", [128, FT * SN])

        s_xa, s_xr, s_xo, s_yz, s_dup = sem("xa_in"), sem("xr_in"), sem("xo_out"), sem("yz_out"), sem("dup")
        s_init = sem("b_init")
        ra_full = [sem(f"ra_full{n}") for n in range(3)]
        ra_free = [sem(f"ra_free{n}") for n in range(3)]
        rm_full = [sem(f"rm_full{n}") for n in range(2)]
        rm_free = [sem(f"rm_free{n}") for n in range(2)]
        s_st = [sem("stats1"), sem("stats2")]
        s_rs = [sem("rs1"), sem("rs2")]
        s_norm = [sem("norm1"), sem("norm2")]
        s_z = [sem("z1_full"), sem("z2_full")]
        s_hi1, s_hi2, s_oth = sem("z1t_hi_done"), sem("z2t_hi_done"), sem("ot_hi_done")
        s_sfull, s_sadd, s_smax, s_ssub = sem("s_full"), sem("s_add"), sem("s_max"), sem("s_sub")
        s_exp, s_ptf, s_pte, s_of, s_rec, s_od = (sem("exp_done"), sem("pt_full"), sem("pt_out"), sem("o_full"),
                                                  sem("o_rec"), sem("o_done"))
        s_x1b, s_xod = sem("x1b_done"), sem("xo_dup")

        FRONT = ["T1A0", "T1C0", "T1A1", "T1C1", "Q0", "K0", "B0", "Q1", "K1", "B1", "V0", "V1", "V2", "V3"]
        V_READERS = {f"V{j}": 2 for j in range(NG)}
        PRO = Ring(FRONT, 3, V_READERS)
        RA = Ring(["OT0", "OT1", "T1A0", "T1C0", "T1A1", "T1C1", "OT2", "Q0", "K0", "B0", "OT3", "Q1", "P0", "P1", "P2",
                   "K1", "B1", "V0", "V1", "V2", "V3"], 3, V_READERS)
        END = Ring(["OT0", "OT1", "OT2", "OT3", "P0", "P1", "P2"], 3, {})
        MLP_USES = ["T2A0", "T2C0", "T2A1", "T2C1"] + [f"G{g}" for g in range(2 * FT)] + ["W0", "W1", "W2", "W3"]
        LIN_USES = ["T3A0", "T3C0", "T3A1", "T3C1", "L0", "L1", "L2", "L3"]
        RM = [Ring(MLP_USES, 2, {}), Ring(MLP_USES + LIN_USES, 2, {})]
        NM = [len(r.uses) // 2 for r in RM]
        PAIRS = [(0, 2), (2, 2), (4, 2), (6, 1)]
        RS_STEPS = 5
        PROJ = [(0, 3), (3, 3), (6, 1)]
        QH = SN // 2

        def ring_a(i):
            if isinstance(i, int) and i < 0:
                return PRO
            return END if isinstance(i, int) and i == 2 * NS - 1 else RA

        def bank_a(i, use):
            return ra[ring_a(i).slot(use)]

        def a_full(i, use):
            ring = ring_a(i)
            s = ring.slot(use)
            before = 0 if ring is PRO else PRO.fills(s) + i * RA.fills(s)
            return ra_full[s], before + ring.filled(use)

        def a_room(i, use):
            ring = ring_a(i)
            s = ring.slot(use)
            before = 0 if ring is PRO else PRO.frees(s) + i * RA.frees(s)
            return ra_free[s], before + ring.freed_before(use)

        def a_freed(i, use, readers=None):
            ring = ring_a(i)
            s, n = a_room(i, use)
            return s, n + (ring.weight[ring.at[use]] if readers is None else readers)

        def m_base(m, l):
            return m * NM[0] if l == 0 else m * NM[1] + NS * (NM[0] - NM[1])

        def m_full(m, l, use):
            return rm_full[RM[l].slot(use)], m_base(m, l) + RM[l].filled(use)

        def m_freed(m, l, use):
            return rm_free[RM[l].slot(use)], m_base(m, l) + RM[l].filled(use)

        def m_room(m, l, use):
            return rm_free[RM[l].slot(use)], m_base(m, l) + RM[l].filled(use) - 1

        def hi2(m, l, n):
            return (m * 4 if l == 0 else m * 8 - NS * 4) + n

        block = ctx.enter_context(nc.Block())

        def bodies(engine, body):
            body(-1, None, None, 0)
            body(0, 0, None, 0)
            body(1, 0, 0, 0)
            with engine.Fori(2, NS - 1) as i:
                body(i, 0, 0, 0)
            body(NS - 1, 0, 0, 1)
            body(NS, 1, 0, 1)
            body(NS + 1, 1, 1, 1)
            with engine.Fori(NS + 2, 2 * NS - 1) as i:
                body(i, 1, 1, 1)
            body(2 * NS - 1, 1, 1, None)
            body(2 * NS, None, 1, None)

        @block.sync
        def _(sp):
            def strip(n, l, yy):
                if l == 0:
                    return dram(xs0, n * (SR * W * DIM) + yy * W * DIM, [[DIM, W], [TT * DIM, ST], [1, DIM]])
                k = n - NS
                off = k * (SR * HP * DIM) + (k // SPI) * (SHIFT * HP * DIM) + (SHIFT + yy) * HP * DIM + SHIFT * DIM
                return dram(xs1, off, [[DIM, W], [2 * HP * DIM, ST], [1, DIM]])

            def load(t, s, n, l):
                for yy in range(2):
                    sp.dma_start(view(t, yy * W, W, 0, [[DIM, ST], [1, DIM]]), strip(n, l, yy)).then_inc(s, 16)

            def store(m, l):
                for yy in range(2):
                    if l == 0:
                        off = m * (SR * HP * DIM) + (m // SPI) * (SHIFT * HP * DIM) + yy * HP * DIM
                        sp.dma_start(dram(xs1, off, [[DIM, W], [2 * HP * DIM, ST], [1, DIM]]),
                                     view(xo, yy * W, W, 0, [[ZW, ST], [1, DIM]])).then_inc(s_xo, 16)
                    else:
                        sp.dma_start(dram(ys, (m - NS) * (SR * W * DIM) + yy * W * DIM, [[DIM, W], [TT * DIM, ST], [1, DIM]]),
                                     view(yz, yy * W, W, 0, [[DIM, ST], [1, DIM]])).then_inc(s_yz, 16)

            def repeat_margins(b0, nb):
                img, row = HP * HP * DIM, HP * DIM
                for b in range(b0, b0 + nb):
                    sp.dma_start(dram(xs1, b * img + W * DIM, [[row, H], [1, SHIFT * DIM]]),
                                 dram(xs1, b * img, [[row, H], [1, SHIFT * DIM]])).then_inc(s_dup, 16)
                    sp.dma_start(dram(xs1, b * img + H * row, [[row, SHIFT], [1, W * DIM]]),
                                 dram(xs1, b * img, [[row, SHIFT], [1, W * DIM]])).then_inc(s_dup, 16)
                    sp.dma_start(dram(xs1, b * img + H * row + W * DIM, [[row, SHIFT], [1, SHIFT * DIM]]),
                                 dram(xs1, b * img, [[row, SHIFT], [1, SHIFT * DIM]])).then_inc(s_dup, 16)

            def body(i, la, lm, ahead=None):
                if ahead is not None:
                    sp.wait_ge(s_norm[0], i + 2)
                    load(xa, s_xa, i + 2, ahead)
                if lm is not None:
                    use = "W3" if lm == 0 else "L3"
                    sp.wait_ge(*m_freed(i - 1, lm, use))
                    store(i - 1, lm)
                if la is not None and not (isinstance(i, int) and i == 2 * NS - 1):
                    sp.wait_ge(*a_freed(i, "P2"))
                    nxt = 1 if (isinstance(i, int) and i == NS - 1) or la == 1 else 0
                    load(xr, s_xr, i + 1, nxt)

            load(xa, s_xa, 0, 0)
            load(xr, s_xr, 0, 0)
            sp.wait_ge(s_norm[0], 1)
            load(xa, s_xa, 1, 0)
            body(0, 0, None, 0)
            body(1, 0, 0, 0)
            with sp.Fori(2, NS - 2) as i:
                body(i, 0, 0, 0)
            sp.wait_ge(s_xo, 32 * (NS - 3))
            repeat_margins(0, B - 1)
            sp.wait_ge(s_dup, 48 * (B - 1))
            body(NS - 2, 0, 0, 1)
            body(NS - 1, 0, 0, 1)
            body(NS, 1, 0, 1)
            sp.wait_ge(s_xo, 32 * NS)
            repeat_margins(B - 1, 1)
            sp.wait_ge(s_dup, 48 * B)
            with sp.Fori(NS + 1, 2 * NS - 2) as i:
                body(i, 1, 1, 1)
            body(2 * NS - 2, 1, 1)
            body(2 * NS - 1, 1, 1)
            body(2 * NS, None, 1)
            sp.wait_ge(s_yz, 32 * NS)

        @block.gpsimd
        def _(pool):
            gp = nc.gpsimd

            def inv_std(n, i):
                me, se, mo, so = (view(st[n], 0, TT, c, [[6, ST]]) for c in (1, 2, 4, 5))
                total, diff, sq, hdiff, sq1, hsq, sq2, var = ln_tmp[n]
                steps = [[(total[:], me, mo, ALU.add), (diff[:], me, mo, ALU.subtract), (sq[:], se, so, ALU.add)],
                         [(mean[n][:], total[:], half[:], ALU.mult), (hdiff[:], diff[:], half[:], ALU.mult),
                          (sq1[:], sq[:], by_dim[:], ALU.mult)],
                         [(hsq[:], hdiff[:], hdiff[:], ALU.mult), (sq2[:], sq1[:], eps[:], ALU.add)],
                         [(var[:], hsq[:], sq2[:], ALU.add)],
                         [(rs[n][:], var[:], mhalf[:], ALU.pow)]]
                pool.wait_ge(s_st[n], i + 1)
                for k, ops in enumerate(steps):
                    if k:
                        pool.wait_ge(s_rs[n], len(steps) * i + k)
                    for o, x_, y_, op in ops:
                        ins = gp.tensor_tensor(o, x_, y_, op)
                    ins.then_inc(s_rs[n], 1)
                assert len(steps) == RS_STEPS

            def repeat_rest(t, s):
                once = view(t, 0, TT, 128, [[ZW, ST], [0, 2], [1, REST]])
                gp.tensor_tensor(view(t, 0, TT, DIM, [[ZW, ST], [REST, 2], [1, REST]]), once,
                                 view(one, 0, TT, 0, [[0, ST], [0, 2], [0, REST]]), ALU.mult).then_inc(s, 1)

            for t, c in ((half, 0.5), (by_dim, 1.0 / DIM), (eps, EPS), (one, 1.0)):
                gp.memset(t[:], c)
            gp.memset(mhalf[:], -0.5).then_inc(s_init, 1)
            pool.wait_ge(s_init, 1)

            def body(i, la, lm, ln):
                if lm is not None:
                    pool.wait_ge(s_norm[1], i)
                    repeat_rest(z2, s_z[1])
                    for n, t in enumerate(range(ST)):
                        ins = gp.tensor_tensor(x1b[:, t * DIM:(t + 1) * DIM], x1[:, t * DIM:(t + 1) * DIM],
                                               keep.w["b2", lm][:], ALU.add)
                    ins.then_inc(s_x1b, 1)
                if ln is not None:
                    inv_std(0, i + 1)
                    pool.wait_ge(s_norm[0], i + 2)
                    repeat_rest(z1, s_z[0])
                if lm == 1:
                    pool.wait_ge(*m_freed(i - 1, 1, "W3"))
                    repeat_rest(xo, s_xod)
                if la is not None:
                    inv_std(1, i)

            bodies(pool, body)

        @block.scalar
        def _(act):
            act_ = nc.scalar.activation

            def body(i, la, lm, ln):
                m = i - 1

                def front_hi(hf):
                    t0, nt = HALF[hf]
                    for part, dst, rows in (("A", z1t[0], 128), ("C", z1t[2], CR)):
                        use = f"T1{part}{hf}"
                        act.wait_ge(*a_full(i, use))
                        act_(view(dst, 0, rows, t0 * 2 * WIN, [[WIN, 2 * nt], [GK, 8], [1, WIN]]),
                             view(bank_a(i, use), 0, rows, 0, [[W, 2 * nt], [WIN, 8], [1, WIN]]), ACT.Copy).then_inc(s_hi1, 1)

                def queries(hf):
                    use = f"Q{hf}"
                    act.wait_ge(*a_full(i, use))
                    for h in range(4):
                        last = act_(qm[:, h * SN + hf * QH:h * SN + (hf + 1) * QH], bank_a(i, use)[:, 0:QH], ACT.Copy,
                                    scale=keep.qmask[:, h:h + 1])
                    last.then_inc(a_freed(i, use)[0], 1)

                def values(j, p):
                    use = f"V{j}"
                    act.wait_ge(*a_full(i, use))
                    act_(view(vb, 0, GK, j * VG + p * 2 * HEADS * VW, [[VW, 2 * HEADS], [1, HD]]),
                         view(bank_a(i, use), 0, GK, 0, [[HD, 2 * HEADS], [1, HD]]), ACT.Copy,
                         scale=keep.kmask[:, p:p + 1]).then_inc(a_freed(i, use)[0], 1)

                def exps(j):
                    act.wait_ge(s_ssub, i * NG + j + 1)
                    act_(pr[:], sm[:], ACT.Exp).then_inc(s_exp, 1)

                def weights_out(j):
                    act.wait_ge(s_ptf, i * NG + j + 1)
                    act_(pt[:, 0:4 * QP], pt_ps[0:GK, 0:4 * QP], ACT.Copy)
                    act_(pt[:, 4 * QP:5 * QP], o_ps[0:GK, PT4:PT4 + QP], ACT.Copy).then_inc(s_pte, 1)

                def outputs_hi(j):
                    use = f"OT{j}"
                    act.wait_ge(*a_full(i, use))
                    for dst, rows, c0 in ((ot[0], 128, 0), (ot[2], CR, 2 * QP)):
                        for p in range(2):
                            last = act_(view(dst, 0, rows, p * WIN * W + j * 2 * WIN, [[WIN, 2], [W, WIN], [1, WIN]]),
                                        view(bank_a(i, use), 0, rows, c0 + p * QP, [[WP, 2], [WIN, WIN], [1, WIN]]), ACT.Copy)
                    last.then_inc(s_oth, 1)

                def t_hi(name, l):
                    for hf, (t0, nt) in enumerate(HALF):
                        for part, dst, rows in (("A", z2t[0], 128), ("C", z2t[2], CR)):
                            use = f"{name}{part}{hf}"
                            act.wait_ge(*m_full(m, l, use))
                            act_(dst[0:rows, t0 * TT:(t0 + nt) * TT], rm[RM[l].slot(use)][0:rows, 0:nt * TT],
                                 ACT.Copy).then_inc(s_hi2, 1)

                if lm is not None:
                    t_hi("T2", lm)
                    for g in range(2 * FT):
                        hf, f = divmod(g, FT)
                        t0, nt = HALF[hf]
                        use = f"G{g}"
                        act.wait_ge(*m_full(m, lm, use))
                        act_(ht[:, f * SN + t0 * TT:f * SN + (t0 + nt) * TT], rm[RM[lm].slot(use)][:, 0:nt * TT],
                             ACT.Gelu_apprx_tanh).then_inc(rm_free[RM[lm].slot(use)], 1)
                if la is not None:
                    exps(0)
                    weights_out(0)
                    exps(1)
                    outputs_hi(0)
                    weights_out(1)
                    exps(2)
                    outputs_hi(1)
                if ln is not None:
                    front_hi(0)
                if la is not None:
                    weights_out(2)
                    exps(3)
                if ln is not None:
                    front_hi(1)
                if la is not None:
                    outputs_hi(2)
                    weights_out(3)
                if ln is not None:
                    queries(0)
                if la is not None:
                    outputs_hi(3)
                if lm == 1:
                    t_hi("T3", 1)
                if ln is not None:
                    queries(1)
                if lm == 1:
                    for n in range(4):
                        use = f"L{n}"
                        t0, nt = PAIRS[n]
                        act.wait_ge(*m_full(m, 1, use))
                        if n == 0:
                            reach(act, s_yz, 32 * (m - NS))
                        act_(yz[:, t0 * DIM:(t0 + nt) * DIM], rm[RM[1].slot(use)][0:TT, 0:nt * DIM],
                             ACT.Copy).then_inc(rm_free[RM[1].slot(use)], 1)
                if ln is not None:
                    for j in range(NG):
                        values(j, 0)

            bodies(act, body)

        @block.vector
        def _(dve):
            v = nc.vector

            def stats(n, x_, i, tiles=range(ST), last=True):
                for t in tiles:
                    ins = v.bn_stats(st[n][:, t * 6:(t + 1) * 6], x_[:, t * DIM:(t + 1) * DIM])
                if last:
                    ins.then_inc(s_st[n], 1)

            def normalise(n, z, x_, i):
                dve.wait_ge(s_rs[n], RS_STEPS * (i + 1))
                for t in range(ST):
                    ins = v.tensor_scalar(z[:, t * ZW:t * ZW + DIM], x_[:, t * DIM:(t + 1) * DIM],
                                          mean[n][:, t:t + 1], rs[n][:, t:t + 1], ALU.subtract, ALU.mult)
                ins.then_inc(s_norm[n], 1)

            v.memset(q4[:], 0.0)
            v.memset(k4[:], 0.0)
            for t in (z1t[2], z2t[2], ot[2]):
                v.memset(t[CR:CK, :].bitcast(F32), 1.0)
            for j in range(NG):
                for p in range(2):
                    v.tensor_copy(view(vb, 0, GK, j * VG + p * 2 * HEADS * VW + HD, [[VW, 2 * HEADS]]),
                                  view(keep.kmask, 0, GK, p, [[0, 2 * HEADS]]))
            v.memset(s_ps[:], 0.0)
            v.memset(o_ps[:], 1.0).then_inc(s_init, 1)

            def body(i, la, lm, ln):
                m = i - 1

                def front_lo(hf):
                    t0, nt = HALF[hf]
                    for n, (part, dst, src, p0, rows) in enumerate((("A", z1t[1], z1t[0], 0, 128),
                                                                   ("C", z1t[2], z1t[2], REST, REST))):
                        use = f"T1{part}{hf}"
                        dve.wait_ge(s_hi1, (i + 1) * 4 + 2 * hf + n + 1)
                        dims = [[WIN, 2 * nt], [GK, 8], [1, WIN]]
                        v.tensor_tensor(view(dst, p0, rows, t0 * 2 * WIN, dims),
                                        view(bank_a(i, use), p0, rows, 0, [[W, 2 * nt], [WIN, 8], [1, WIN]]),
                                        view(src, p0, rows, t0 * 2 * WIN, dims).bitcast(F32),
                                        ALU.subtract).then_inc(a_freed(i, use)[0], 1)

                def keys(hf):
                    use = f"K{hf}"
                    dve.wait_ge(*a_full(i, use))
                    cols = slice(hf * QH, (hf + 1) * QH)
                    v.tensor_copy(kt[:, cols], bank_a(i, use)[:, 0:QH]).then_inc(a_freed(i, use)[0], 1)
                    use = f"B{hf}"
                    dve.wait_ge(*a_full(i, use))
                    v.tensor_scalar(q4[0:HD, cols], bank_a(i, use)[0:HD, 0:QH], float(HD) ** -0.5, None, ALU.mult)
                    v.tensor_copy(k4[0:HD, cols], bank_a(i, use)[HD:2 * HD, 0:QH]).then_inc(a_freed(i, use)[0], 1)

                def values(j, p):
                    use = f"V{j}"
                    dve.wait_ge(*a_full(i, use))
                    dve.wait_ge(*a_freed(i, use, 1))
                    v.tensor_scalar(view(vb, 0, GK, j * VG + p * 2 * HEADS * VW, [[VW, 2 * HEADS], [1, HD]]),
                                    view(bank_a(i, use), 0, GK, 0, [[HD, 2 * HEADS], [1, HD]]),
                                    keep.kmask[:, p:p + 1], None, ALU.mult).then_inc(a_freed(i, use)[0], 1)

                def scores(j, n_, l):
                    n = n_ * NG + j + 1
                    dve.wait_ge(s_sfull, n)
                    if l == 0:
                        tab = keep.tabs[:, 0:HEADS * GK]
                    else:
                        bottom = (n_ % SPI) // (SPI - 1)
                        off = bottom * (2 * HEADS * GK) + (1 + (j == NG - 1)) * HEADS * GK
                        tab = view(keep.tabs, 0, QP, off, [[1, HEADS * GK]])
                    v.tensor_tensor(sc[:], s_ps[0:QP, 0:HEADS * GK], tab, ALU.add).then_inc(s_sadd, 1)
                    dve.wait_ge(s_sadd, n)
                    s3 = sc[:].rearrange("q (g k) -> q g k", k=WT)
                    v.tensor_reduce(mx[:], s3, AX.X, ALU.max).then_inc(s_smax, 1)
                    dve.wait_ge(s_smax, n)
                    reach(dve, s_exp, n_ * NG + j)
                    v.tensor_tensor(sm[:].rearrange("q (g k) -> q g k", k=WT), s3,
                                    view(mx, 0, QP, 0, [[1, 2 * HEADS], [0, WT]]), ALU.subtract).then_inc(s_ssub, 1)

                def outputs(j):
                    n = i * NG + j + 1
                    dve.wait_ge(s_of, n)
                    v.reciprocal(rd[:], view(o_ps, 0, QP, HD, [[VW, 2 * HEADS]])).then_inc(s_rec, 1)
                    dve.wait_ge(s_rec, n)
                    for p in range(2):
                        v.tensor_tensor(view(os_, 0, QP, p * ZW, [[HD, 4], [1, HD]]),
                                        view(o_ps, 0, QP, p * VW, [[2 * VW, 4], [1, HD]]),
                                        view(rd, 0, QP, p, [[2, 4], [0, HD]]), ALU.mult)
                    v.tensor_tensor(view(os_, 0, QP, 128, [[ZW, 2], [HD, 3], [1, HD]]),
                                    view(o_ps, 0, QP, 4 * 2 * VW, [[VW, 2], [0, 3], [1, HD]]),
                                    view(rd, 0, QP, 8, [[1, 2], [0, 3], [0, HD]]), ALU.mult).then_inc(s_od, 1)

                def outputs_lo(j):
                    use = f"OT{j}"
                    dve.wait_ge(s_oth, i * NG + j + 1)
                    for dst, src, p0, rows, c0 in ((ot[1], ot[0], 0, 128, 0), (ot[2], ot[2], REST, REST, 2 * QP)):
                        for p in range(2):
                            o = p * WIN * W + j * 2 * WIN
                            dims = [[WIN, 2], [W, WIN], [1, WIN]]
                            ins = v.tensor_tensor(view(dst, p0, rows, o, dims),
                                                  view(bank_a(i, use), p0, rows, c0 + p * QP, [[WP, 2], [WIN, WIN], [1, WIN]]),
                                                  view(src, p0, rows, o, dims).bitcast(F32), ALU.subtract)
                    ins.then_inc(a_freed(i, use)[0], 1)

                def t_lo(name, l, first):
                    for hf, (t0, nt) in enumerate(HALF):
                        cols = slice(t0 * TT, (t0 + nt) * TT)
                        for n, (part, dst, src, rows) in enumerate((("A", z2t[1], z2t[0], slice(0, 128)),
                                                                   ("C", z2t[2], z2t[2], slice(REST, 2 * REST)))):
                            use = f"{name}{part}{hf}"
                            dve.wait_ge(s_hi2, hi2(m, l, first + 2 * hf + n + 1))
                            v.tensor_tensor(dst[rows, cols], rm[RM[l].slot(use)][rows, 0:nt * TT], src[rows, cols].bitcast(F32),
                                            ALU.subtract).then_inc(rm_free[RM[l].slot(use)], 1)

                def mlp_out(n):
                    use = f"W{n}"
                    t0, nt = PAIRS[n]
                    dve.wait_ge(*m_full(m, lm, use))
                    if n == 0:
                        dve.wait_ge(s_x1b, m + 1)
                        reach(dve, s_xo, 32 * m if lm == 0 else 32 * NS)
                    v.tensor_tensor(view(xo, 0, TT, t0 * ZW, [[ZW, nt], [1, DIM]]),
                                    view(rm[RM[lm].slot(use)], 0, TT, 0, [[DIM, nt], [1, DIM]]),
                                    view(x1b, 0, TT, t0 * DIM, [[DIM, nt], [1, DIM]]),
                                    ALU.add).then_inc(rm_free[RM[lm].slot(use)], 1)

                if lm is not None:
                    t_lo("T2", lm, 0)
                if ln is not None:
                    dve.wait_ge(s_xa, 32 * (i + 2))
                    stats(0, xa, i + 1)
                    normalise(0, z1, xa, i + 1)
                if lm is not None:
                    mlp_out(0)
                if la is not None:
                    scores(1, i, la)
                    outputs(0)
                if lm is not None:
                    mlp_out(1)
                if la is not None:
                    outputs_lo(0)
                    scores(2, i, la)
                    outputs(1)
                if lm is not None:
                    mlp_out(2)
                if la is not None:
                    outputs_lo(1)
                if ln is not None:
                    front_lo(0)
                if la is not None:
                    scores(3, i, la)
                    outputs(2)
                if ln is not None:
                    front_lo(1)
                if lm is not None:
                    mlp_out(3)
                if la is not None:
                    outputs_lo(2)
                    outputs(3)
                if ln is not None:
                    keys(0)
                if la is not None:
                    outputs_lo(3)
                if lm == 1:
                    t_lo("T3", 1, 4)
                if la is not None:
                    dve.wait_ge(s_xr, 32 * (i + 1))
                    reach(dve, s_x1b, i)
                    for n, (t0, nt) in enumerate(PROJ):
                        use = f"P{n}"
                        dve.wait_ge(*a_full(i, use))
                        cols = slice(t0 * DIM, (t0 + nt) * DIM)
                        v.tensor_tensor(x1[:, cols], bank_a(i, use)[0:TT, 0:nt * DIM], xr[:, cols],
                                        ALU.add).then_inc(a_freed(i, use)[0], 1)
                    for n, (t0, nt) in enumerate(PROJ):
                        dve.wait_ge(*a_freed(i, f"P{n}"))
                        stats(1, x1, i, range(t0, t0 + nt), last=(n == 2))
                if ln is not None:
                    keys(1)
                    values(0, 1)
                if la is not None:
                    normalise(1, z2, x1, i)
                if ln is not None:
                    for j in range(1, NG):
                        values(j, 1)
                    scores(0, i + 1, ln)

            bodies(dve, body)

        @block.tensor
        def _(pe):
            mm, tr = nc.tensor.matmul, nc.tensor.transpose
            pe.wait_ge(s_init, 2)

            def turn(z, hf, bank_of, room, full, name):
                t0, nt = HALF[hf]
                for part, f0, rows in (("A", 0, 128), ("C", 128, CR)):
                    use = f"{name}{part}{hf}"
                    reach(pe, *room(use))
                    for t in range(nt):
                        c = (t0 + t) * ZW + f0
                        last = tr(bank_of(use)[0:rows, t * TT:(t + 1) * TT], z[:, c:c + rows], keep.ident[0:TT, 0:TT])
                    last.then_inc(full(use), 1)

            def body(i, la, lm, ln):
                m = i - 1

                def room_a(use):
                    reach(pe, *a_room(i, use))

                def filled_a(use, last):
                    last.then_inc(a_full(i, use)[0], 1)

                def bank_m(use):
                    return rm[RM[lm].slot(use)]

                def room_m(use):
                    reach(pe, *m_room(m, lm, use))

                def front_turned(hf):
                    if hf == 0:
                        pe.wait_ge(s_z[0], i + 2)
                    turn(z1, hf, lambda u: bank_a(i, u), lambda u: a_room(i, u), lambda u: a_full(i, u)[0], "T1")

                def front_product(name, hf):
                    c0, n = {"Q": (0, 128), "K": (128, 128), "B": (256, 2 * HD)}[name]
                    use = f"{name}{hf}"
                    if use == "Q0":
                        pe.wait_ge(*a_freed(i, "T1C1"))
                    room_a(use)
                    filled_a(use, split_passes(nc, bank_a(i, use)[0:n, 0:QH], *[t[:, hf * QH:(hf + 1) * QH] for t in z1t],
                                               *[w[:, c0:c0 + n] for w in keep.w["qkv", ln]], True))

                def values(j):
                    use = f"V{j}"
                    room_a(use)
                    wv = [w[:, 2 * DIM:3 * DIM] for w in keep.w["qkv", ln]]
                    for w in range(2):
                        c = slice((2 * j + w) * GK, (2 * j + w + 1) * GK)
                        last = split_passes(nc, bank_a(i, use)[0:GK, w * DIM:(w + 1) * DIM], *[t[:, c] for t in z1t], *wv, False)
                    filled_a(use, last)

                def scores(j, n):
                    if j % 2 == 0:
                        for name in "QB":
                            pe.wait_ge(*a_freed(n - 1, f"{name}{j // 2}"))
                    reach(pe, s_sadd, n * NG + j)
                    for h in range(HEADS):
                        for p in range(2):
                            for w in range(2):
                                c = (2 * j + w) * GK + p * WT
                                q = qm[:, h * SN + c:h * SN + c + WT] if h < 4 else q4[:, c:c + WT]
                                k = (kt if h < 4 else k4)[:, c:c + WT]
                                last = mm(s_ps[w * WP:w * WP + WT, (2 * h + p) * WT:(2 * h + p + 1) * WT], q, k,
                                          start=True, stop=True)
                    last.then_inc(s_sfull, 1)

                def weights_turned(j):
                    n = i * NG + j
                    pe.wait_ge(s_exp, n + 1)
                    reach(pe, s_pte, n)
                    reach(pe, s_od, n)
                    for h in range(HEADS):
                        o = pt_ps[0:GK, h * QP:(h + 1) * QP] if h < 4 else o_ps[0:GK, PT4:PT4 + QP]
                        last = tr(o, pr[:, h * GK:(h + 1) * GK], keep.ident[0:QP, 0:QP])
                    last.then_inc(s_ptf, 1)

                def outputs(j):
                    pe.wait_ge(s_pte, i * NG + j + 1)
                    pe.wait_ge(*a_freed(i - 1, f"V{j}"))
                    for h in range(HEADS):
                        for w in range(2):
                            last = mm(o_ps[w * WP:w * WP + WT, h * 2 * VW:(h + 1) * 2 * VW],
                                      pt[:, h * QP + w * WP:h * QP + w * WP + WT],
                                      view(vb, 0, GK, j * VG + (w * HEADS + h) * VW, [[2 * HEADS * VW, 2], [1, VW]]),
                                      start=True, stop=True)
                    last.then_inc(s_of, 1)

                def outputs_turned(j):
                    use = f"OT{j}"
                    pe.wait_ge(s_od, i * NG + j + 1)
                    room_a(use)
                    for f0, rows, c0 in ((0, 128, 0), (128, CR, 2 * QP)):
                        for p in range(2):
                            last = tr(bank_a(i, use)[0:rows, c0 + p * QP:c0 + (p + 1) * QP],
                                      os_[:, p * ZW + f0:p * ZW + f0 + rows], keep.ident[0:QP, 0:QP])
                    filled_a(use, last)

                def mlp_in(gs):
                    for g in gs:
                        use = f"G{g}"
                        hf, f = divmod(g, FT)
                        t0, nt = HALF[hf]
                        room_m(use)
                        last = split_passes(nc, bank_m(use)[:, 0:nt * TT], *[t[:, t0 * TT:(t0 + nt) * TT] for t in z2t],
                                            *[w[:, f * 128:(f + 1) * 128] for w in keep.w["w1", lm]], True)
                        last.then_inc(rm_full[RM[lm].slot(use)], 1)

                def mlp_out(n):
                    use = f"W{n}"
                    t0, nt = PAIRS[n]
                    room_m(use)
                    for t in range(nt):
                        for f in range(FT):
                            c = f * SN + (t0 + t) * TT
                            last = mm(bank_m(use)[0:TT, t * DIM:(t + 1) * DIM], ht[:, c:c + TT],
                                      keep.w["w2", lm][:, f * DIM:(f + 1) * DIM], start=(f == 0), stop=(f == FT - 1))
                    last.then_inc(rm_full[RM[lm].slot(use)], 1)

                def mlp_turned(z, name):
                    for hf in range(2):
                        turn(z, hf, bank_m, lambda u: m_room(m, lm, u), lambda u: m_full(m, lm, u)[0], name)

                if lm is not None:
                    pe.wait_ge(s_z[1], m + 1)
                    mlp_turned(z2, "T2")
                    pe.wait_ge(*m_freed(m, lm, "T2C1"))
                    mlp_in(range(2 * FT))
                    mlp_out(0)
                if la is not None:
                    weights_turned(0)
                    scores(1, i)
                    outputs(0)
                if lm is not None:
                    mlp_out(1)
                if la is not None:
                    outputs_turned(0)
                    weights_turned(1)
                    scores(2, i)
                    outputs(1)
                if lm is not None:
                    mlp_out(2)
                if la is not None:
                    outputs_turned(1)
                if ln is not None:
                    front_turned(0)
                if la is not None:
                    weights_turned(2)
                    scores(3, i)
                    outputs(2)
                if ln is not None:
                    front_turned(1)
                if lm is not None:
                    mlp_out(3)
                if la is not None:
                    outputs_turned(2)
                    weights_turned(3)
                if ln is not None:
                    front_product("Q", 0)
                if la is not None:
                    outputs(3)
                if ln is not None:
                    front_product("K", 0)
                    front_product("B", 0)
                if la is not None:
                    outputs_turned(3)
                if lm == 1:
                    pe.wait_ge(s_xod, m - NS + 1)
                    mlp_turned(xo, "T3")
                if ln is not None:
                    front_product("Q", 1)
                if la is not None:
                    pe.wait_ge(*a_freed(i, "OT3"))
                    for n, (t0, nt) in enumerate(PROJ):
                        use = f"P{n}"
                        room_a(use)
                        for t in range(nt):
                            c = slice((t0 + t) * TT, (t0 + t + 1) * TT)
                            last = split_passes(nc, bank_a(i, use)[0:TT, t * DIM:(t + 1) * DIM], *[o[:, c] for o in ot],
                                                *[w[:] for w in keep.w["proj", la]], False)
                        filled_a(use, last)
                if lm == 1:
                    pe.wait_ge(*m_freed(m, 1, "T3C1"))
                    for n, (t0, nt) in enumerate(PAIRS):
                        use = f"L{n}"
                        room_m(use)
                        for t in range(nt):
                            c = slice((t0 + t) * TT, (t0 + t + 1) * TT)
                            last = split_passes(nc, bank_m(use)[0:TT, t * DIM:(t + 1) * DIM], *[z[:, c] for z in z2t],
                                                *[w[:] for w in keep.w["lin", 1]], False)
                        last.then_inc(rm_full[RM[1].slot(use)], 1)
                if ln is not None:
                    front_product("K", 1)
                    front_product("B", 1)
                    values(0)
                    scores(0, i + 1)
                    for j in range(1, NG):
                        values(j)

            bodies(pe, body)


def phase_c(nc, keep, f_syn, ys, out):
    with ExitStack() as ctx:
        def sb(name, shape, dt=F32):
            return ctx.enter_context(nc.sbuf_tensor(name, shape, dt))

        def sem(name):
            return ctx.enter_context(nc.semaphore(name))

        KG = 3
        G = K // KG
        acc = [ctx.enter_context(nc.psum_tensor(f"c_acc{n}", [128, 512], F32)) for n in range(2)]
        fin = [ctx.enter_context(nc.psum_tensor(f"c_fin{n}", [128, 512], F32)) for n in range(2)]
        taps = [sb(f"c_taps{n}", [TT, NJ * TT]) for n in range(2)]
        band_hi = sb("c_band_hi", [TT, K * NJ * TT], F32R)
        band_lo = sb("c_band_lo", [TT, K * NJ * TT], F32R)
        y = [sb(f"c_y{u}", [TT, NT * DIM]) for u in range(2)]
        y_hi = sb("c_y_hi", [TT, PADT * K * C], F32R)
        y_lo = sb("c_y_lo", [TT, PADT * K * C], F32R)
        conv = [sb(f"c_conv{u}", [TT, C * NT]) for u in range(2)]
        direct = [sb(f"c_direct{u}", [TT, C * NT]) for u in range(2)]
        one = sb("c_one", [TT, 1])
        res = [sb(f"c_res{u}", [TT, 4 * TT]) for u in range(2)]

        s_taps = [sem(f"c_taps_in{n}") for n in range(2)]
        s_bhi, s_blo, s_zero, s_one = sem("c_band_hi_done"), sem("c_band_lo_done"), sem("c_zero"), sem("c_one_set")
        s_y = [sem(f"c_y_in{u}") for u in range(2)]
        s_hi, s_lo = sem("c_y_hi_done"), sem("c_y_lo_done")
        s_g = sem("c_filters")
        s_conv, s_dir, s_fin, s_res = sem("c_conv_out"), sem("c_direct_out"), sem("c_final"), sem("c_res_done")
        s_store = [sem(f"c_store{u}") for u in range(2)]
        KC = K * C
        block = ctx.enter_context(nc.Block())

        @block.sync
        def _(sp):
            def load_image(img, u):
                for yy in range(2):
                    first = 2 - yy
                    for t0, nt in ((0, first), (first, NT - first)):
                        y0 = (2 * t0 + yy - SHIFT) % H
                        for x0, nx in ((0, SHIFT), (SHIFT, W - SHIFT)):
                            off = y0 * W * DIM + ((x0 - SHIFT) % W) * DIM
                            sp.dma_start(view(y[u], yy * W + x0, nx, t0 * DIM, [[DIM, nt], [1, DIM]]),
                                         dram(ys, img * (H * W * DIM) + off, [[DIM, nx], [TT * DIM, nt], [1, DIM]])
                                         ).then_inc(s_y[u], 16)

            def load_taps(k):
                for r in range(2):
                    for yy in range(2):
                        if k >= 2 and (r, yy) == (0, 0):
                            sp.wait_ge(s_blo, k - 1)
                        sp.dma_start(view(taps[k % 2], r * W, W, yy * W, [[TT, NJ], [1, W]]),
                                     dram(f_syn.tensor, (k * 11 + r - yy + 1) * FROW, [[1, W], [2 * FROW, NJ], [1, W]])
                                     ).then_inc(s_taps[k % 2], 16)

            load_image(0, 0)
            load_taps(0)
            load_taps(1)
            load_image(1, 1)
            for k in range(2, K):
                load_taps(k)

            def store_image(img, u):
                sp.wait_ge(s_res, img + 1)
                sp.dma_start(dram(out.tensor, img * (C * H * W), [[TT, TT], [TT * TT, 4], [1, TT]]),
                             view(res[u], 0, TT, 0, [[TT, 4], [1, TT]])).then_inc(s_store[u], 16)

            with sp.Fori(0, B // 2 - 1) as pair:
                for u in range(2):
                    img = pair * 2 + u
                    sp.wait_ge(s_lo, (img + 1) * G)
                    sp.wait_ge(s_dir, img + 1)
                    load_image(img + 2, u)
                    store_image(img, u)
            for u in range(2):
                store_image(B - 2 + u, u)
            for u in range(2):
                sp.wait_ge(s_store[u], 16 * (B // 2))

        @block.gpsimd
        def _(pool):
            nc.gpsimd.memset(one[:], 1.0).then_inc(s_one, 1)
            pool.wait_ge(s_one, 1)
            with pool.Fori(0, B // 2) as pair:
                for u in range(2):
                    img = pair * 2 + u
                    pool.wait_ge(s_y[u], (pair + 1) * 128)
                    pool.wait_ge(s_fin, img - u)
                    src = view(y[u], 0, TT, KC, [[1, C], [DIM, NT]])
                    nc.gpsimd.tensor_tensor(direct[u][:].rearrange("p (c t) -> p c t", t=NT), src,
                                            view(one, 0, TT, 0, [[0, C], [0, NT]]), ALU.mult).then_inc(s_dir, 1)

        @block.scalar
        def _(act):
            for k in range(K):
                act.wait_ge(s_taps[k % 2], 64 * (k // 2 + 1))
                nc.scalar.activation(band_hi[:, k * NJ * TT:(k + 1) * NJ * TT], taps[k % 2][:], ACT.Copy).then_inc(s_bhi, 1)
            act.wait_ge(s_zero, 1)
            with act.Fori(0, B // 2) as pair:
                for u in range(2):
                    img = pair * 2 + u
                    act.wait_ge(s_y[u], (pair + 1) * 128)
                    for g in range(G):
                        if u == 0:
                            act.wait_ge(s_g, pair * (2 * G))
                        else:
                            act.wait_ge(s_g, pair * (2 * G) + g + 1)
                        nc.scalar.activation(view(y_hi, 0, TT, 2 * KC + g * KG * C, [[KC, NT], [1, KG * C]]),
                                             view(y[u], 0, TT, g * KG * C, [[DIM, NT], [1, KG * C]]), ACT.Copy).then_inc(s_hi, 1)
                    act.wait_ge(s_g, (img + 1) * G)
                    nc.scalar.activation(conv[u][:].rearrange("p (c t) -> p c t", t=NT),
                                         view(acc[u], 0, TT, 0, [[1, C], [C, NT]]), ACT.Copy).then_inc(s_conv, 1)

        @block.vector
        def _(dve):
            nc.vector.memset(y_hi[:].bitcast(F32), 0.0)
            nc.vector.memset(y_lo[:].bitcast(F32), 0.0).then_inc(s_zero, 1)
            for k in range(K):
                dve.wait_ge(s_bhi, k + 1)
                cols = slice(k * NJ * TT, (k + 1) * NJ * TT)
                nc.vector.tensor_tensor(band_lo[:, cols], taps[k % 2][:], band_hi[:, cols].bitcast(F32),
                                        ALU.subtract).then_inc(s_blo, 1)
            with dve.Fori(0, B // 2) as pair:
                for u in range(2):
                    img = pair * 2 + u
                    for g in range(G):
                        dve.wait_ge(s_hi, img * G + g + 1)
                        o = 2 * KC + g * KG * C
                        dims = [[KC, NT], [1, KG * C]]
                        nc.vector.tensor_tensor(view(y_lo, 0, TT, o, dims),
                                                view(y[u], 0, TT, g * KG * C, [[DIM, NT], [1, KG * C]]),
                                                view(y_hi, 0, TT, o, dims).bitcast(F32), ALU.subtract).then_inc(s_lo, 1)
                    dve.wait_ge(s_fin, img + 1)
                    dve.wait_ge(s_store[u], pair * 16)
                    nc.vector.tensor_copy(res[u][:], fin[u][0:TT, 0:4 * TT]).then_inc(s_res, 1)

        @block.tensor
        def _(pe):
            mm = nc.tensor.matmul
            pe.wait_ge(s_blo, K)
            with pe.Fori(0, B // 2) as pair:
                for u in range(2):
                    img = pair * 2 + u
                    pe.wait_ge(s_conv, img - u)
                    n = 0
                    for g in range(G):
                        pe.wait_ge(s_lo, img * G + g + 1)
                        for k in range(g * KG, (g + 1) * KG):
                            for j in range(NJ):
                                cols = slice((k * NJ + j) * TT, (k * NJ + j + 1) * TT)
                                o, dims = j * KC + k * C, [[KC, NT], [1, C]]
                                for a, b in ((band_hi, y_hi), (band_hi, y_lo), (band_lo, y_hi)):
                                    last = mm(acc[u][0:TT, 0:NT * C], a[:, cols], view(b, 0, TT, o, dims),
                                              start=(n == 0), stop=(n == K * NJ * 3 - 1))
                                    n += 1
                        last.then_inc(s_g, 1)
                    pe.wait_ge(s_conv, img + 1)
                    pe.wait_ge(s_dir, img + 1)
                    pe.wait_ge(s_res, img - u)
                    for q in range(4):
                        cols = slice(q * TT, (q + 1) * TT)
                        mm(fin[u][0:TT, cols], conv[u][:, cols], keep.flip[0:TT, :], start=True, stop=False)
                        last = mm(fin[u][0:TT, cols], direct[u][:, cols], keep.ident[0:TT, 0:TT], start=False, stop=True)
                    last.then_inc(s_fin, 1)


_ORDER = ["x", "xf", "f_ana", "f_syn", "ln1g", "ln1b", "qkvw", "qkvb", "projw", "projb", "rel", "ln2g", "ln2b",
          "w1", "b1", "w2", "b2", "linwT", "linb", "convwT", "convb", "wmask"]


def kernel(**inputs):
    import numpy as np
    import concourse.bacc as bacc
    from concourse.bass_utils import run_bass_kernel_spmd

    src = {k.replace("L0_conv_", ""): np.asarray(v) for k, v in inputs.items()}

    def padded_rows(f):
        rows = np.zeros((K, FS + 2, FROW), f.dtype)
        rows[:, 1:FS + 1, PADF:PADF + FS] = f
        return rows

    arrays = dict(src)
    arrays["xf"] = src["x"][..., ::-1]
    arrays["f_ana"] = padded_rows(src["f_ana"].reshape(K, FS, FS)[..., ::-1])
    arrays["f_syn"] = padded_rows(src["f_syn"].reshape(K, FS, FS))
    side = 2 * WIN - 1
    arrays["rel"] = src["rpb"].transpose(0, 2, 1).reshape(2 * HEADS, side, side)[:, ::-1, ::-1]
    arrays["linwT"] = src["linw"].T
    arrays["convwT"] = src["convw"].reshape(C, DIM).T
    late = np.arange(WIN) >= WIN - SHIFT
    apart_y = np.repeat(late, WIN)[:, None] != np.repeat(late, WIN)[None, :]
    apart_x = np.tile(late, WIN)[:, None] != np.tile(late, WIN)[None, :]
    wmask = np.zeros((QP, 4, 2, WT), np.float32)
    for bottom in range(2):
        for right in range(2):
            for w in range(2):
                for p in range(2):
                    apart = (apart_y & (bottom and p == 1)) | (apart_x & (right and w == 1))
                    wmask[w * WP:w * WP + WT, bottom * 2 + right, p] = np.where(apart, np.float32(-100), np.float32(0))
    arrays["wmask"] = wmask.reshape(QP, 4 * GK)

    nc = bacc.Bacc("TRN2", target_bir_lowering=False, num_devices=1)
    given, args = {}, []
    for name in _ORDER:
        a = np.ascontiguousarray(arrays[name])
        given[f"in_{name}"] = a
        args.append(nc.dram_tensor(f"in_{name}", a.shape, mybir.dt.from_np(a.dtype), kind="ExternalInput").ap())
    res = nc.dram_tensor("out_0", (B, C, H, W), F32, kind="ExternalOutput").ap()
    build(nc, *args, res)
    r = run_bass_kernel_spmd(nc, [given], core_ids=[0])
    return r.results[0]["out_0"]
```

```python
from contextlib import ExitStack

import concourse.bass as bass
from concourse import mybir

F32 = mybir.dt.float32
F32R = mybir.dt.float32r
ALU = mybir.AluOpType
ACT = mybir.ActivationFunctionType
AX = mybir.AxisListType

B, C, H, W = 8, 16, 56, 56
K, FS, WIN = 9, 9, 7
DIM = K * C + C
HEADS, HD = 5, 32
MLP = 4 * DIM
SHIFT = WIN // 2
EPS = 1e-5
LO, REST = 128, DIM - 128
CR = 3 * REST
CK = CR + 2
TT = 2 * W
NT = H // 2
PADT = NT + 4
NJ = 5
SR = 2 * WIN
ST = SR // 2
SN = SR * W
SPI = H // SR
NS = B * SPI
HALF = [(0, 4), (4, 3)]
WT = WIN * WIN
WP = 64
QP = WP + WT
GK = 2 * WT
NG = W // (2 * WIN)
VW = HD + 1
FT = MLP // 128
PADF = W - FS // 2 - 1
FROW = 112
ZW = 128 + CR
HP = H + SHIFT


def view(t, p0, n, off, dims):
    row = t.shape[-1]
    return bass.AP(tensor=t, offset=p0 * row + off, ap=[[row, n]] + [list(d) for d in dims])


def dram(t, off, dims):
    return bass.AP(tensor=t, offset=off, ap=[list(d) for d in dims])


def reach(engine, sem, value):
    if isinstance(value, int) and value <= 0:
        return
    engine.wait_ge(sem, value)


class Ring:

    def __init__(self, uses, banks, readers):
        self.uses, self.banks = uses, banks
        self.at = {u: n for n, u in enumerate(uses)}
        self.weight = [readers.get(u, 1) for u in uses]

    def slot(self, use):
        return self.at[use] % self.banks

    def filled(self, use):
        return self.at[use] // self.banks + 1

    def freed_before(self, use):
        n = self.at[use]
        return sum(self.weight[m] for m in range(n % self.banks, n, self.banks))

    def fills(self, slot):
        return len(range(slot, len(self.uses), self.banks))

    def frees(self, slot):
        return sum(self.weight[slot::self.banks])


def split_passes(nc, out, hi, lo, rest, w_hi, w_lo, w_rest, act_moves):
    pairs = [(hi, w_hi), (lo, w_hi), (hi, w_lo), (rest, w_rest)]
    for n, (a, w) in enumerate(pairs):
        lhs, rhs = (w, a) if act_moves else (a, w)
        last = nc.tensor.matmul(out, lhs, rhs, start=(n == 0), stop=(n == len(pairs) - 1))
    return last


def build(nc, x, xf, f_ana, f_syn, ln1g, ln1b, qkvw, qkvb, projw, projb, rel, ln2g, ln2b, w1, b1, w2, b2,
          linwT, linb, convwT, convb, wmask, out):
    xs0 = nc.dram_tensor("xs0", [B, H, W, DIM], F32, kind="Internal")
    xs1 = nc.dram_tensor("xs1", [B, HP, HP, DIM], F32, kind="Internal")
    ys = nc.dram_tensor("ys", [B, H, W, DIM], F32, kind="Internal")
    relT = nc.dram_tensor("relT", [WT, 2 * HEADS * WT], F32, kind="Internal")
    with ExitStack() as ctx:
        keep = Persistent(nc, ctx)
        phase_a(nc, keep, x, xf, f_ana, ln1g, ln1b, qkvw, qkvb, projw, projb, rel, relT, ln2g, ln2b, w1, b1,
                w2, b2, linwT, linb, convwT, convb, wmask, xs0)
        phase_b(nc, keep, xs0, xs1, ys)
        phase_c(nc, keep, f_syn, ys, out)


class Persistent:

    def __init__(self, nc, ctx):
        def sb(name, shape, dt=F32):
            return ctx.enter_context(nc.sbuf_tensor(name, shape, dt))
        self.ident = sb("ident", [128, 128])
        self.flip = sb("flip", [128, TT])
        self.qmask = sb("qmask", [128, 4])
        self.kmask = sb("kmask", [GK, 2])
        self.tabs = sb("tabs", [QP, 5 * HEADS * GK])
        self.w = {}
        for l in range(2):
            for name, n in (("qkv", 3 * DIM), ("proj", DIM), ("w1", MLP)):
                self.w[name, l] = self.split(sb, f"{name}{l}", n)
            self.w["w2", l] = sb(f"w2_{l}", [128, FT * DIM])
            self.w["b2", l] = sb(f"b2_{l}", [TT, DIM])
        self.w["lin", 1] = self.split(sb, "lin", DIM)

    @staticmethod
    def split(sb, name, n):
        return (sb(name + "_hi", [128, n], F32R), sb(name + "_lo", [128, n], F32R), sb(name + "_rest", [CK, n], F32R))


def phase_a(nc, keep, x, xf, f_ana, ln1g, ln1b, qkvw, qkvb, projw, projb, rel, relT, ln2g, ln2b, w1, b1, w2, b2,
            linwT, linb, convwT, convb, wmask, xs0):
    with ExitStack() as ctx:
        def sb(name, shape, dt=F32):
            return ctx.enter_context(nc.sbuf_tensor(name, shape, dt))

        def sem(name):
            return ctx.enter_context(nc.semaphore(name))

        NB = 5
        psum = [ctx.enter_context(nc.psum_tensor(f"a_ps{n}", [128, 512], F32)) for n in range(8)]
        nat_ps, mir_ps, conv_ps = psum[0], psum[1], psum[3:]
        taps = [sb(f"a_taps{n}", [TT, NJ * TT]) for n in range(2)]
        band_hi = sb("a_band_hi", [TT, K * NJ * TT], F32R)
        band_lo = sb("a_band_lo", [TT, K * NJ * TT], F32R)
        xin = [sb(f"a_xin{u}", [TT, 4 * TT]) for u in range(2)]
        xfin = [sb(f"a_xfin{u}", [TT, 4 * TT]) for u in range(2)]
        img_hi = sb("a_img_hi", [TT, PADT * C], F32R)
        img_lo = sb("a_img_lo", [TT, PADT * C], F32R)
        tok = [sb(f"a_tok{u}", [TT, NT * DIM]) for u in range(2)]
        mats = []
        for l in range(2):
            mats += [("qkv", l, 3 * DIM, qkvw, qkvb, 0), ("proj", l, DIM, projw, projb, None),
                     ("w1", l, MLP, w1, b1, 1)]
        raw_a = {m[:2]: sb(f"raw_a_{m[0]}{m[1]}", [128, m[2]]) for m in mats}
        raw_c = {m[:2]: sb(f"raw_c_{m[0]}{m[1]}", [CR, m[2]]) for m in mats}
        gain_a, gain_c = sb("gain_a", [128, 4]), sb("gain_c", [CR, 4])
        lnb_a, lnb_c = sb("lnb_a", [128, 4]), sb("lnb_c", [CR, 4])
        scaled, scaled_c = sb("scaled", [128, MLP]), sb("scaled_c", [CR, MLP])
        starts, width = {}, 0
        for m in mats:
            starts[m[:2]], width = width, width + m[2]
        starts["lin", 1], width = width, width + DIM
        brow = sb("brow", [CK, width])
        bhi, blo = sb("bhi", [CK, width], F32R), sb("blo", [CK, width])
        sign = sb("sign", [128, 1])
        lwt_a, lwt_b = sb("lwt_a", [128, ZW]), sb("lwt_b", [C, ZW])
        mix_a, mix_b = sb("mix_a", [128, DIM]), sb("mix_b", [C, DIM])
        linb_a, linb_b = sb("linb_a", [128, 1]), sb("linb_b", [C, 1])
        relb, msk = sb("relb", [QP, 2 * HEADS * WT]), sb("msk", [QP, 4 * GK])

        s_taps = [sem(f"a_taps_in{n}") for n in range(2)]
        s_bhi, s_blo = sem("a_band_hi_done"), sem("a_band_lo_done")
        s_xin = [sem(f"a_x_in{u}") for u in range(2)]
        s_nat_T, s_mir_T, s_nat, s_ihi, s_ilo = sem("a_nat_T"), sem("a_mir_T"), sem("a_nat"), sem("a_img_hi"), sem("a_img_lo")
        s_conv = [sem(f"a_conv{n}") for n in range(NB)]
        s_free = [sem(f"a_conv_free{n}") for n in range(NB)]
        s_store = [sem(f"a_store{u}") for u in range(2)]
        s_pool, s_zero, s_mixz = sem("a_pool"), sem("a_zero"), sem("a_mixz")
        s_raw, s_small, s_mix = sem("a_raw"), sem("a_small"), sem("a_mix")
        s_relT, s_relb = sem("a_relT"), sem("a_relb")
        s_bps, s_prep = sem("a_bias_ps"), sem("a_prep")
        s_brow, s_bhirow = sem("a_bias_rows"), sem("a_bias_hi")

        def bank_of(u, k):
            return (u * K + k) % NB

        def nth(u, k):
            return (u * K + k) // NB

        per = [len(range(b, 2 * K, NB)) for b in range(NB)]
        def pieces(m, cols):
            if m != "qkv":
                return [(0, 0, cols)]
            return [(0, 0, 128), (128, DIM, 128), (2 * 128, 128, HD), (2 * 128 + HD, DIM + 128, HD), (2 * DIM, 2 * DIM, DIM)]

        n_pieces = sum(len(pieces(m[0], m[2])) for m in mats)
        RAWS = 16 * (2 * n_pieces)
        SMALL = 16 * (2 * 4 * 2 + 2 * 2 + 2 + 4 + n_pieces + 1)
        MIX = 16 * (K + 2)
        block = ctx.enter_context(nc.Block())

        @block.sync
        def _(sp):
            def load_taps(k):
                for r in range(2):
                    for yy in range(2):
                        if k >= 2 and (r, yy) == (0, 0):
                            sp.wait_ge(s_blo, k - 1)
                        sp.dma_start(view(taps[k % 2], r * W, W, yy * W, [[TT, NJ], [1, W]]),
                                     dram(f_ana.tensor, (k * 11 + r - yy + 1) * FROW, [[1, W], [2 * FROW, NJ], [1, W]])
                                     ).then_inc(s_taps[k % 2], 16)

            def load_image(img, u):
                for t, src in ((xin[u], x), (xfin[u], xf)):
                    sp.dma_start(view(t, 0, TT, 0, [[TT, 4], [1, TT]]),
                                 dram(src.tensor, img * (C * H * W), [[TT, TT], [TT * TT, 4], [1, TT]])
                                 ).then_inc(s_xin[u], 16)

            def store_image(pair, u):
                for k in (K - 2, K - 1):
                    sp.wait_ge(s_free[bank_of(u, k)], pair * per[bank_of(u, k)] + nth(u, k) + 1)
                sp.wait_ge(s_nat, pair * 2 + u + 1)
                sp.dma_start(dram(xs0, (pair * 2 + u) * (H * W * DIM), [[DIM, TT], [TT * DIM, NT], [1, DIM]]),
                             view(tok[u], 0, TT, 0, [[DIM, NT], [1, DIM]])).then_inc(s_store[u], 16)

            load_image(0, 0)
            load_taps(0)
            load_taps(1)
            load_image(1, 1)
            for k in range(2, K):
                load_taps(k)
            for m, l, cols, wt, _, _ in mats:
                for d0, s0, nn in pieces(m, cols):
                    sp.dma_start(raw_a[m, l][:, d0:d0 + nn],
                                 dram(wt.tensor, l * DIM * cols + s0, [[cols, 128], [1, nn]])).then_inc(s_raw, 16)
                    sp.dma_start(raw_c[m, l][:, d0:d0 + nn],
                                 dram(wt.tensor, (l * DIM + 128) * cols + s0, [[0, 3], [cols, REST], [1, nn]])).then_inc(s_raw, 16)
            for l in range(2):
                for ln, (g, b) in enumerate(((ln1g, ln1b), (ln2g, ln2b))):
                    col = 2 * l + ln
                    for ta, tc, src in ((gain_a, gain_c, g), (lnb_a, lnb_c, b)):
                        sp.dma_start(ta[:, col:col + 1], dram(src.tensor, l * DIM, [[1, 128], [1, 1]])).then_inc(s_small, 16)
                        sp.dma_start(tc[:, col:col + 1],
                                     dram(src.tensor, l * DIM + 128, [[0, 3], [1, REST], [1, 1]])).then_inc(s_small, 16)
                sp.dma_start(view(keep.w["w2", l], 0, 128, 0, [[DIM, FT], [1, DIM]]),
                              dram(w2.tensor, l * MLP * DIM, [[DIM, 128], [128 * DIM, FT], [1, DIM]])).then_inc(s_small, 16)
                sp.dma_start(keep.w["b2", l][:], dram(b2.tensor, l * DIM, [[0, TT], [1, DIM]])).then_inc(s_small, 16)
            sp.wait_ge(s_zero, 1)
            for m, l, cols, _, b, _ in mats:
                c0 = starts[m, l]
                for d0, s0, nn in pieces(m, cols):
                    sp.dma_start(brow[CR:CK, c0 + d0:c0 + d0 + nn],
                                  dram(b.tensor, l * cols + s0, [[0, 2], [1, nn]])).then_inc(s_small, 16)
            for t, r0, r1 in ((lwt_a, 0, 128), (lwt_b, 128, K * C)):
                sp.dma_start(t[:, 0:128], linwT[r0:r1, 0:128]).then_inc(s_small, 16)
                sp.dma_start(view(t, 0, r1 - r0, 128, [[REST, 3], [1, REST]]),
                             dram(linwT.tensor, r0 * DIM + 128, [[DIM, r1 - r0], [0, 3], [1, REST]])).then_inc(s_small, 16)
            sp.dma_start(linb_a[:], dram(linb.tensor, 0, [[1, 128], [1, 1]])).then_inc(s_small, 16)
            sp.dma_start(linb_b[:], dram(linb.tensor, 128, [[1, C], [1, 1]])).then_inc(s_small, 16)
            c0 = starts["lin", 1]
            sp.dma_start(brow[CR:CK, c0 + K * C:c0 + DIM], dram(convb.tensor, 0, [[0, 2], [1, C]])).then_inc(s_small, 16)
            sp.wait_ge(s_mixz, 1)
            for k in range(K):
                t, p0 = (mix_a, k * C) if k < 8 else (mix_b, 0)
                sp.dma_start(t[p0:p0 + C, k * C:(k + 1) * C], convwT[0:C, :]).then_inc(s_mix, 16)
            sp.dma_start(mix_a[:, K * C:DIM], convwT[C:C + 128, :]).then_inc(s_mix, 16)
            sp.dma_start(mix_b[:, K * C:DIM], convwT[C + 128:DIM, :]).then_inc(s_mix, 16)

            def body(pair):
                for u in range(2):
                    sp.wait_ge(s_nat_T, pair * 2 + u + 1)
                    sp.wait_ge(s_mir_T, pair * 2 + u + 1)
                    load_image(pair * 2 + u + 2, u)
                    store_image(pair, u)

            body(0)
            with sp.Fori(1, B // 2 - 1) as pair:
                body(pair)
            for u in range(2):
                store_image(B // 2 - 1, u)
            for u in range(2):
                sp.wait_ge(s_store[u], 16 * (B // 2))

        @block.gpsimd
        def _(pool):
            gp = nc.gpsimd
            n = [0]

            def step(ins):
                n[0] += 1
                ins.then_inc(s_pool, 1)
                pool.wait_ge(s_pool, n[0])

            for t in (mix_a, mix_b, keep.flip):
                gp.memset(t[:], 0.0)
            gp.memset(relb[:], 0.0)
            gp.memset(keep.qmask[:], float(HD) ** -0.5)
            gp.memset(keep.kmask[:], 1.0)
            gp.memset(keep.ident[:], 0.0).then_inc(s_mixz, 1)
            pool.wait_ge(s_mixz, 1)
            step(gp.affine_select(out=keep.ident[:], in_=keep.ident[:], compare_op=ALU.not_equal, fill=1.0, base=0,
                                  pattern=[[-1, 128]], channel_multiplier=1))
            step(gp.tensor_tensor(sign[:], keep.ident[:, CR:CR + 1], keep.ident[:, CR + 1:CK], ALU.subtract))
            for r in range(2):
                cols = keep.flip[:, r * W:(r + 1) * W]
                gp.affine_select(out=cols, in_=cols, compare_op=ALU.not_equal, fill=1.0,
                                 base=-(r * W + W - 1), pattern=[[1, W]], channel_multiplier=1)
            step(gp.affine_select(out=keep.qmask[:], in_=keep.qmask[:], compare_op=ALU.is_ge, fill=0.0, base=0,
                                  pattern=[[-HD, 4]], channel_multiplier=1))
            gp.affine_select(out=keep.qmask[:], in_=keep.qmask[:], compare_op=ALU.is_ge, fill=0.0, base=HD - 1,
                             pattern=[[HD, 4]], channel_multiplier=-1)
            gp.affine_select(out=keep.kmask[:, 0:1], in_=keep.kmask[:, 0:1], compare_op=ALU.is_ge, fill=0.0,
                             base=WT - 1, pattern=[[0, 1]], channel_multiplier=-1)
            gp.affine_select(out=keep.kmask[:, 1:2], in_=keep.kmask[:, 1:2], compare_op=ALU.is_ge, fill=0.0,
                             base=-WT, pattern=[[0, 1]], channel_multiplier=1)
            with pool.Fori(0, WIN) as yi:
                for xi in range(WIN):
                    pool.dma_start(dram(relT, yi * (WIN * 2 * HEADS * WT) + xi * (2 * HEADS * WT),
                                        [[WT, 2 * HEADS], [WIN, WIN], [1, WIN]]),
                                   dram(rel.tensor, yi * (-(2 * WIN - 1)) + ((WIN - 1) * (2 * WIN - 1) + WIN - 1 - xi),
                                        [[(2 * WIN - 1) ** 2, 2 * HEADS], [2 * WIN - 1, WIN], [1, WIN]])
                                   ).then_inc(s_relT, 16)
            pool.wait_ge(s_relT, 16 * WT)
            for p0 in (0, WP):
                pool.dma_start(relb[p0:p0 + WT, :],
                               dram(relT, 0, [[2 * HEADS * WT, WT], [1, 2 * HEADS * WT]])).then_inc(s_relb, 16)
            pool.dma_start(msk[:], wmask).then_inc(s_relb, 16)
            pool.wait_ge(s_raw, RAWS)
            pool.wait_ge(s_small, SMALL)
            for m, l, cols, _, _, ln in mats:
                hi, lo, rest = keep.w[m, l]
                ra, rc = raw_a[m, l], raw_c[m, l]
                if ln is not None:
                    g = 2 * l + ln
                    gp.tensor_scalar(scaled[:, 0:cols], ra[:], gain_a[:, g:g + 1], None, ALU.mult)
                    step(gp.tensor_scalar(scaled_c[:, 0:cols], rc[:], gain_c[:, g:g + 1], None, ALU.mult))
                    ra, rc = scaled, scaled_c
                gp.tensor_copy(hi[:], ra[:, 0:cols])
                step(gp.tensor_copy(rest[0:CR, :], rc[:, 0:cols]))
                step(gp.tensor_tensor(lo[:], ra[:, 0:cols], hi[:].bitcast(F32), ALU.subtract))
                step(gp.tensor_tensor(rest[2 * REST:CR, :], rc[2 * REST:CR, 0:cols],
                                      rest[2 * REST:CR, :].bitcast(F32), ALU.subtract))
            pool.wait_ge(s_relb, 48)
            for edge in range(5):
                for h in range(HEADS):
                    o = view(keep.tabs, 0, QP, edge * HEADS * GK + h * GK, [[WT, 2], [1, WT]])
                    r = view(relb, 0, QP, (min(edge, 1) * HEADS + h) * WT, [[0, 2], [1, WT]])
                    if edge == 0:
                        last = gp.tensor_copy(o, r)
                    else:
                        last = gp.tensor_tensor(o, r, view(msk, 0, QP, (edge - 1) * GK, [[WT, 2], [1, WT]]), ALU.add)
            step(last)

        @block.scalar
        def _(act):
            def band(k):
                act.wait_ge(s_taps[k % 2], 64 * (k // 2 + 1))
                nc.scalar.activation(band_hi[:, k * NJ * TT:(k + 1) * NJ * TT], taps[k % 2][:], ACT.Copy).then_inc(s_bhi, 1)

            def body(pair, u):
                img = pair * 2 + u
                with_bands = isinstance(img, int) and img == 0

                def output(k):
                    b = bank_of(u, k)
                    act.wait_ge(s_conv[b], pair * per[b] + nth(u, k) + 1)
                    nc.scalar.activation(view(tok[u], 0, TT, k * C, [[DIM, NT], [1, C]]),
                                         view(conv_ps[b], 0, TT, 0, [[C, NT], [1, C]]), ACT.Copy).then_inc(s_free[b], 1)

                act.wait_ge(s_mir_T, img + 1)
                b = bank_of(1 - u, K - 1)
                reach(act, s_conv[b], pair * per[b] + u * (nth(0, K - 1) + 1))
                act.wait_ge(s_zero, 1)
                nc.scalar.activation(view(img_hi, 0, TT, 2 * C, [[1, C], [C, NT]]),
                                     view(mir_ps, 0, TT, 0, [[NT, C], [1, NT]]), ACT.Relu).then_inc(s_ihi, 1)
                act.wait_ge(s_nat_T, img + 1)
                reach(act, s_store[u], pair * 16)
                nc.scalar.activation(view(tok[u], 0, TT, K * C, [[1, C], [DIM, NT]]),
                                     view(nat_ps, 0, TT, 0, [[NT, C], [1, NT]]), ACT.Relu).then_inc(s_nat, 1)
                for k in range(K):
                    if with_bands:
                        band(k)
                    if k % 2 == 1 and k > 2:
                        output(k - 3)
                for k in range(K - 3, K, 2):
                    output(k)

            body(0, 0)
            body(0, 1)
            with act.Fori(1, B // 2) as pair:
                for u in range(2):
                    body(pair, u)
            act.wait_ge(s_brow, 1)
            for m, l in starts:
                cols = slice(starts[m, l], starts[m, l] + keep.w[m, l][2].shape[1])
                nc.scalar.activation(bhi[CR:CK, cols], brow[CR:CK, cols], ACT.Copy).then_inc(s_bhirow, 1)

        @block.vector
        def _(dve):
            nc.vector.memset(brow[:], 0.0)
            nc.vector.memset(img_hi[:].bitcast(F32), 0.0)
            nc.vector.memset(img_lo[:].bitcast(F32), 0.0).then_inc(s_zero, 1)

            def band(k):
                dve.wait_ge(s_bhi, k + 1)
                cols = slice(k * NJ * TT, (k + 1) * NJ * TT)
                nc.vector.tensor_tensor(band_lo[:, cols], taps[k % 2][:], band_hi[:, cols].bitcast(F32),
                                        ALU.subtract).then_inc(s_blo, 1)

            def body(pair, u):
                img = pair * 2 + u
                with_bands = isinstance(img, int) and img == 0

                def output(k):
                    b = bank_of(u, k)
                    dve.wait_ge(s_conv[b], pair * per[b] + nth(u, k) + 1)
                    reach(dve, s_store[u], pair * 16)
                    nc.vector.tensor_copy(view(tok[u], 0, TT, k * C, [[DIM, NT], [1, C]]),
                                          view(conv_ps[b], 0, TT, 0, [[C, NT], [1, C]])).then_inc(s_free[b], 1)

                dve.wait_ge(s_ihi, img + 1)
                nc.vector.scalar_tensor_tensor(view(img_lo, 0, TT, 2 * C, [[1, C], [C, NT]]),
                                               view(mir_ps, 0, TT, 0, [[NT, C], [1, NT]]), 0.0,
                                               view(img_hi, 0, TT, 2 * C, [[1, C], [C, NT]]).bitcast(F32),
                                               ALU.max, ALU.subtract).then_inc(s_ilo, 1)
                for k in range(K):
                    if with_bands:
                        band(k)
                    if k % 2 == 0 and k > 2:
                        output(k - 3)
                output(K - 2)

            body(0, 0)
            body(0, 1)
            with dve.Fori(1, B // 2) as pair:
                for u in range(2):
                    body(pair, u)
            n = 0

            def step(ins):
                nonlocal n
                n += 1
                ins.then_inc(s_prep, 1)
                dve.wait_ge(s_prep, n)

            dve.wait_ge(s_small, SMALL)
            dve.wait_ge(s_bps, 1)
            dve.wait_ge(s_pool, 2)
            hi, lo, rest = keep.w["lin", 1]
            nc.vector.tensor_copy(hi[:], psum[6][:, 0:DIM])
            step(nc.vector.tensor_copy(rest[0:CR, :], psum[6][0:CR, DIM:2 * DIM]))
            nc.vector.tensor_tensor(lo[:], psum[6][:, 0:DIM], hi[:].bitcast(F32), ALU.subtract)
            nc.vector.tensor_tensor(rest[2 * REST:CR, :], psum[6][2 * REST:CR, DIM:2 * DIM],
                                    rest[2 * REST:CR, :].bitcast(F32), ALU.subtract)
            for m, l, banks in (("qkv", 0, (0,)), ("w1", 0, (1, 2)), ("qkv", 1, (3,)), ("w1", 1, (4, 5)), ("lin", 1, (7,))):
                c0 = starts[m, l]
                left = {"qkv": 3 * DIM, "w1": MLP, "lin": DIM}[m]
                for b in banks:
                    nn = min(512, left)
                    last = nc.vector.tensor_tensor(brow[CR:CK, c0:c0 + nn], brow[CR:CK, c0:c0 + nn],
                                                   psum[b][CR:CK, 0:nn], ALU.add)
                    c0, left = c0 + nn, left - nn
            last.then_inc(s_brow, 1)
            dve.wait_ge(s_brow, 1)
            cols = slice(0, width)
            step(nc.vector.tensor_scalar(blo[CR:CK, cols], brow[CR:CK, cols], keep.ident[CR:CK, CR + 1:CK], None, ALU.mult))
            for n_w, (m, l) in enumerate(starts):
                rest = keep.w[m, l][2]
                cols = slice(starts[m, l], starts[m, l] + rest.shape[1])
                dve.wait_ge(s_bhirow, n_w + 1)
                nc.vector.scalar_tensor_tensor(rest[CR:CK, :], bhi[CR:CK, cols].bitcast(F32), sign[CR:CK, :],
                                               blo[CR:CK, cols], ALU.mult, ALU.add)

        @block.tensor
        def _(pe):
            def turn(u, img):
                pe.wait_ge(s_xin[u], (img - u) * 16 + 32)
                reach(pe, s_ilo, img)
                for q in range(4):
                    last = nc.tensor.transpose(mir_ps[0:TT, q * TT:(q + 1) * TT], xfin[u][:, q * TT:(q + 1) * TT],
                                               keep.ident[0:TT, 0:TT])
                last.then_inc(s_mir_T, 1)
                reach(pe, s_nat, img)
                for q in range(4):
                    last = nc.tensor.transpose(nat_ps[0:TT, q * TT:(q + 1) * TT], xin[u][:, q * TT:(q + 1) * TT],
                                               keep.ident[0:TT, 0:TT])
                last.then_inc(s_nat_T, 1)

            pe.wait_ge(s_pool, 1)

            def body(pair, u):
                img = pair * 2 + u
                turn(u, img)
                pe.wait_ge(s_ilo, img + 1)
                for k in range(K):
                    if isinstance(img, int) and img == 0:
                        pe.wait_ge(s_blo, k + 1)
                    b = bank_of(u, k)
                    reach(pe, s_free[b], pair * per[b] + nth(u, k))
                    n = 0
                    for j in range(NJ):
                        cols = slice((k * NJ + j) * TT, (k * NJ + j + 1) * TT)
                        rows = slice(j * C, (j + NT) * C)
                        for a, m in ((band_hi, img_hi), (band_hi, img_lo), (band_lo, img_hi)):
                            last = nc.tensor.matmul(conv_ps[b][0:TT, 0:NT * C], a[:, cols], m[:, rows],
                                                    start=(n == 0), stop=(n == 3 * NJ - 1))
                            n += 1
                    last.then_inc(s_conv[b], 1)

            body(0, 0)
            body(0, 1)
            with pe.Fori(1, B // 2) as pair:
                for u in range(2):
                    body(pair, u)
            pe.wait_ge(s_raw, RAWS)
            pe.wait_ge(s_small, SMALL)
            pe.wait_ge(s_mix, MIX)
            for b in range(NB):
                pe.wait_ge(s_free[b], per[b] * (B // 2))
            pe.wait_ge(s_nat, B)
            pe.wait_ge(s_ilo, B)

            def bcast(t, p, col, n):
                return view(t, 0, p, col, [[0, n]])

            for (m, l, ln), banks in ((("qkv", 0, 0), (0,)), (("w1", 0, 1), (1, 2)), (("qkv", 1, 0), (3,)), (("w1", 1, 1), (4, 5))):
                c0, total = 0, raw_a[m, l].shape[1]
                for b in banks:
                    nn = min(512, total - c0)
                    nc.tensor.matmul(psum[b][0:CK, 0:nn], bcast(lnb_a, 128, 2 * l + ln, CK), raw_a[m, l][:, c0:c0 + nn],
                                     start=True, stop=False)
                    nc.tensor.matmul(psum[b][0:CK, 0:nn], bcast(lnb_c, REST, 2 * l + ln, CK), raw_c[m, l][0:REST, c0:c0 + nn],
                                     start=False, stop=True)
                    c0 += nn
            for o, wa, wb in ((psum[6][:, 0:DIM], lwt_a[:, 0:128], lwt_b[:, 0:128]),
                              (psum[6][0:CR, DIM:2 * DIM], lwt_a[:, 128:ZW], lwt_b[:, 128:ZW]),
                              (psum[7][0:CK, 0:DIM], bcast(linb_a, 128, 0, CK), bcast(linb_b, C, 0, CK))):
                nc.tensor.matmul(o, wa, mix_a[:], start=True, stop=False)
                last = nc.tensor.matmul(o, wb, mix_b[:], start=False, stop=True)
            last.then_inc(s_bps, 1)


def phase_b(nc, keep, xs0, xs1, ys):
    with ExitStack() as ctx:
        def sb(name, shape, dt=F32):
            return ctx.enter_context(nc.sbuf_tensor(name, shape, dt))

        def sem(name):
            return ctx.enter_context(nc.semaphore(name))

        def bank(name):
            return ctx.enter_context(nc.psum_tensor(name, [128, 512], F32))

        ra = [bank(f"ra{n}") for n in range(3)]
        rm = [bank(f"rm{n}") for n in range(2)]
        s_ps, pt_ps, o_ps = bank("s_ps"), bank("pt_ps"), bank("o_ps")
        PT4 = HEADS * 2 * VW

        xa, xr = sb("xa", [TT, ST * DIM]), sb("xr", [TT, ST * DIM])
        x1, x1b = sb("x1", [TT, ST * DIM]), sb("x1b", [TT, ST * DIM])
        xo, yz = sb("xo", [TT, ST * ZW]), sb("yz", [TT, ST * DIM])
        z1, z2 = sb("z1", [TT, ST * ZW]), sb("z2", [TT, ST * ZW])
        st = [sb(f"st{n}", [TT, ST * 6]) for n in range(2)]
        mean = [sb(f"mean{n}", [TT, ST]) for n in range(2)]
        rs = [sb(f"rs{n}", [TT, ST]) for n in range(2)]
        half, mhalf, by_dim, eps = sb("half", [TT, ST]), sb("mhalf", [TT, ST]), sb("by_dim", [TT, ST]), sb("eps", [TT, ST])
        one = sb("one", [TT, 1])
        ln_tmp = [[sb(f"ln_tmp{n}_{k}", [TT, ST]) for k in range(8)] for n in range(2)]
        z1t = [sb("z1t_hi", [128, SN], F32R), sb("z1t_lo", [128, SN], F32R), sb("z1t_rest", [CK, SN], F32R)]
        z2t = [sb("z2t_hi", [128, SN], F32R), sb("z2t_lo", [128, SN], F32R), sb("z2t_rest", [CK, SN], F32R)]
        ot = [sb("ot_hi", [128, SN], F32R), sb("ot_lo", [128, SN], F32R), sb("ot_rest", [CK, SN], F32R)]
        qm = sb("qm", [128, 4 * SN])
        kt = sb("kt", [128, SN])
        q4, k4 = sb("q4", [128, SN]), sb("k4", [128, SN])
        VG = 2 * 2 * HEADS * VW
        vb = sb("vb", [GK, NG * VG])
        sc = sb("sc", [QP, HEADS * GK])
        mx = sb("mx", [QP, 2 * HEADS])
        sm = [sb(f"sm{n}", [QP, HEADS * GK]) for n in range(2)]
        pr = sb("pr", [QP, HEADS * GK])
        pt = sb("pt", [GK, HEADS * QP])
        rd = sb("rd", [QP, 2 * HEADS])
        os_ = sb("os", [QP, 2 * ZW])
        ht = sb("ht", [128, FT * SN])

        s_xa, s_xr, s_xo, s_yz, s_dup = sem("xa_in"), sem("xr_in"), sem("xo_out"), sem("yz_out"), sem("dup")
        s_init = sem("b_init")
        ra_full = [sem(f"ra_full{n}") for n in range(3)]
        ra_free = [sem(f"ra_free{n}") for n in range(3)]
        rm_full = [sem(f"rm_full{n}") for n in range(2)]
        rm_free = [sem(f"rm_free{n}") for n in range(2)]
        s_st = [sem("stats1"), sem("stats2")]
        s_rs = [sem("rs1"), sem("rs2")]
        s_pow = sem("pow2")
        s_norm = [sem("norm1"), sem("norm2")]
        s_z = [sem("z1_full"), sem("z2_full")]
        s_hi1, s_hi2, s_oth = sem("z1t_hi_done"), sem("z2t_hi_done"), sem("ot_hi_done")
        s_sfull, s_sadd, s_smax, s_ssub = sem("s_full"), sem("s_add"), sem("s_max"), sem("s_sub")
        s_exp, s_ptf, s_pte, s_of, s_rec, s_od = (sem("exp_done"), sem("pt_full"), sem("pt_out"), sem("o_full"),
                                                  sem("o_rec"), sem("o_done"))
        s_x1b, s_xod = sem("x1b_done"), sem("xo_dup")

        FRONT = ["T1A0", "T1C0", "T1A1", "T1C1", "Q0", "K0", "B0", "Q1", "K1", "B1", "V0", "V1", "V2", "V3"]
        V_READERS = {f"V{j}": 2 for j in range(NG)}
        PRO = Ring(FRONT, 3, V_READERS)
        RA = Ring(["OT0", "OT1", "T1A0", "T1C0", "T1A1", "T1C1", "OT2", "Q0", "K0", "OT3", "P0", "P1", "B0", "Q1", "P2",
                   "K1", "B1", "V0", "V1", "V2", "V3"], 3, V_READERS)
        END = Ring(["OT0", "OT1", "OT2", "OT3", "P0", "P1", "P2"], 3, {})
        PAIRS = [(0, 2), (2, 1), (3, 1), (4, 1), (5, 1), (6, 1)]
        LPAIRS = [(0, 2), (2, 2), (4, 2), (6, 1)]
        T2 = ["T2A0", "T2C0", "T2A1", "T2C1"]
        MLP_USES = [f"G{g}" for g in range(2 * FT)] + [f"W{n}" for n in range(len(PAIRS))]
        LIN_USES = ["T3A0", "T3C0", "T3A1", "T3C1", "L0", "L1", "L2", "L3"]
        RM0 = Ring(T2, 2, {})
        RM = [Ring(MLP_USES + T2, 2, {}), Ring(MLP_USES + LIN_USES + T2, 2, {})]
        RS_STEPS = [5, 3]
        PROJ = [(0, 1), (1, 3), (4, 3)]
        QH = SN // 2

        def ring_a(i):
            if isinstance(i, int) and i < 0:
                return PRO
            return END if isinstance(i, int) and i == 2 * NS - 1 else RA

        def bank_a(i, use):
            return ra[ring_a(i).slot(use)]

        def a_full(i, use):
            ring = ring_a(i)
            s = ring.slot(use)
            before = 0 if ring is PRO else PRO.fills(s) + i * RA.fills(s)
            return ra_full[s], before + ring.filled(use)

        def a_room(i, use):
            ring = ring_a(i)
            s = ring.slot(use)
            before = 0 if ring is PRO else PRO.frees(s) + i * RA.frees(s)
            return ra_free[s], before + ring.freed_before(use)

        def a_freed(i, use, readers=None):
            ring = ring_a(i)
            s, n = a_room(i, use)
            return s, n + (ring.weight[ring.at[use]] if readers is None else readers)

        def ring_m(i, lm):
            return RM0 if lm is None else RM[lm]

        def bank_m(i, lm, use):
            return rm[ring_m(i, lm).slot(use)]

        def m_before(i, lm, per):
            if lm is None:
                return 0
            return per[0] + ((i - 1) * per[1] if lm == 0 else NS * per[1] + (i - NS - 1) * per[2])

        M_USES = [len(r.uses) // 2 for r in (RM0, *RM)]

        def m_count(i, lm, use):
            return m_before(i, lm, M_USES) + ring_m(i, lm).filled(use)

        def m_full(i, lm, use):
            return rm_full[ring_m(i, lm).slot(use)], m_count(i, lm, use)

        def m_freed(i, lm, use):
            return rm_free[ring_m(i, lm).slot(use)], m_count(i, lm, use)

        def m_room(i, lm, use):
            return rm_free[ring_m(i, lm).slot(use)], m_count(i, lm, use) - 1

        def t2_freed(i, lm):
            return rm_free[1], m_before(i, lm, M_USES)

        def hi2(i, lm, name, n):
            return m_before(i, lm, [4, 4, 8]) + (4 if name == "T2" and lm == 1 else 0) + n

        block = ctx.enter_context(nc.Block())

        def bodies(engine, body):
            body(-1, None, None, 0)
            body(0, 0, None, 0)
            body(1, 0, 0, 0)
            with engine.Fori(2, NS - 1) as i:
                body(i, 0, 0, 0)
            body(NS - 1, 0, 0, 1)
            body(NS, 1, 0, 1)
            body(NS + 1, 1, 1, 1)
            with engine.Fori(NS + 2, 2 * NS - 1) as i:
                body(i, 1, 1, 1)
            body(2 * NS - 1, 1, 1, None)
            body(2 * NS, None, 1, None)

        @block.sync
        def _(sp):
            def strip(n, l, yy):
                if l == 0:
                    return dram(xs0, n * (SR * W * DIM) + yy * W * DIM, [[DIM, W], [TT * DIM, ST], [1, DIM]])
                k = n - NS
                off = k * (SR * HP * DIM) + (k // SPI) * (SHIFT * HP * DIM) + (SHIFT + yy) * HP * DIM + SHIFT * DIM
                return dram(xs1, off, [[DIM, W], [2 * HP * DIM, ST], [1, DIM]])

            def load(t, s, n, l):
                for yy in range(2):
                    sp.dma_start(view(t, yy * W, W, 0, [[DIM, ST], [1, DIM]]), strip(n, l, yy)).then_inc(s, 16)

            def store(m, l):
                for yy in range(2):
                    if l == 0:
                        off = m * (SR * HP * DIM) + (m // SPI) * (SHIFT * HP * DIM) + yy * HP * DIM
                        sp.dma_start(dram(xs1, off, [[DIM, W], [2 * HP * DIM, ST], [1, DIM]]),
                                     view(xo, yy * W, W, 0, [[ZW, ST], [1, DIM]])).then_inc(s_xo, 16)
                    else:
                        sp.dma_start(dram(ys, (m - NS) * (SR * W * DIM) + yy * W * DIM, [[DIM, W], [TT * DIM, ST], [1, DIM]]),
                                     view(yz, yy * W, W, 0, [[DIM, ST], [1, DIM]])).then_inc(s_yz, 16)

            def repeat_margins(b0, nb):
                img, row = HP * HP * DIM, HP * DIM
                for b in range(b0, b0 + nb):
                    sp.dma_start(dram(xs1, b * img + W * DIM, [[row, H], [1, SHIFT * DIM]]),
                                 dram(xs1, b * img, [[row, H], [1, SHIFT * DIM]])).then_inc(s_dup, 16)
                    sp.dma_start(dram(xs1, b * img + H * row, [[row, SHIFT], [1, W * DIM]]),
                                 dram(xs1, b * img, [[row, SHIFT], [1, W * DIM]])).then_inc(s_dup, 16)
                    sp.dma_start(dram(xs1, b * img + H * row + W * DIM, [[row, SHIFT], [1, SHIFT * DIM]]),
                                 dram(xs1, b * img, [[row, SHIFT], [1, SHIFT * DIM]])).then_inc(s_dup, 16)

            def body(i, la, lm, ahead=None):
                if ahead is not None:
                    sp.wait_ge(s_norm[0], i + 2)
                    load(xa, s_xa, i + 2, ahead)
                if lm is not None:
                    use = "W5" if lm == 0 else "L3"
                    sp.wait_ge(*m_freed(i, lm, use))
                    store(i - 1, lm)
                if la is not None and not (isinstance(i, int) and i == 2 * NS - 1):
                    sp.wait_ge(*a_freed(i, "P2"))
                    nxt = 1 if (isinstance(i, int) and i == NS - 1) or la == 1 else 0
                    load(xr, s_xr, i + 1, nxt)

            load(xa, s_xa, 0, 0)
            load(xr, s_xr, 0, 0)
            sp.wait_ge(s_norm[0], 1)
            load(xa, s_xa, 1, 0)
            body(0, 0, None, 0)
            body(1, 0, 0, 0)
            with sp.Fori(2, NS - 2) as i:
                body(i, 0, 0, 0)
            sp.wait_ge(s_xo, 32 * (NS - 3))
            repeat_margins(0, B - 1)
            sp.wait_ge(s_dup, 48 * (B - 1))
            body(NS - 2, 0, 0, 1)
            body(NS - 1, 0, 0, 1)
            body(NS, 1, 0, 1)
            sp.wait_ge(s_xo, 32 * NS)
            repeat_margins(B - 1, 1)
            sp.wait_ge(s_dup, 48 * B)
            with sp.Fori(NS + 1, 2 * NS - 2) as i:
                body(i, 1, 1, 1)
            body(2 * NS - 2, 1, 1)
            body(2 * NS - 1, 1, 1)
            body(2 * NS, None, 1)
            sp.wait_ge(s_yz, 32 * NS)

        @block.gpsimd
        def _(pool):
            gp = nc.gpsimd

            def inv_std(i):
                me, se, mo, so = (view(st[0], 0, TT, c, [[6, ST]]) for c in (1, 2, 4, 5))
                total, diff, sq, hdiff, sq1, hsq, sq2, var = ln_tmp[0]
                steps = [[(total[:], me, mo, ALU.add), (diff[:], me, mo, ALU.subtract), (sq[:], se, so, ALU.add)],
                         [(mean[0][:], total[:], half[:], ALU.mult), (hdiff[:], diff[:], half[:], ALU.mult),
                          (sq1[:], sq[:], by_dim[:], ALU.mult)],
                         [(hsq[:], hdiff[:], hdiff[:], ALU.mult), (sq2[:], sq1[:], eps[:], ALU.add)],
                         [(var[:], hsq[:], sq2[:], ALU.add)],
                         [(rs[0][:], var[:], mhalf[:], ALU.pow)]]
                pool.wait_ge(s_st[0], i + 1)
                for k, ops in enumerate(steps):
                    if k:
                        pool.wait_ge(s_rs[0], len(steps) * i + k)
                    for o, x_, y_, op in ops:
                        ins = gp.tensor_tensor(o, x_, y_, op)
                    ins.then_inc(s_rs[0], 1)
                assert len(steps) == RS_STEPS[0]

            def repeat_rest(t, s, t0=0, nt=ST):
                once = view(t, 0, TT, t0 * ZW + 128, [[ZW, nt], [0, 2], [1, REST]])
                gp.tensor_tensor(view(t, 0, TT, t0 * ZW + DIM, [[ZW, nt], [REST, 2], [1, REST]]), once,
                                 view(one, 0, TT, 0, [[0, nt], [0, 2], [0, REST]]), ALU.mult).then_inc(s, 1)

            for t, c in ((half, 0.5), (by_dim, 1.0 / DIM), (eps, EPS), (one, 1.0)):
                gp.memset(t[:], c)
            gp.memset(mhalf[:], -0.5).then_inc(s_init, 1)
            pool.wait_ge(s_init, 1)

            def body(i, la, lm, ln):
                if ln is not None:
                    inv_std(i + 1)
                    pool.wait_ge(s_norm[0], i + 2)
                    repeat_rest(z1, s_z[0])
                if lm == 1:
                    for use, (t0, nt) in zip(("W2", "W5"), HALF):
                        pool.wait_ge(*m_freed(i, 1, use))
                        repeat_rest(xo, s_xod, t0, nt)
                if la is not None:
                    for hf, (t0, nt) in enumerate(HALF):
                        pool.wait_ge(s_rs[1], RS_STEPS[1] * (2 * i + hf + 1))
                        gp.tensor_tensor(rs[1][:, t0:t0 + nt], ln_tmp[1][5][:, t0:t0 + nt], mhalf[:, 0:nt], ALU.pow).then_inc(s_pow, 1)
                    for hf in range(2):
                        pool.wait_ge(s_norm[1], 2 * i + hf + 1)
                        repeat_rest(z2, s_z[1], *HALF[hf])
                    for t in range(ST):
                        ins = gp.tensor_tensor(x1b[:, t * DIM:(t + 1) * DIM], x1[:, t * DIM:(t + 1) * DIM],
                                               keep.w["b2", la][:], ALU.add)
                    ins.then_inc(s_x1b, 1)

            bodies(pool, body)

        @block.scalar
        def _(act):
            act_ = nc.scalar.activation

            def body(i, la, lm, ln):
                m = i - 1

                def front_hi(hf):
                    t0, nt = HALF[hf]
                    for part, dst, rows in (("A", z1t[0], 128), ("C", z1t[2], CR)):
                        use = f"T1{part}{hf}"
                        act.wait_ge(*a_full(i, use))
                        act_(view(dst, 0, rows, t0 * 2 * WIN, [[WIN, 2 * nt], [GK, 8], [1, WIN]]),
                             view(bank_a(i, use), 0, rows, 0, [[W, 2 * nt], [WIN, 8], [1, WIN]]), ACT.Copy).then_inc(s_hi1, 1)

                def queries(hf):
                    use = f"Q{hf}"
                    act.wait_ge(*a_full(i, use))
                    for h in range(4):
                        last = act_(qm[:, h * SN + hf * QH:h * SN + (hf + 1) * QH], bank_a(i, use)[:, 0:QH], ACT.Copy,
                                    scale=keep.qmask[:, h:h + 1])
                    last.then_inc(a_freed(i, use)[0], 1)

                def keys(hf):
                    use = f"K{hf}"
                    act.wait_ge(*a_full(i, use))
                    act_(kt[:, hf * QH:(hf + 1) * QH], bank_a(i, use)[:, 0:QH], ACT.Copy).then_inc(a_freed(i, use)[0], 1)

                def fifth_head(hf):
                    use = f"B{hf}"
                    act.wait_ge(*a_full(i, use))
                    cols = slice(hf * QH, (hf + 1) * QH)
                    act_(q4[0:HD, cols], bank_a(i, use)[0:HD, 0:QH], ACT.Copy, scale=float(HD) ** -0.5)
                    act_(k4[0:HD, cols], bank_a(i, use)[HD:2 * HD, 0:QH], ACT.Copy).then_inc(a_freed(i, use)[0], 1)

                def values(j, p):
                    use = f"V{j}"
                    act.wait_ge(*a_full(i, use))
                    act_(view(vb, 0, GK, j * VG + p * 2 * HEADS * VW, [[VW, 2 * HEADS], [1, HD]]),
                         view(bank_a(i, use), 0, GK, 0, [[HD, 2 * HEADS], [1, HD]]), ACT.Copy,
                         scale=keep.kmask[:, p:p + 1]).then_inc(a_freed(i, use)[0], 1)

                def exps(j):
                    act.wait_ge(s_ssub, i * NG + j + 1)
                    act_(pr[:], sm[j % 2][:], ACT.Exp).then_inc(s_exp, 1)

                def weights_out(j):
                    act.wait_ge(s_ptf, i * NG + j + 1)
                    act_(pt[:, 0:4 * QP], pt_ps[0:GK, 0:4 * QP], ACT.Copy)
                    act_(pt[:, 4 * QP:5 * QP], o_ps[0:GK, PT4:PT4 + QP], ACT.Copy).then_inc(s_pte, 1)

                def outputs_hi(j):
                    use = f"OT{j}"
                    act.wait_ge(*a_full(i, use))
                    for dst, rows, c0 in ((ot[0], 128, 0), (ot[2], CR, 2 * QP)):
                        for p in range(2):
                            last = act_(view(dst, 0, rows, p * WIN * W + j * 2 * WIN, [[WIN, 2], [W, WIN], [1, WIN]]),
                                        view(bank_a(i, use), 0, rows, c0 + p * QP, [[WP, 2], [WIN, WIN], [1, WIN]]), ACT.Copy)
                    last.then_inc(s_oth, 1)

                def t_hi(name, hf):
                    t0, nt = HALF[hf]
                    for part, dst, rows in (("A", z2t[0], 128), ("C", z2t[2], CR)):
                        use = f"{name}{part}{hf}"
                        act.wait_ge(*m_full(i, lm, use))
                        act_(dst[0:rows, t0 * TT:(t0 + nt) * TT], bank_m(i, lm, use)[0:rows, 0:nt * TT],
                             ACT.Copy).then_inc(s_hi2, 1)

                if lm is not None:
                    for g in range(2 * FT):
                        hf, f = divmod(g, FT)
                        t0, nt = HALF[hf]
                        use = f"G{g}"
                        act.wait_ge(*m_full(i, lm, use))
                        act_(ht[:, f * SN + t0 * TT:f * SN + (t0 + nt) * TT], bank_m(i, lm, use)[:, 0:nt * TT],
                             ACT.Gelu_apprx_tanh).then_inc(m_freed(i, lm, use)[0], 1)
                if la is not None:
                    exps(0)
                    weights_out(0)
                    exps(1)
                    outputs_hi(0)
                    weights_out(1)
                    exps(2)
                    outputs_hi(1)
                    weights_out(2)
                if ln is not None:
                    front_hi(0)
                if la is not None:
                    exps(3)
                if ln is not None:
                    front_hi(1)
                if la is not None:
                    outputs_hi(2)
                    weights_out(3)
                if ln is not None:
                    queries(0)
                    keys(0)
                if la is not None:
                    outputs_hi(3)
                if lm == 1:
                    t_hi("T3", 0)
                if ln is not None:
                    fifth_head(0)
                    queries(1)
                if lm == 1:
                    t_hi("T3", 1)
                if ln is not None:
                    keys(1)
                    fifth_head(1)
                    values(0, 0)
                if lm == 1:
                    for n in range(4):
                        use = f"L{n}"
                        t0, nt = LPAIRS[n]
                        act.wait_ge(*m_full(i, 1, use))
                        if n == 0:
                            reach(act, s_yz, 32 * (m - NS))
                        act_(yz[:, t0 * DIM:(t0 + nt) * DIM], bank_m(i, 1, use)[0:TT, 0:nt * DIM],
                             ACT.Copy).then_inc(m_freed(i, 1, use)[0], 1)
                if la is not None:
                    t_hi("T2", 0)
                if ln is not None:
                    values(1, 0)
                if la is not None:
                    t_hi("T2", 1)

            bodies(act, body)

        @block.vector
        def _(dve):
            v = nc.vector

            def stats(n, x_, i, tiles=range(ST), last=True):
                for t in tiles:
                    ins = v.bn_stats(st[n][:, t * 6:(t + 1) * 6], x_[:, t * DIM:(t + 1) * DIM])
                if last:
                    ins.then_inc(s_st[n], 1)

            def variance(i, hf):
                t0, nt = HALF[hf]
                me, se, mo, so = (view(st[1], 0, TT, t0 * 6 + c, [[6, nt]]) for c in (1, 2, 4, 5))
                total, diff, sq, hsq, sq2, var = (t[:, t0:t0 + nt] for t in ln_tmp[1][0:6])
                n = 2 * i + hf
                dve.wait_ge(s_st[1], n + 1)
                v.tensor_tensor(total, me, mo, ALU.add)
                v.tensor_tensor(diff, me, mo, ALU.subtract)
                v.tensor_tensor(sq, se, so, ALU.add).then_inc(s_rs[1], 1)
                dve.wait_ge(s_rs[1], RS_STEPS[1] * n + 1)
                v.tensor_scalar(mean[1][:, t0:t0 + nt], total, 0.5, None, ALU.mult)
                v.tensor_scalar(sq2, sq, 1.0 / DIM, EPS, ALU.mult, ALU.add)
                v.scalar_tensor_tensor(hsq, diff, 0.25, diff, ALU.mult, ALU.mult).then_inc(s_rs[1], 1)
                dve.wait_ge(s_rs[1], RS_STEPS[1] * n + 2)
                v.tensor_tensor(var, hsq, sq2, ALU.add).then_inc(s_rs[1], 1)

            def normalise(n, z, x_, i, parts):
                if n == 0:
                    dve.wait_ge(s_rs[0], RS_STEPS[0] * (i + 1))
                for hf, (t0, nt) in enumerate(parts):
                    if n == 1:
                        dve.wait_ge(s_pow, 2 * i + hf + 1)
                    for t in range(t0, t0 + nt):
                        ins = v.tensor_scalar(z[:, t * ZW:t * ZW + DIM], x_[:, t * DIM:(t + 1) * DIM],
                                              mean[n][:, t:t + 1], rs[n][:, t:t + 1], ALU.subtract, ALU.mult)
                    ins.then_inc(s_norm[n], 1)

            v.memset(q4[:], 0.0)
            v.memset(k4[:], 0.0)
            for t in (z1t[2], z2t[2], ot[2]):
                v.memset(t[CR:CK, :].bitcast(F32), 1.0)
            for j in range(NG):
                for p in range(2):
                    v.tensor_copy(view(vb, 0, GK, j * VG + p * 2 * HEADS * VW + HD, [[VW, 2 * HEADS]]),
                                  view(keep.kmask, 0, GK, p, [[0, 2 * HEADS]]))
            v.memset(s_ps[:], 0.0)
            v.memset(o_ps[:], 1.0).then_inc(s_init, 1)

            def body(i, la, lm, ln):
                m = i - 1

                def front_lo(hf):
                    t0, nt = HALF[hf]
                    for n, (part, dst, src, p0, rows) in enumerate((("A", z1t[1], z1t[0], 0, 128),
                                                                   ("C", z1t[2], z1t[2], REST, REST))):
                        use = f"T1{part}{hf}"
                        dve.wait_ge(s_hi1, (i + 1) * 4 + 2 * hf + n + 1)
                        dims = [[WIN, 2 * nt], [GK, 8], [1, WIN]]
                        v.tensor_tensor(view(dst, p0, rows, t0 * 2 * WIN, dims),
                                        view(bank_a(i, use), p0, rows, 0, [[W, 2 * nt], [WIN, 8], [1, WIN]]),
                                        view(src, p0, rows, t0 * 2 * WIN, dims).bitcast(F32),
                                        ALU.subtract).then_inc(a_freed(i, use)[0], 1)

                def values(j, p):
                    use = f"V{j}"
                    dve.wait_ge(*a_full(i, use))
                    if p == 1:
                        dve.wait_ge(*a_freed(i, use, 1))
                    v.tensor_scalar(view(vb, 0, GK, j * VG + p * 2 * HEADS * VW, [[VW, 2 * HEADS], [1, HD]]),
                                    view(bank_a(i, use), 0, GK, 0, [[HD, 2 * HEADS], [1, HD]]),
                                    keep.kmask[:, p:p + 1], None, ALU.mult).then_inc(a_freed(i, use)[0], 1)

                def scores(j, n_, l):
                    n = n_ * NG + j + 1
                    dve.wait_ge(s_sfull, n)
                    if l == 0:
                        tab = keep.tabs[:, 0:HEADS * GK]
                    else:
                        bottom = (n_ % SPI) // (SPI - 1)
                        off = bottom * (2 * HEADS * GK) + (1 + (j == NG - 1)) * HEADS * GK
                        tab = view(keep.tabs, 0, QP, off, [[1, HEADS * GK]])
                    reach(dve, s_ssub, n - 1)
                    v.tensor_tensor(sc[:], s_ps[0:QP, 0:HEADS * GK], tab, ALU.add).then_inc(s_sadd, 1)
                    dve.wait_ge(s_sadd, n)
                    s3 = sc[:].rearrange("q (g k) -> q g k", k=WT)
                    v.tensor_reduce(mx[:], s3, AX.X, ALU.max).then_inc(s_smax, 1)
                    dve.wait_ge(s_smax, n)
                    reach(dve, s_exp, n - 2)
                    v.tensor_tensor(sm[j % 2][:].rearrange("q (g k) -> q g k", k=WT), s3,
                                    view(mx, 0, QP, 0, [[1, 2 * HEADS], [0, WT]]), ALU.subtract).then_inc(s_ssub, 1)

                def outputs(j):
                    n = i * NG + j + 1
                    dve.wait_ge(s_of, n)
                    v.reciprocal(rd[:], view(o_ps, 0, QP, HD, [[VW, 2 * HEADS]])).then_inc(s_rec, 1)
                    dve.wait_ge(s_rec, n)
                    v.tensor_tensor(view(os_, 0, QP, 0, [[ZW, 2], [HD, 4], [1, HD]]),
                                    view(o_ps, 0, QP, 0, [[VW, 2], [2 * VW, 4], [1, HD]]),
                                    view(rd, 0, QP, 0, [[1, 2], [2, 4], [0, HD]]), ALU.mult)
                    v.tensor_tensor(view(os_, 0, QP, 128, [[ZW, 2], [HD, 3], [1, HD]]),
                                    view(o_ps, 0, QP, 4 * 2 * VW, [[VW, 2], [0, 3], [1, HD]]),
                                    view(rd, 0, QP, 8, [[1, 2], [0, 3], [0, HD]]), ALU.mult).then_inc(s_od, 1)

                def outputs_lo(j):
                    use = f"OT{j}"
                    dve.wait_ge(s_oth, i * NG + j + 1)
                    for dst, src, p0, rows, c0 in ((ot[1], ot[0], 0, 128, 0), (ot[2], ot[2], REST, REST, 2 * QP)):
                        for p in range(2):
                            o = p * WIN * W + j * 2 * WIN
                            dims = [[WIN, 2], [W, WIN], [1, WIN]]
                            ins = v.tensor_tensor(view(dst, p0, rows, o, dims),
                                                  view(bank_a(i, use), p0, rows, c0 + p * QP, [[WP, 2], [WIN, WIN], [1, WIN]]),
                                                  view(src, p0, rows, o, dims).bitcast(F32), ALU.subtract)
                    ins.then_inc(a_freed(i, use)[0], 1)

                def t_lo(name, hf):
                    t0, nt = HALF[hf]
                    cols = slice(t0 * TT, (t0 + nt) * TT)
                    for n, (part, dst, src, rows) in enumerate((("A", z2t[1], z2t[0], slice(0, 128)),
                                                               ("C", z2t[2], z2t[2], slice(REST, 2 * REST)))):
                        use = f"{name}{part}{hf}"
                        dve.wait_ge(s_hi2, hi2(i, lm, name, 2 * hf + n + 1))
                        v.tensor_tensor(dst[rows, cols], bank_m(i, lm, use)[rows, 0:nt * TT], src[rows, cols].bitcast(F32),
                                        ALU.subtract).then_inc(m_freed(i, lm, use)[0], 1)

                def mlp_out(n):
                    use = f"W{n}"
                    t0, nt = PAIRS[n]
                    dve.wait_ge(*m_full(i, lm, use))
                    if n == 0:
                        dve.wait_ge(s_x1b, m + 1)
                        reach(dve, s_xo, 32 * m if lm == 0 else 32 * NS)
                    v.tensor_tensor(view(xo, 0, TT, t0 * ZW, [[ZW, nt], [1, DIM]]),
                                    view(bank_m(i, lm, use), 0, TT, 0, [[DIM, nt], [1, DIM]]),
                                    view(x1b, 0, TT, t0 * DIM, [[DIM, nt], [1, DIM]]),
                                    ALU.add).then_inc(m_freed(i, lm, use)[0], 1)

                if ln is not None:
                    dve.wait_ge(s_xa, 32 * (i + 2))
                    stats(0, xa, i + 1)
                if la is not None:
                    scores(1, i, la)
                if ln is not None:
                    normalise(0, z1, xa, i + 1, [(0, ST)])
                if lm is not None:
                    mlp_out(0)
                if la is not None:
                    outputs(0)
                    scores(2, i, la)
                if lm is not None:
                    mlp_out(1)
                if la is not None:
                    outputs_lo(0)
                    outputs(1)
                    scores(3, i, la)
                if lm is not None:
                    mlp_out(2)
                if la is not None:
                    outputs_lo(1)
                if ln is not None:
                    front_lo(0)
                if la is not None:
                    outputs(2)
                if ln is not None:
                    front_lo(1)
                if lm is not None:
                    mlp_out(3)
                if la is not None:
                    outputs_lo(2)
                    outputs(3)
                if lm is not None:
                    mlp_out(4)
                if la is not None:
                    outputs_lo(3)
                if lm is not None:
                    mlp_out(5)
                if lm == 1:
                    t_lo("T3", 0)
                if la is not None:
                    dve.wait_ge(s_xr, 32 * (i + 1))
                    reach(dve, s_x1b, i)

                    def residual(n):
                        use = f"P{n}"
                        dve.wait_ge(*a_full(i, use))
                        cols = slice(PROJ[n][0] * DIM, sum(PROJ[n]) * DIM)
                        v.tensor_tensor(x1[:, cols], bank_a(i, use)[0:TT, 0:PROJ[n][1] * DIM], xr[:, cols],
                                        ALU.add).then_inc(a_freed(i, use)[0], 1)

                    def x1_stats(n, last):
                        dve.wait_ge(*a_freed(i, f"P{n}"))
                        stats(1, x1, i, range(PROJ[n][0], sum(PROJ[n])), last)

                    residual(0)
                    residual(1)
                    x1_stats(0, False)
                    x1_stats(1, True)
                    variance(i, 0)
                    residual(2)
                    x1_stats(2, True)
                    variance(i, 1)
                if lm == 1:
                    t_lo("T3", 1)
                if la is not None:
                    normalise(1, z2, x1, i, HALF)
                if ln is not None:
                    values(0, 1)
                if la is not None:
                    t_lo("T2", 0)
                if ln is not None:
                    values(1, 1)
                if la is not None:
                    t_lo("T2", 1)
                if ln is not None:
                    for j in (2, 3):
                        values(j, 0)
                        values(j, 1)
                    scores(0, i + 1, ln)

            bodies(dve, body)

        @block.tensor
        def _(pe):
            mm, tr = nc.tensor.matmul, nc.tensor.transpose
            pe.wait_ge(s_init, 2)

            def turn(z, hf, bank_of, room, full, name):
                t0, nt = HALF[hf]
                for part, f0, rows in (("A", 0, 128), ("C", 128, CR)):
                    use = f"{name}{part}{hf}"
                    reach(pe, *room(use))
                    for t in range(nt):
                        c = (t0 + t) * ZW + f0
                        last = tr(bank_of(use)[0:rows, t * TT:(t + 1) * TT], z[:, c:c + rows], keep.ident[0:TT, 0:TT])
                    last.then_inc(full(use), 1)

            def body(i, la, lm, ln):
                m = i - 1

                def room_a(use):
                    reach(pe, *a_room(i, use))

                def filled_a(use, last):
                    last.then_inc(a_full(i, use)[0], 1)

                def room_m(use):
                    reach(pe, *m_room(i, lm, use))

                def filled_m(use, last):
                    last.then_inc(m_full(i, lm, use)[0], 1)

                def front_turned(hf):
                    if hf == 0:
                        pe.wait_ge(s_z[0], i + 2)
                    turn(z1, hf, lambda u: bank_a(i, u), lambda u: a_room(i, u), lambda u: a_full(i, u)[0], "T1")

                def front_product(name, hf):
                    c0, n = {"Q": (0, 128), "K": (128, 128), "B": (256, 2 * HD)}[name]
                    use = f"{name}{hf}"
                    if use == "Q0":
                        pe.wait_ge(*a_freed(i, "T1C1"))
                    room_a(use)
                    filled_a(use, split_passes(nc, bank_a(i, use)[0:n, 0:QH], *[t[:, hf * QH:(hf + 1) * QH] for t in z1t],
                                               *[w[:, c0:c0 + n] for w in keep.w["qkv", ln]], True))

                def values(j):
                    use = f"V{j}"
                    room_a(use)
                    wv = [w[:, 2 * DIM:3 * DIM] for w in keep.w["qkv", ln]]
                    for w in range(2):
                        c = slice((2 * j + w) * GK, (2 * j + w + 1) * GK)
                        last = split_passes(nc, bank_a(i, use)[0:GK, w * DIM:(w + 1) * DIM], *[t[:, c] for t in z1t], *wv, False)
                    filled_a(use, last)

                def scores(j, n):
                    if j % 2 == 0:
                        for name in "QKB":
                            pe.wait_ge(*a_freed(n - 1, f"{name}{j // 2}"))
                    reach(pe, s_sadd, n * NG + j)
                    for h in range(HEADS):
                        for p in range(2):
                            for w in range(2):
                                c = (2 * j + w) * GK + p * WT
                                q = qm[:, h * SN + c:h * SN + c + WT] if h < 4 else q4[:, c:c + WT]
                                k = (kt if h < 4 else k4)[:, c:c + WT]
                                last = mm(s_ps[w * WP:w * WP + WT, (2 * h + p) * WT:(2 * h + p + 1) * WT], q, k,
                                          start=True, stop=True)
                    last.then_inc(s_sfull, 1)

                def weights_turned(j):
                    n = i * NG + j
                    pe.wait_ge(s_exp, n + 1)
                    reach(pe, s_pte, n)
                    reach(pe, s_od, n)
                    for h in range(HEADS):
                        o = pt_ps[0:GK, h * QP:(h + 1) * QP] if h < 4 else o_ps[0:GK, PT4:PT4 + QP]
                        last = tr(o, pr[:, h * GK:(h + 1) * GK], keep.ident[0:QP, 0:QP])
                    last.then_inc(s_ptf, 1)

                def outputs(j):
                    pe.wait_ge(s_pte, i * NG + j + 1)
                    pe.wait_ge(*a_freed(i - 1, f"V{j}"))
                    for h in range(HEADS):
                        for w in range(2):
                            last = mm(o_ps[w * WP:w * WP + WT, h * 2 * VW:(h + 1) * 2 * VW],
                                      pt[:, h * QP + w * WP:h * QP + w * WP + WT],
                                      view(vb, 0, GK, j * VG + (w * HEADS + h) * VW, [[2 * HEADS * VW, 2], [1, VW]]),
                                      start=True, stop=True)
                    last.then_inc(s_of, 1)

                def outputs_turned(j):
                    use = f"OT{j}"
                    pe.wait_ge(s_od, i * NG + j + 1)
                    room_a(use)
                    for f0, rows, c0 in ((0, 128, 0), (128, CR, 2 * QP)):
                        for p in range(2):
                            last = tr(bank_a(i, use)[0:rows, c0 + p * QP:c0 + (p + 1) * QP],
                                      os_[:, p * ZW + f0:p * ZW + f0 + rows], keep.ident[0:QP, 0:QP])
                    filled_a(use, last)

                def mlp_in(gs):
                    for g in gs:
                        use = f"G{g}"
                        hf, f = divmod(g, FT)
                        t0, nt = HALF[hf]
                        room_m(use)
                        last = split_passes(nc, bank_m(i, lm, use)[:, 0:nt * TT], *[t[:, t0 * TT:(t0 + nt) * TT] for t in z2t],
                                            *[w[:, f * 128:(f + 1) * 128] for w in keep.w["w1", lm]], True)
                        filled_m(use, last)

                def mlp_out(n):
                    use = f"W{n}"
                    t0, nt = PAIRS[n]
                    room_m(use)
                    for t in range(nt):
                        for f in range(FT):
                            c = f * SN + (t0 + t) * TT
                            last = mm(bank_m(i, lm, use)[0:TT, t * DIM:(t + 1) * DIM], ht[:, c:c + TT],
                                      keep.w["w2", lm][:, f * DIM:(f + 1) * DIM], start=(f == 0), stop=(f == FT - 1))
                    filled_m(use, last)

                def projection(n):
                    use = f"P{n}"
                    room_a(use)
                    for t in range(PROJ[n][0], sum(PROJ[n])):
                        c = slice(t * TT, (t + 1) * TT)
                        o = (t - PROJ[n][0]) * DIM
                        last = split_passes(nc, bank_a(i, use)[0:TT, o:o + DIM], *[x_[:, c] for x_ in ot],
                                            *[w[:] for w in keep.w["proj", la]], False)
                    filled_a(use, last)

                def mlp_turned(z, name, hf):
                    turn(z, hf, lambda u: bank_m(i, lm, u), lambda u: m_room(i, lm, u), lambda u: m_full(i, lm, u)[0], name)

                if lm is not None:
                    pe.wait_ge(*t2_freed(i, lm))
                    mlp_in(range(4))
                if la is not None:
                    scores(1, i)
                if lm is not None:
                    mlp_in(range(4, 2 * FT))
                    mlp_out(0)
                if la is not None:
                    weights_turned(0)
                    scores(2, i)
                    outputs(0)
                if lm is not None:
                    mlp_out(1)
                if la is not None:
                    outputs_turned(0)
                    weights_turned(1)
                    scores(3, i)
                    outputs(1)
                if lm is not None:
                    mlp_out(2)
                if la is not None:
                    outputs_turned(1)
                    weights_turned(2)
                if ln is not None:
                    front_turned(0)
                if la is not None:
                    outputs(2)
                if ln is not None:
                    front_turned(1)
                if lm is not None:
                    mlp_out(3)
                if la is not None:
                    outputs_turned(2)
                    weights_turned(3)
                if ln is not None:
                    front_product("Q", 0)
                    front_product("K", 0)
                if la is not None:
                    outputs(3)
                if lm is not None:
                    mlp_out(4)
                if la is not None:
                    outputs_turned(3)
                if lm is not None:
                    mlp_out(5)
                if lm == 1:
                    pe.wait_ge(s_xod, 2 * (m - NS) + 1)
                    mlp_turned(xo, "T3", 0)
                if la is not None:
                    pe.wait_ge(*a_freed(i, "OT3"))
                    projection(0)
                    projection(1)
                if ln is not None:
                    front_product("B", 0)
                    front_product("Q", 1)
                if la is not None:
                    projection(2)
                if lm == 1:
                    pe.wait_ge(s_xod, 2 * (m - NS) + 2)
                    mlp_turned(xo, "T3", 1)
                if ln is not None:
                    front_product("K", 1)
                    front_product("B", 1)
                    values(0)
                    scores(0, i + 1)
                if lm == 1:
                    pe.wait_ge(*m_freed(i, 1, "T3C1"))
                    for n, (t0, nt) in enumerate(LPAIRS):
                        use = f"L{n}"
                        room_m(use)
                        for t in range(nt):
                            c = slice((t0 + t) * TT, (t0 + t + 1) * TT)
                            last = split_passes(nc, bank_m(i, lm, use)[0:TT, t * DIM:(t + 1) * DIM], *[z[:, c] for z in z2t],
                                                *[w[:] for w in keep.w["lin", 1]], False)
                        filled_m(use, last)
                if la is not None:
                    pe.wait_ge(s_z[1], 2 * i + 1)
                    mlp_turned(z2, "T2", 0)
                if ln is not None:
                    values(1)
                if la is not None:
                    pe.wait_ge(s_z[1], 2 * i + 2)
                    mlp_turned(z2, "T2", 1)
                if ln is not None:
                    values(2)
                    values(3)

            bodies(pe, body)


def phase_c(nc, keep, f_syn, ys, out):
    with ExitStack() as ctx:
        def sb(name, shape, dt=F32):
            return ctx.enter_context(nc.sbuf_tensor(name, shape, dt))

        def sem(name):
            return ctx.enter_context(nc.semaphore(name))

        KG = 3
        G = K // KG
        acc = [ctx.enter_context(nc.psum_tensor(f"c_acc{n}", [128, 512], F32)) for n in range(2)]
        fin = [ctx.enter_context(nc.psum_tensor(f"c_fin{n}", [128, 512], F32)) for n in range(2)]
        taps = [sb(f"c_taps{n}", [TT, NJ * TT]) for n in range(2)]
        band_hi = sb("c_band_hi", [TT, K * NJ * TT], F32R)
        band_lo = sb("c_band_lo", [TT, K * NJ * TT], F32R)
        y = [sb(f"c_y{u}", [TT, NT * DIM]) for u in range(2)]
        y_hi = sb("c_y_hi", [TT, PADT * K * C], F32R)
        y_lo = sb("c_y_lo", [TT, PADT * K * C], F32R)
        conv = [sb(f"c_conv{u}", [TT, C * NT]) for u in range(2)]
        direct = [sb(f"c_direct{u}", [TT, C * NT]) for u in range(2)]
        one = sb("c_one", [TT, 1])
        res = [sb(f"c_res{u}", [TT, 4 * TT]) for u in range(2)]

        s_taps = [sem(f"c_taps_in{n}") for n in range(2)]
        s_bhi, s_blo, s_zero, s_one = sem("c_band_hi_done"), sem("c_band_lo_done"), sem("c_zero"), sem("c_one_set")
        s_y = [sem(f"c_y_in{u}") for u in range(2)]
        s_hi, s_lo = sem("c_y_hi_done"), sem("c_y_lo_done")
        s_g = sem("c_filters")
        s_conv, s_dir, s_fin, s_res = sem("c_conv_out"), sem("c_direct_out"), sem("c_final"), sem("c_res_done")
        s_store = [sem(f"c_store{u}") for u in range(2)]
        KC = K * C

        def first(img):
            return isinstance(img, int) and img == 0

        block = ctx.enter_context(nc.Block())

        @block.sync
        def _(sp):
            def load_image(img, u):
                for yy in range(2):
                    first = 2 - yy
                    for t0, nt in ((0, first), (first, NT - first)):
                        y0 = (2 * t0 + yy - SHIFT) % H
                        for x0, nx in ((0, SHIFT), (SHIFT, W - SHIFT)):
                            off = y0 * W * DIM + ((x0 - SHIFT) % W) * DIM
                            sp.dma_start(view(y[u], yy * W + x0, nx, t0 * DIM, [[DIM, nt], [1, DIM]]),
                                         dram(ys, img * (H * W * DIM) + off, [[DIM, nx], [TT * DIM, nt], [1, DIM]])
                                         ).then_inc(s_y[u], 16)

            def load_taps(k):
                for r in range(2):
                    for yy in range(2):
                        if k >= 2 and (r, yy) == (0, 0):
                            sp.wait_ge(s_blo, k - 1)
                        sp.dma_start(view(taps[k % 2], r * W, W, yy * W, [[TT, NJ], [1, W]]),
                                     dram(f_syn.tensor, (k * 11 + r - yy + 1) * FROW, [[1, W], [2 * FROW, NJ], [1, W]])
                                     ).then_inc(s_taps[k % 2], 16)

            load_image(0, 0)
            load_taps(0)
            load_taps(1)
            load_image(1, 1)
            for k in range(2, K):
                load_taps(k)

            def store_image(img, u):
                sp.wait_ge(s_res, img + 1)
                sp.dma_start(dram(out.tensor, img * (C * H * W), [[TT, TT], [TT * TT, 4], [1, TT]]),
                             view(res[u], 0, TT, 0, [[TT, 4], [1, TT]])).then_inc(s_store[u], 16)

            def body(pair):
                for u in range(2):
                    img = pair * 2 + u
                    sp.wait_ge(s_lo, (img + 1) * G)
                    sp.wait_ge(s_dir, img + 1)
                    load_image(img + 2, u)
                    store_image(img, u)

            body(0)
            with sp.Fori(1, B // 2 - 1) as pair:
                body(pair)
            for u in range(2):
                store_image(B - 2 + u, u)
            for u in range(2):
                sp.wait_ge(s_store[u], 16 * (B // 2))

        @block.gpsimd
        def _(pool):
            nc.gpsimd.memset(one[:], 1.0).then_inc(s_one, 1)
            pool.wait_ge(s_one, 1)

            def body(pair):
                for u in range(2):
                    img = pair * 2 + u
                    pool.wait_ge(s_y[u], (pair + 1) * 128)
                    reach(pool, s_fin, img - 1)
                    src = view(y[u], 0, TT, KC, [[1, C], [DIM, NT]])
                    nc.gpsimd.tensor_tensor(direct[u][:].rearrange("p (c t) -> p c t", t=NT), src,
                                            view(one, 0, TT, 0, [[0, C], [0, NT]]), ALU.mult).then_inc(s_dir, 1)

            body(0)
            with pool.Fori(1, B // 2) as pair:
                body(pair)

        @block.scalar
        def _(act):
            def band(k):
                act.wait_ge(s_taps[k % 2], 64 * (k // 2 + 1))
                nc.scalar.activation(band_hi[:, k * NJ * TT:(k + 1) * NJ * TT], taps[k % 2][:], ACT.Copy).then_inc(s_bhi, 1)

            def sum_out(img, u):
                act.wait_ge(s_g, (img + 1) * G)
                reach(act, s_fin, img - 1)
                nc.scalar.activation(conv[u][:].rearrange("p (c t) -> p c t", t=NT),
                                     view(acc[u], 0, TT, 0, [[1, C], [C, NT]]), ACT.Copy).then_inc(s_conv, 1)

            def body(pair, u):
                img = pair * 2 + u
                for g in range(G):
                    if g == 0:
                        act.wait_ge(s_y[u], (pair + 1) * 128)
                    if not first(img):
                        act.wait_ge(s_g, (img - 1) * G + g + 1)
                    if g == G - 1 and not first(img):
                        sum_out(img - 1, 1 - u)
                    nc.scalar.activation(view(y_hi, 0, TT, 2 * KC + g * KG * C, [[KC, NT], [1, KG * C]]),
                                         view(y[u], 0, TT, g * KG * C, [[DIM, NT], [1, KG * C]]), ACT.Copy).then_inc(s_hi, 1)
                    if first(img):
                        for k in range(g * KG, (g + 1) * KG):
                            band(k)

            act.wait_ge(s_zero, 1)
            body(0, 0)
            body(0, 1)
            with act.Fori(1, B // 2) as pair:
                for u in range(2):
                    body(pair, u)
            sum_out(B - 1, 1)

        @block.vector
        def _(dve):
            nc.vector.memset(y_hi[:].bitcast(F32), 0.0)
            nc.vector.memset(y_lo[:].bitcast(F32), 0.0).then_inc(s_zero, 1)

            def band(k):
                dve.wait_ge(s_bhi, k + 1)
                cols = slice(k * NJ * TT, (k + 1) * NJ * TT)
                nc.vector.tensor_tensor(band_lo[:, cols], taps[k % 2][:], band_hi[:, cols].bitcast(F32),
                                        ALU.subtract).then_inc(s_blo, 1)

            def result(pair, u):
                dve.wait_ge(s_fin, pair * 2 + u + 1)
                reach(dve, s_store[u], pair * 16)
                nc.vector.tensor_copy(res[u][:], fin[u][0:TT, 0:4 * TT]).then_inc(s_res, 1)

            def body(pair, u):
                img = pair * 2 + u
                for g in range(G):
                    dve.wait_ge(s_hi, img * G + g + 1)
                    o = 2 * KC + g * KG * C
                    dims = [[KC, NT], [1, KG * C]]
                    nc.vector.tensor_tensor(view(y_lo, 0, TT, o, dims),
                                            view(y[u], 0, TT, g * KG * C, [[DIM, NT], [1, KG * C]]),
                                            view(y_hi, 0, TT, o, dims).bitcast(F32), ALU.subtract).then_inc(s_lo, 1)
                    if first(img):
                        for k in range(g * KG, (g + 1) * KG):
                            band(k)
                if not first(img):
                    result(pair if u == 1 else pair - 1, 1 - u)

            body(0, 0)
            body(0, 1)
            with dve.Fori(1, B // 2) as pair:
                for u in range(2):
                    body(pair, u)
            result(B // 2 - 1, 1)

        @block.tensor
        def _(pe):
            mm = nc.tensor.matmul

            def turned(img, u):
                pe.wait_ge(s_conv, img + 1)
                pe.wait_ge(s_dir, img + 1)
                reach(pe, s_res, img - 1)
                for q in range(4):
                    cols = slice(q * TT, (q + 1) * TT)
                    mm(fin[u][0:TT, cols], conv[u][:, cols], keep.flip[0:TT, :], start=True, stop=False)
                    last = mm(fin[u][0:TT, cols], direct[u][:, cols], keep.ident[0:TT, 0:TT], start=False, stop=True)
                last.then_inc(s_fin, 1)

            def body(pair, u):
                img = pair * 2 + u
                reach(pe, s_conv, img - 1)
                n = 0
                for g in range(G):
                    pe.wait_ge(s_lo, img * G + g + 1)
                    for k in range(g * KG, (g + 1) * KG):
                        if first(img):
                            pe.wait_ge(s_blo, k + 1)
                        for j in range(NJ):
                            cols = slice((k * NJ + j) * TT, (k * NJ + j + 1) * TT)
                            o, dims = j * KC + k * C, [[KC, NT], [1, C]]
                            for a, b in ((band_hi, y_hi), (band_hi, y_lo), (band_lo, y_hi)):
                                last = mm(acc[u][0:TT, 0:NT * C], a[:, cols], view(b, 0, TT, o, dims),
                                          start=(n == 0), stop=(n == K * NJ * 3 - 1))
                                n += 1
                    last.then_inc(s_g, 1)
                    if g == 0 and not first(img):
                        turned(img - 1, 1 - u)
            body(0, 0)
            body(0, 1)
            with pe.Fori(1, B // 2) as pair:
                for u in range(2):
                    body(pair, u)
            turned(B - 1, 1)


_ORDER = ["x", "xf", "f_ana", "f_syn", "ln1g", "ln1b", "qkvw", "qkvb", "projw", "projb", "rel", "ln2g", "ln2b",
          "w1", "b1", "w2", "b2", "linwT", "linb", "convwT", "convb", "wmask"]


def kernel(**inputs):
    import numpy as np
    import concourse.bacc as bacc
    from concourse.bass_utils import run_bass_kernel_spmd

    src = {k.replace("L0_conv_", ""): np.asarray(v) for k, v in inputs.items()}

    def padded_rows(f):
        rows = np.zeros((K, FS + 2, FROW), f.dtype)
        rows[:, 1:FS + 1, PADF:PADF + FS] = f
        return rows

    arrays = dict(src)
    arrays["xf"] = src["x"][..., ::-1]
    arrays["f_ana"] = padded_rows(src["f_ana"].reshape(K, FS, FS)[..., ::-1])
    arrays["f_syn"] = padded_rows(src["f_syn"].reshape(K, FS, FS))
    side = 2 * WIN - 1
    arrays["rel"] = src["rpb"].transpose(0, 2, 1).reshape(2 * HEADS, side, side)[:, ::-1, ::-1]
    arrays["linwT"] = src["linw"].T
    arrays["convwT"] = src["convw"].reshape(C, DIM).T
    late = np.arange(WIN) >= WIN - SHIFT
    apart_y = np.repeat(late, WIN)[:, None] != np.repeat(late, WIN)[None, :]
    apart_x = np.tile(late, WIN)[:, None] != np.tile(late, WIN)[None, :]
    wmask = np.zeros((QP, 4, 2, WT), np.float32)
    for bottom in range(2):
        for right in range(2):
            for w in range(2):
                for p in range(2):
                    apart = (apart_y & (bottom and p == 1)) | (apart_x & (right and w == 1))
                    wmask[w * WP:w * WP + WT, bottom * 2 + right, p] = np.where(apart, np.float32(-100), np.float32(0))
    arrays["wmask"] = wmask.reshape(QP, 4 * GK)

    nc = bacc.Bacc("TRN2", target_bir_lowering=False, num_devices=1)
    given, args = {}, []
    for name in _ORDER:
        a = np.ascontiguousarray(arrays[name])
        given[f"in_{name}"] = a
        args.append(nc.dram_tensor(f"in_{name}", a.shape, mybir.dt.from_np(a.dtype), kind="ExternalInput").ap())
    res = nc.dram_tensor("out_0", (B, C, H, W), F32, kind="ExternalOutput").ap()
    build(nc, *args, res)
    r = run_bass_kernel_spmd(nc, [given], core_ids=[0])
    return r.results[0]["out_0"]
```
